# Optimizing a Trainium2 kernel written in Bass

```python
import numpy as np
import jax
import jax.numpy as jnp

def _softmax(x, axis=-1):
    return jax.nn.softmax(x, axis=axis)

def _gelu(x):
    return jax.nn.gelu(x, approximate=True)

def _silu(x):
    return jax.nn.silu(x)

def _sigmoid(x):
    return jax.nn.sigmoid(x)

def _layernorm(x, axis=-1, eps=1e-05):
    m = jnp.mean(x, axis=axis, keepdims=True)
    v = jnp.var(x, axis=axis, keepdims=True)
    return (x - m) / jnp.sqrt(v + eps)

def _scatter_add(tgt, idx, src, axis=0):
    return tgt.at[idx].add(src)

def _segment_sum(src, seg, n):
    return jax.ops.segment_sum(src, seg, n)
kernel_name = 'mk_lm_tower_d1_tok_ids2048_r4_e46c6d'

def setup_inputs(seed: int=0):
    np.random.seed(seed)
    _w = jnp.asarray

    def _rec_inputs():
        import jax
        import jax.numpy as jnp
        _rk = jax.random.key(seed)
        x = jax.random.randint(jax.random.fold_in(_rk, 1), (16, 256), 0, 128, jnp.int32)
        return x
    x = _rec_inputs()

    def _L0_tok_setup():
        import jax, jax.numpy as jnp
        import numpy as np
        VOCAB = 128
        D_VIS = 512
        D_TXT = 512
        EPS = 1e-06
        VOCAB_OFFSET = 0

        def rms_norm(x, weight, eps):
            xf = x.astype(jnp.float32)
            var = jnp.mean(xf * xf, axis=-1, keepdims=True)
            normed = xf * jax.lax.rsqrt(var + eps)
            if weight is not None:
                normed = normed * weight.astype(jnp.float32)
            return normed.astype(x.dtype)
        key = jax.random.key(seed)
        k_ids, k_emb, k_w, k_proj = jax.random.split(key, 4)
        input_ids = jax.random.randint(k_ids, (8, 1024), 0, VOCAB, dtype=jnp.int64)
        emb_table = jax.random.normal(k_emb, (VOCAB, D_VIS), dtype=jnp.float32) * 0.02
        norm_weight = jnp.ones((D_VIS,), dtype=jnp.float32) + 0.01 * jax.random.normal(k_w, (D_VIS,), dtype=jnp.float32)
        proj_weight = jax.random.normal(k_proj, (D_TXT, D_VIS), dtype=jnp.float32) * 0.02
        return {'input_ids': input_ids, 'emb_table': emb_table, 'norm_weight': norm_weight, 'proj_weight': proj_weight}
    _L0_tok_all = _L0_tok_setup()
    _L0_tok_in = {k: v for k, v in _L0_tok_all.items() if k in ('emb_table', 'norm_weight', 'proj_weight')}
    del _L0_tok_all

    def _L0_attn_setup():
        import jax, jax.numpy as jnp
        import numpy as np
        B, T, HID = (1, 512, 512)
        H = 16
        D = HID // H
        EPS = 1e-05

        def _layer_norm(x, eps=1e-05):
            mu = jnp.mean(x, axis=-1, keepdims=True)
            var = jnp.mean((x - mu) ** 2, axis=-1, keepdims=True)
            return (x - mu) * jax.lax.rsqrt(var + eps)

        def _feature_map(x, gamma, beta):
            return _layer_norm(x * gamma + beta)
        key = jax.random.key(seed)
        ks = jax.random.split(key, 8)
        s = HID ** (-0.5)
        return {'hidden_states': jax.random.normal(ks[0], (B, T, HID), jnp.float32), 'Wq': jax.random.normal(ks[1], (HID, HID), jnp.float32) * s, 'Wk': jax.random.normal(ks[2], (HID, HID), jnp.float32) * s, 'Wv': jax.random.normal(ks[3], (HID, HID), jnp.float32) * s, 'Wo': jax.random.normal(ks[4], (HID, HID), jnp.float32) * s, 'gamma': 1.0 + 0.1 * jax.random.normal(ks[5], (D,), jnp.float32), 'beta': 0.1 * jax.random.normal(ks[6], (D,), jnp.float32)}
    _L0_attn_all = _L0_attn_setup()
    _L0_attn_in = {k: v for k, v in _L0_attn_all.items() if k in ('Wq', 'Wk', 'Wv', 'Wo', 'gamma', 'beta')}
    del _L0_attn_all

    def _L0_ffn_setup():
        import jax, jax.numpy as jnp
        import numpy as np
        HIDDEN = 512
        INTER = 2048
        SCALE = 64.0

        def fwht(x):
            orig_shape = x.shape
            n = orig_shape[-1]
            x = x.reshape(-1, n)
            h = 1
            while h < n:
                x = x.reshape(-1, n // (2 * h), 2, h)
                a, b = (x[:, :, 0, :], x[:, :, 1, :])
                x = jnp.stack([a + b, a - b], axis=2).reshape(-1, n)
                h *= 2
            return (x / jnp.sqrt(jnp.asarray(n, x.dtype))).reshape(orig_shape)
        key = jax.random.key(seed)
        ks = jax.random.split(key, 8)
        inp = jax.random.normal(ks[0], (4, 512, HIDDEN), dtype=jnp.float32)
        SU_ug = jnp.where(jax.random.bernoulli(ks[1], 0.5, (HIDDEN,)), 1.0, -1.0).astype(jnp.float32)
        SU_dp = jnp.where(jax.random.bernoulli(ks[2], 0.5, (INTER,)), 1.0, -1.0).astype(jnp.float32)
        Wscale_ug = jax.random.uniform(ks[3], (2 * INTER,), jnp.float32, 0.5, 1.5)
        Wscale_dp = jax.random.uniform(ks[4], (HIDDEN,), jnp.float32, 0.5, 1.5)
        W_up = jax.random.normal(ks[5], (INTER, HIDDEN), dtype=jnp.float32) * 0.02
        W_gate = jax.random.normal(ks[6], (INTER, HIDDEN), dtype=jnp.float32) * 0.02
        W_down = jax.random.normal(ks[7], (HIDDEN, INTER), dtype=jnp.float32) * 0.02
        return {'input': inp, 'SU_ug': SU_ug, 'SU_dp': SU_dp, 'Wscale_ug': Wscale_ug, 'Wscale_dp': Wscale_dp, 'W_up': W_up, 'W_gate': W_gate, 'W_down': W_down}
    _L0_ffn_all = _L0_ffn_setup()
    _L0_ffn_in = {k: v for k, v in _L0_ffn_all.items() if k in ('SU_ug', 'SU_dp', 'Wscale_ug', 'Wscale_dp', 'W_up', 'W_gate', 'W_down')}
    del _L0_ffn_all
    return {'x': x, 'L0_tok_emb_table': _L0_tok_in['emb_table'], 'L0_tok_norm_weight': _L0_tok_in['norm_weight'], 'L0_tok_proj_weight': _L0_tok_in['proj_weight'], 'L0_attn_Wq': _L0_attn_in['Wq'], 'L0_attn_Wk': _L0_attn_in['Wk'], 'L0_attn_Wv': _L0_attn_in['Wv'], 'L0_attn_Wo': _L0_attn_in['Wo'], 'L0_attn_gamma': _L0_attn_in['gamma'], 'L0_attn_beta': _L0_attn_in['beta'], 'L0_ffn_SU_ug': _L0_ffn_in['SU_ug'], 'L0_ffn_SU_dp': _L0_ffn_in['SU_dp'], 'L0_ffn_Wscale_ug': _L0_ffn_in['Wscale_ug'], 'L0_ffn_Wscale_dp': _L0_ffn_in['Wscale_dp'], 'L0_ffn_W_up': _L0_ffn_in['W_up'], 'L0_ffn_W_gate': _L0_ffn_in['W_gate'], 'L0_ffn_W_down': _L0_ffn_in['W_down']}

def reference(x, L0_tok_emb_table, L0_tok_norm_weight, L0_tok_proj_weight, L0_attn_Wq, L0_attn_Wk, L0_attn_Wv, L0_attn_Wo, L0_attn_gamma, L0_attn_beta, L0_ffn_SU_ug, L0_ffn_SU_dp, L0_ffn_Wscale_ug, L0_ffn_Wscale_dp, L0_ffn_W_up, L0_ffn_W_gate, L0_ffn_W_down):
    import jax
    import jax.numpy as jnp

    def _L0_tok_ref(input_ids, emb_table, norm_weight, proj_weight):
        import jax, jax.numpy as jnp
        import numpy as np
        VOCAB = 128
        D_VIS = 512
        D_TXT = 512
        EPS = 1e-06
        VOCAB_OFFSET = 0

        def rms_norm(x, weight, eps):
            xf = x.astype(jnp.float32)
            var = jnp.mean(xf * xf, axis=-1, keepdims=True)
            normed = xf * jax.lax.rsqrt(var + eps)
            if weight is not None:
                normed = normed * weight.astype(jnp.float32)
            return normed.astype(x.dtype)
        hard_emb = emb_table[input_ids - VOCAB_OFFSET]
        hard_emb_norm = rms_norm(hard_emb, norm_weight, EPS)
        proj = jnp.einsum('bsd,ed->bse', hard_emb_norm, proj_weight)
        return rms_norm(proj, None, EPS)

    def _L0_attn_ref(hidden_states, Wq, Wk, Wv, Wo, gamma, beta):
        import jax, jax.numpy as jnp
        import numpy as np
        B, T, HID = (1, 512, 512)
        H = 16
        D = HID // H
        EPS = 1e-05

        def _layer_norm(x, eps=1e-05):
            mu = jnp.mean(x, axis=-1, keepdims=True)
            var = jnp.mean((x - mu) ** 2, axis=-1, keepdims=True)
            return (x - mu) * jax.lax.rsqrt(var + eps)

        def _feature_map(x, gamma, beta):
            return _layer_norm(x * gamma + beta)
        b, t, _ = hidden_states.shape
        q = (hidden_states @ Wq.T).reshape(b, t, H, D)
        k = (hidden_states @ Wk.T).reshape(b, t, H, D)
        v = (hidden_states @ Wv.T).reshape(b, t, H, D)
        q = _feature_map(q, gamma, beta)
        k = _feature_map(k, gamma, beta)
        q = q * D ** (-0.5)
        attn = jnp.einsum('bqhd,bkhd->bhqk', q, k) ** 2
        mask = jnp.tril(jnp.ones((t, t), dtype=bool))
        attn = jnp.where(mask, attn, 0.0)
        o = jnp.einsum('bhqk,bkhd->bqhd', attn, v)
        z = jnp.sum(attn, axis=-1)
        o = o / (jnp.swapaxes(z, 1, 2)[..., None] + EPS)
        o = o.reshape(b, t, H * D)
        return o @ Wo.T

    def _L0_ffn_ref(input, SU_ug, SU_dp, Wscale_ug, Wscale_dp, W_up, W_gate, W_down):
        import jax, jax.numpy as jnp
        import numpy as np
        HIDDEN = 512
        INTER = 2048
        SCALE = 64.0

        def fwht(x):
            orig_shape = x.shape
            n = orig_shape[-1]
            x = x.reshape(-1, n)
            h = 1
            while h < n:
                x = x.reshape(-1, n // (2 * h), 2, h)
                a, b = (x[:, :, 0, :], x[:, :, 1, :])
                x = jnp.stack([a + b, a - b], axis=2).reshape(-1, n)
                h *= 2
            return (x / jnp.sqrt(jnp.asarray(n, x.dtype))).reshape(orig_shape)
        n = SU_ug.shape[0]
        x = input.reshape(-1, n)
        x = fwht(x * SU_ug) / SCALE
        x_up = x @ W_up.T * (Wscale_ug[:INTER] * SCALE)
        x_gate = x @ W_gate.T * (Wscale_ug[INTER:] * SCALE)
        x = jax.nn.silu(x_gate) * x_up
        x = fwht(x * SU_dp) / SCALE
        x = x @ W_down.T * (Wscale_dp * SCALE)
        return x.reshape(input.shape)
    h = _L0_tok_ref(x, L0_tok_emb_table, L0_tok_norm_weight, L0_tok_proj_weight)
    h = h + _L0_attn_ref(_layernorm(h, axis=-1), L0_attn_Wq, L0_attn_Wk, L0_attn_Wv, L0_attn_Wo, L0_attn_gamma, L0_attn_beta)
    h = h + _L0_ffn_ref(_layernorm(h, axis=-1), L0_ffn_SU_ug, L0_ffn_SU_dp, L0_ffn_Wscale_ug, L0_ffn_Wscale_dp, L0_ffn_W_up, L0_ffn_W_gate, L0_ffn_W_down)
    return h

_drawn_inputs = setup_inputs


def setup_inputs(seed=0):
    import zlib

    import numpy as np

    out = dict(_drawn_inputs(seed))
    spreads = {}
    factors = {}
    for name, (base, spread) in spreads.items():
        noise = np.random.default_rng([zlib.crc32(name.encode()), seed]).standard_normal(out[name].shape)
        drawn = base * np.exp(spread * noise) if base else spread * noise
        out[name] = jnp.asarray(drawn.astype(out[name].dtype))
    for name, factor in factors.items():
        out[name] = (out[name] * factor).astype(out[name].dtype)
    return out
```

```python
from contextlib import ExitStack

import concourse.bass as bass
from concourse import mybir

ALU = mybir.AluOpType
ACT = mybir.ActivationFunctionType
AX = mybir.AxisListType
F32 = mybir.dt.float32
F16 = mybir.dt.float16
I32 = mybir.dt.int32
U32 = mybir.dt.uint32

P = 128
SLOTS = 32
UNIT_SLOTS = 24
W_TOP = 2.0 ** 9
V_TOP = 2.0 ** 10
A_TOP = 2.0 ** 10
TINY = 1e-30
EXPONENT = 0x7F800000


def units_of_slot(s):
    if s < UNIT_SLOTS:
        g = s // 3
        return [[4 * g, 4 * g + 1], [4 * g + 2], [4 * g + 3]][s % 3]
    return [32 + 2 * (s - UNIT_SLOTS), 33 + 2 * (s - UNIT_SLOTS)]


def tower(nc, x, emb, norm_w, proj_w, wq, wk, wv, wo, gamma, beta, su_ug, su_dp, wsc_ug, wsc_dp,
          w_up, w_gate, w_down, c_square, c_half, c_column, out):
    VOCAB, D = emb.shape
    BATCH, SEQ = x.shape
    DH = gamma.shape[0]
    H = D // DH
    INTER = w_up.shape[0]
    DC = D // P
    FT = INTER // P
    T = 512
    NB = BATCH * SEQ // T
    QUADS = H // 4
    GROUPS = 2 * INTER // 512
    GU_UNITS = GROUPS * DC
    UNITS = GU_UNITS + FT
    PARAMS = 9 * 16
    assert VOCAB == P and SEQ == 256 and D == 512 and DH == 32 and FT == 16 and T == 2 * SEQ

    x_rows = x.rearrange("(n s) t -> n (s t)", s=2)
    x_cols = x.rearrange("(n s) (c p) -> n p (s c)", s=2, p=P)
    out_rows = out.rearrange("(n s) (c p) d -> n (s c) p d", s=2, p=P)

    def rows(v, n):
        return v.rearrange("(a n) -> a n", a=1).broadcast_to([P, n])

    ctx = ExitStack()
    with ctx:
        def sb(name, shape, dt=F32):
            return ctx.enter_context(nc.sbuf_tensor(name, shape, dt))

        def sem(name):
            return ctx.enter_context(nc.semaphore(name))

        h_table = nc.dram_tensor("h_table", [VOCAB, D], F32, kind="Internal").ap()

        wgu = sb("wgu", [P, 2, GROUPS, DC, 512], F16)
        wd = sb("wd", [P, 2, FT, D], F16)
        att = sb("att", [P, 2, H, P], F16)
        val = sb("val", [P, 2, D], F16)
        wo_t = sb("wo_t", [P, 2, DC, D], F16)
        c16 = sb("c16", [P, 672], F16)
        ident16, cum0, cum1 = c16[:, 0:128], c16[:, 128:384], c16[:, 384:512]
        iota_row, ones16 = c16[:, 512:640], c16[:, 640:672]
        ccol = sb("ccol", [P, 257])
        eps_row, iota_col = ccol[:, 0:256], ccol[:, 256:257]
        hid = sb("hid", [P, 2, FT, T], F16)
        xT = sb("xT", [P, 2, DC, T], F16)
        h1 = sb("h1", [P, 2, 4, D])
        oT = sb("oT", [P, 2, QUADS, T], F16)
        prod = sb("prod", [P, 2, T])
        p16 = sb("p16", [P, 2, 4, T], F16)
        cnt = sb("cnt", [P, T])
        onehotT = sb("onehotT", [P, T], F16)
        onehot = sb("onehot", [P, 4, P], F16)
        ids_b = sb("ids_b", [P, T], I32)
        ids_c = sb("ids_c", [P, 4], I32)
        ids_f = sb("ids_f", [P, 4])
        wide = sb("wide", [P, D])
        sg = sb("sg", [P, T])
        x16 = sg[:, :].bitcast(F16).rearrange("p (l d) -> p l d", l=2)
        a32 = sb("a32", [P, T])
        o_out = a32
        h_row = sb("h_row", [P, D])
        den = h_row
        bn = sb("bn", [P, 6])
        mv = sb("mv", [P, 2])
        ve = sb("ve", [P, 1])
        rstd = sb("rstd", [P, 1])
        mhalf = sb("mhalf", [P, 64])
        su_u = sb("su_u", [P, DC])
        su_d = sb("su_d", [P, FT])
        ws_g = sb("ws_g", [P, 2 * FT])
        ws_d = sb("ws_d", [P, DC])
        sc = sb("sc", [P, 2 * FT])
        kap = sb("kap", [P, FT])
        vn = sb("vn", [P, 16])
        gl = sb("gl", [P, 8])
        k_o, k_d = gl[:, 0:1], gl[:, 1:2]

        raw = [hid[:, 0, 0:8, :].rearrange("p a b -> p (a b)").bitcast(F32),
               hid[:, 0, 8:16, :].rearrange("p a b -> p (a b)").bitcast(F32),
               hid[:, 1, 0:8, :].rearrange("p a b -> p (a b)").bitcast(F32)]
        mixed = hid[:, 1, 8:16, :].rearrange("p a b -> p (a b)").bitcast(F32)
        down_tmp = p16[:, :, :, :].rearrange("p a b c -> p (a b c)").bitcast(F32)
        late = h1[:, 1, :, :].rearrange("p a b -> p (a b)")
        wt = late[:, 0:1024].rearrange("p (a b) -> p a b", a=2)
        diag = late[:, 1024:1536].rearrange("p (a b) -> p a b", a=4)
        ss, rn, rnp, inv = [late[:, 1792 + 32 * i:1824 + 32 * i] for i in range(4)]
        ebound, einv, su_e, ssd, st4, red = [late[:, 1920 + 16 * i:1936 + 16 * i] for i in range(6)]
        ident, hada = late[:, 1536:1664], late[:, 1664:1792]
        g32 = wgu[:, :, :, :, :].rearrange("p a b c d -> p (a b c d)").bitcast(F32)
        d32 = wd[:, :, :, :].rearrange("p a b c -> p (a b c)").bitcast(F32)
        small_raw = [g32[:, 2048 * i:2048 * (i + 1)].rearrange("p (a b) -> p a b", a=4) for i in range(5)]
        small_t = [g32[:, 10240 + 2048 * i:12288 + 2048 * i].rearrange("p (a b) -> p a b", a=4) for i in range(3)]
        small_t.append(d32[:, 0:2048].rearrange("p (a b) -> p a b", a=4))
        emb_s, embn, nw_b = d32[:, 2048:2560], d32[:, 2560:3072], d32[:, 3072:3584]
        h_tok, x1 = d32[:, 3584:4096], d32[:, 4096:4608]
        xTf = d32[:, 4608:5120]
        qk = d32[:, 5120:6144]
        qk2 = d32[:, 6144:7168]
        gb = d32[:, 7168:7232]
        stat = d32[:, 7232:7360]
        qkT = d32[:, 2048:3072]
        sq = small_raw[0]

        banks = [ctx.enter_context(nc.psum_tensor(f"bank{i}", [P, 512], F32)) for i in range(8)]
        GATE, UP = banks[0:2], banks[2:4]
        Y = banks[0:4]
        PICK = banks[4:6]
        HEADS, NORM = banks[6], banks[7]
        WOUT = banks[6:8]
        TURN, HADA = banks[0:2], banks[2:4]

        names = """c_land e_land p_land w_land gb_land gu_land0 gu_land1 gu_land2 d_land par_land h_stored
        ids_land idc_land hrow_land stored
        dve_step pool_step act_step
        emb_ss emb_n t_ready t_copied vt_ready vt_copied proj_ready tok_ready x1_ready qkv_ready
        feat_ready score_ready a_sq a_hi a_lo v_hi v_lo wo_hi wo_lo wo_scale
        wv_sq wv_ss wv_diag wo_sq pow_asked pow_given qk_turned qk_copied
        gu_ss gu_rn gu_pow gu_diag mixA_dve mixA_pool mixB_dve mixB_pool
        turned turned_copied hada_ready w_hi w_lo
        d_ss d_mix_dve d_mix_pool d_diag e_ready e_reduced
        onehotT_ready onehot_ready count_ready count_copied picked p_done ph_done pl_done
        heads_ready den_done rden_done o_done oh_done ol_done
        wo_ready h1_done bn_done mv_done ve_done rstd_done xn_done xh_done xl_done
        flip_ready xT_done
        gate_ready up_ready silu_done a_done ah_done al_done y_ready y_done y_last_done""".split()
        S = {n: sem(n) for n in names}

        ctx.enter_context(nc.allow_non_contiguous_dma(reason="short columns"))
        block = ctx.enter_context(nc.Block())

        @block.sync
        def _(sp):
            nc.sync.dma_start(emb_s, emb).then_inc(S["e_land"], 16)
            nc.sync.dma_start(nw_b, rows(norm_w, D)).then_inc(S["e_land"], 16)
            nc.sync.dma_start(late[:, 1536:1792], c_square).then_inc(S["c_land"], 16)
            nc.sync.dma_start(small_raw[0], proj_w.rearrange("(c p) d -> p c d", p=P)).then_inc(S["p_land"], 16)
            for i, w in enumerate((wq, wk, wv)):
                nc.sync.dma_start(small_raw[1 + i], w.rearrange("(c p) d -> p c d", p=P)).then_inc(S["w_land"], 16)
            nc.sync.dma_start(small_raw[4], wo.rearrange("(c p) d -> p c d", p=P)).then_inc(S["w_land"], 16)

            def gu_load(g):
                if g >= 3:
                    sp.wait_ge(S["turned"], 4 * (g - 2))
                src = (w_gate if g < GROUPS // 2 else w_up)[512 * (g % (GROUPS // 2)):512 * (g % (GROUPS // 2)) + 512, :]
                nc.sync.dma_start(raw[g % 3].rearrange("p (a b) -> p a b", a=4),
                                  src.rearrange("(c p) d -> p c d", p=P)).then_inc(S[f"gu_land{g % 3}"], 16)

            for g in range(GROUPS):
                gu_load(g)
                if g == 2:
                    nc.sync.dma_start(ids_b[:, :], x_rows[0:1, :].broadcast_to([P, T])).then_inc(S["ids_land"], 16)
                    nc.sync.dma_start(ids_c[:, :], x_cols[0, :, :]).then_inc(S["idc_land"], 16)
            for dt, group in enumerate((5, 6, 7, 7)):
                sp.wait_ge(S["turned"], 4 * (group + 1))
                dst = [raw[2], raw[0], raw[1], mixed][dt]
                nc.sync.dma_start(dst, w_down[dt * P:(dt + 1) * P, :]).then_inc(S["d_land"], 16)

            def block_io(b, n):
                if n is not None:
                    sp.wait_ge(S["c_land"], 16)
                    sp.wait_ge(S["onehotT_ready"], n)
                    nc.sync.dma_start(ids_b[:, :], x_rows[bass.ds(n, 1), :].broadcast_to([P, T])).then_inc(S["ids_land"], 16)
                    sp.wait_ge(S["c_land"], 16)
                    sp.wait_ge(S["hrow_land"], 64 * n)
                    nc.sync.dma_start(ids_c[:, :], x_cols[bass.ds(n, 1), :, :].rearrange("a p c -> (a p) c"))\
                        .then_inc(S["idc_land"], 16)
                for m in range(4):
                    sp.wait_ge(S["c_land"], 16)
                    if m < 3:
                        sp.wait_ge(S["y_done"], 3 * b + m + 1)
                    else:
                        sp.wait_ge(S["y_last_done"], b + 1)
                    nc.sync.dma_start(out_rows[bass.ds(b, 1), m, :, :].rearrange("a p d -> (a p) d"), o_out[:, :])\
                        .then_inc(S["stored"], 16)

            with sp.Fori(0, NB - 1) as b:
                block_io(b, b + 1)
            block_io(NB - 1, None)
            sp.wait_ge(S["stored"], 16 * 4 * NB)
            sp.wait_ge(S["h_stored"], 16)

        @block.gpsimd
        def _(pool):
            steps = [0]

            def link(ins):
                steps[0] += 1
                ins.then_inc(S["pool_step"], 1)
                pool.wait_ge(S["pool_step"], steps[0])

            link(nc.gpsimd.memset(mhalf[:, :], -0.5))

            def power(dst, src):
                return nc.gpsimd.tensor_tensor(dst, src, mhalf[:, 0:src.shape[1]], ALU.pow)

            pool.wait_ge(S["pow_asked"], 1)
            power(stat[:, 1:2], stat[:, 0:1]).then_inc(S["pow_given"], 1)
            pool.wait_ge(S["wv_ss"], 1)
            power(vn[:, 4:8], vn[:, 0:4]).then_inc(S["wv_diag"], 1)
            pool.wait_ge(S["pow_asked"], 2)
            power(stat[:, 3:4], stat[:, 2:3]).then_inc(S["pow_given"], 1)
            pool.wait_ge(S["pow_asked"], 3)
            power(stat[:, 5:6], stat[:, 4:5]).then_inc(S["pow_given"], 1)
            pool.wait_ge(S["wo_scale"], 1)
            link(nc.gpsimd.partition_all_reduce(red[:, 0:1], st4[:, 4:5], P, bass.bass_isa.ReduceOp.add))
            nc.gpsimd.partition_all_reduce(red[:, 1:2], st4[:, 5:6], P, bass.bass_isa.ReduceOp.max)\
                .then_inc(S["wo_scale"], 1)
            pool.wait_ge(S["wo_scale"], 3)
            power(red[:, 3:4], red[:, 2:3]).then_inc(S["wo_scale"], 1)
            pool.wait_ge(S["pow_asked"], 4)
            power(stat[:, 96:128], stat[:, 64:96]).then_inc(S["pow_given"], 1)

            def gu_front(g):
                v = raw[g % 3].rearrange("p (q a b) -> p q a b", a=2, b=P)
                t = mixed.rearrange("p (q a b) -> p q a b", a=2, b=P)
                pool.wait_ge(S["gu_land%d" % (g % 3)], 16 * (g // 3 + 1))
                if g:
                    pool.wait_ge(S["mixB_dve"], g)
                    pool.wait_ge(S["mixB_pool"], g)
                nc.gpsimd.tensor_tensor(t[:, :, 1, :], v[:, :, 0, :], v[:, :, 1, :], ALU.subtract)\
                    .then_inc(S["mixA_pool"], 1)
                pool.wait_ge(S["gu_rn"], g + 1)
                power(rn[:, 4 * g:4 * g + 4], ss[:, 4 * g:4 * g + 4]).then_inc(S["gu_pow"], 1)
                pool.wait_ge(S["mixA_dve"], g + 1)
                pool.wait_ge(S["mixA_pool"], g + 1)
                v2 = raw[g % 3].rearrange("p (f a b) -> p f a b", a=2, b=2 * P)
                t2 = mixed.rearrange("p (f a b) -> p f a b", a=2, b=2 * P)
                nc.gpsimd.tensor_tensor(v2[:, :, 1, :], t2[:, :, 0, :], t2[:, :, 1, :], ALU.subtract)\
                    .then_inc(S["mixB_pool"], 1)

            def down_front():
                pool.wait_ge(S["d_land"], 64)
                pool.wait_ge(S["d_ss"], 16)
                pool.wait_ge(S["heads_ready"], QUADS)
                pool.wait_ge(S["pl_done"], H)
                k = 0
                for dt in range(4):
                    bufs = [[raw[2], raw[0], raw[1], mixed][dt], down_tmp]
                    for st in range(4):
                        if k:
                            pool.wait_ge(S["d_mix_dve"], k)
                            pool.wait_ge(S["d_mix_pool"], k)
                        a, c = [bufs[(st + i) % 2].rearrange("p (q a b) -> p q a b", a=2, b=P << st) for i in (0, 1)]
                        nc.gpsimd.tensor_tensor(c[:, :, 1, :], a[:, :, 0, :], a[:, :, 1, :], ALU.subtract)\
                            .then_inc(S["d_mix_pool"], 1)
                        k += 1
                pool.wait_ge(S["e_ready"], 1)
                link(nc.gpsimd.partition_all_reduce(red[:, 4:5], st4[:, 8:9], P, bass.bass_isa.ReduceOp.add))
                nc.gpsimd.partition_all_reduce(red[:, 5:6], st4[:, 9:10], P, bass.bass_isa.ReduceOp.max)\
                    .then_inc(S["e_reduced"], 1)
                pool.wait_ge(S["e_ready"], 2)
                power(red[:, 7:8], red[:, 6:7]).then_inc(S["e_reduced"], 1)

            def attend(n, s):
                if s < H:
                    h = s
                    pool.wait_ge(S["ph_done"], H * n + h + 1)
                    nc.gpsimd.tensor_tensor(p16[:, 1, h % 4, :], prod[:, h % 2, :], p16[:, 0, h % 4, :], ALU.subtract)\
                        .then_inc(S["pl_done"], 1)
                if s in (4, 8, 12, 16):
                    q = s // 4 - 1
                    pool.wait_ge(S["oh_done"], QUADS * n + q + 1)
                    nc.gpsimd.tensor_tensor(oT[:, 1, q, :], wide[:, :], oT[:, 0, q, :], ALU.subtract)\
                        .then_inc(S["ol_done"], 1)
                if s in (17, 19, 21, 23):
                    m = (s - 17) // 2
                    pool.wait_ge(S["h_stored"], 16)
                    pool.wait_ge(S["o_done"], QUADS * n + QUADS)
                    pool.wait_ge(S["h1_done"], 4 * n + m)
                    nc.gpsimd.indirect_dma_start(h_row[:, :], None, h_table,
                                                 bass.IndirectOffsetOnAxis(ids_c[:, m:m + 1].bitcast(U32), axis=0))\
                        .then_inc(S["hrow_land"], 16)
                if s in (18, 20, 22, 24):
                    m = (s - 18) // 2
                    pool.wait_ge(S["ve_done"], 4 * n + m + 1)
                    power(rstd[:, :], ve[:, :]).then_inc(S["rstd_done"], 1)
                    pool.wait_ge(S["xh_done"], 4 * n + m + 1)
                    nc.gpsimd.tensor_tensor(x16[:, 1, :], wide[:, :], x16[:, 0, :], ALU.subtract)\
                        .then_inc(S["xl_done"], 1)

            def feed(b, s):
                if s < FT:
                    pool.wait_ge(S["ah_done"], FT * b + s + 1)
                    nc.gpsimd.tensor_tensor(hid[:, 1, s, :], a32[:, :], hid[:, 0, s, :], ALU.subtract)\
                        .then_inc(S["al_done"], 1)

            gu_front(0)
            for s in range(SLOTS):
                if s < UNIT_SLOTS and s % 3 == 1 and s // 3 + 1 < GROUPS:
                    gu_front(s // 3 + 1)
                if s == UNIT_SLOTS:
                    down_front()
                attend(0, s)
            with pool.Fori(0, NB - 1) as b:
                for s in range(SLOTS):
                    feed(b, s)
                    attend(b + 1, s)
            for s in range(SLOTS):
                feed(NB - 1, s)

        @block.vector
        def _(dve):
            steps = [0]

            def link(ins):
                steps[0] += 1
                ins.then_inc(S["dve_step"], 1)
                dve.wait_ge(S["dve_step"], steps[0])

            def power_of_two(dst, src):
                return nc.vector.tensor_scalar(dst.bitcast(U32), src.bitcast(U32), EXPONENT, None, ALU.bitwise_and)

            dve.wait_ge(S["emb_ss"], 1)
            nc.vector.tensor_scalar(stat[:, 0:1], stat[:, 10:11], 1.0 / D, 1e-6, ALU.mult, ALU.add).then_inc(S["pow_asked"], 1)
            dve.wait_ge(S["pow_given"], 1)
            nc.vector.scalar_tensor_tensor(embn, emb_s, stat[:, 1:2], nw_b, ALU.mult, ALU.mult).then_inc(S["emb_n"], 1)
            dve.wait_ge(S["wv_sq"], 4)
            nc.vector.tensor_scalar(vn[:, 0:4], vn[:, 12:16], TINY, None, ALU.max).then_inc(S["wv_ss"], 1)
            dve.wait_ge(S["wv_diag"], 1)
            link(power_of_two(vn[:, 4:8], vn[:, 4:8]))
            link(nc.vector.reciprocal(vn[:, 8:12], vn[:, 4:8]))
            dve.wait_ge(S["c_land"], 16)
            for rt in range(DC):
                last = nc.vector.tensor_scalar(diag[:, rt, :], ident, vn[:, 4 + rt:5 + rt], None, ALU.mult)
            last.then_inc(S["wv_diag"], 1)
            dve.wait_ge(S["emb_ss"], 2)
            nc.vector.tensor_scalar(stat[:, 2:3], stat[:, 11:12], 1.0 / D, 1e-6, ALU.mult, ALU.add).then_inc(S["pow_asked"], 1)
            dve.wait_ge(S["pow_given"], 2)
            nc.vector.tensor_scalar(h_tok, banks[7][:, :], stat[:, 3:4], None, ALU.mult).then_inc(S["tok_ready"], 1)
            dve.wait_ge(S["tok_ready"], 1)
            link(nc.vector.bn_stats(bn[:, :], h_tok))
            link(nc.vector.bn_aggr(mv[:, :], bn[:, :]))
            nc.vector.tensor_scalar(stat[:, 4:5], mv[:, 1:2], 1e-5, None, ALU.add).then_inc(S["pow_asked"], 1)
            dve.wait_ge(S["pow_given"], 3)
            nc.vector.tensor_scalar(x1, h_tok, mv[:, 0:1], stat[:, 5:6], ALU.subtract, ALU.mult).then_inc(S["x1_ready"], 1)
            dve.wait_ge(S["wo_sq"], 4)
            nc.vector.reduce_sum(st4[:, 4:5], st4[:, 0:4], AX.X)
            nc.vector.reduce_max(st4[:, 5:6], vn[:, 8:12], AX.X).then_inc(S["wo_scale"], 1)
            dve.wait_ge(S["wo_scale"], 2)
            link(nc.vector.tensor_tensor(red[:, 2:3], red[:, 1:2], red[:, 1:2], ALU.mult))
            nc.vector.scalar_tensor_tensor(red[:, 2:3], red[:, 0:1], TINY, red[:, 2:3], ALU.max, ALU.mult).then_inc(S["wo_scale"], 1)
            dve.wait_ge(S["wo_scale"], 4)
            link(power_of_two(gl[:, 2:3], red[:, 3:4]))
            link(nc.vector.tensor_scalar(vn[:, 0:4], vn[:, 8:12], gl[:, 2:3], 2.0 ** 15, ALU.mult, ALU.mult))
            link(nc.vector.reciprocal(gl[:, 4:5], gl[:, 2:3]))
            nc.vector.tensor_scalar(k_o, gl[:, 4:5], 2.0 ** -15 / V_TOP, None, ALU.mult).then_inc(S["wo_scale"], 1)
            dve.wait_ge(S["par_land"], PARAMS)
            dve.wait_ge(S["qkv_ready"], 1)

            def heads(v, n=2 * H):
                return v.rearrange("p (h d) -> p h d", d=DH)

            def wide_row(v, n):
                return v.rearrange("p (a d) -> p a d", a=1).broadcast_to([P, n, DH])

            for i in range(2):
                last = nc.vector.tensor_tensor(heads(qk[:, 512 * i:512 * i + 512]), heads(banks[2 + i][:, :]),
                                               wide_row(gb[:, 0:32], H), ALU.mult)
            link(last)
            link(nc.vector.tensor_tensor(heads(qk2), heads(qk), wide_row(gb[:, 32:64], 2 * H), ALU.add))
            link(nc.vector.reduce_sum(stat[:, 32:64], heads(qk2), AX.X))
            link(nc.vector.tensor_scalar(stat[:, 32:64], stat[:, 32:64], 1.0 / DH, None, ALU.mult))

            def per_head(v):
                return v.rearrange("p (h a) -> p h a", a=1).broadcast_to([P, 2 * H, DH])

            link(nc.vector.tensor_tensor(heads(qk), heads(qk2), per_head(stat[:, 32:64]), ALU.subtract))
            link(nc.vector.tensor_tensor(qk2, qk, qk, ALU.mult))
            link(nc.vector.reduce_sum(stat[:, 64:96], heads(qk2), AX.X))
            nc.vector.tensor_scalar(stat[:, 64:96], stat[:, 64:96], 1.0 / DH, 1e-5, ALU.mult, ALU.add)\
                .then_inc(S["pow_asked"], 1)
            dve.wait_ge(S["v_hi"], 1)
            nc.vector.scalar_tensor_tensor(val[:, 1, :], banks[4][:, :], V_TOP, val[:, 0, :], ALU.mult, ALU.subtract)\
                .then_inc(S["v_lo"], 1)
            dve.wait_ge(S["pow_given"], 4)
            nc.vector.tensor_tensor(heads(qk2), heads(qk), per_head(stat[:, 96:128]), ALU.mult).then_inc(S["feat_ready"], 1)
            for k in range(DC):
                dve.wait_ge(S["wo_hi"], k + 1)
                nc.vector.scalar_tensor_tensor(wo_t[:, 1, k, :], TURN[k % 2][:, :], vn[:, k:k + 1], wo_t[:, 0, k, :],
                                               ALU.mult, ALU.subtract).then_inc(S["wo_lo"], 1)
            att_v = att[:, :, :, :].rearrange("p l (q j) v -> p l j q v", j=4)
            for j in range(4):
                dve.wait_ge(S["a_hi"], j + 1)
                nc.vector.scalar_tensor_tensor(att_v[:, 1, j, :, :], sq[:, j, :].rearrange("p (q v) -> p q v", v=P), 32.0,
                                               att_v[:, 0, j, :, :], ALU.mult, ALU.subtract).then_inc(S["a_lo"], 1)
            link(nc.vector.tensor_scalar(su_u[:, :], su_u[:, :], W_TOP, None, ALU.mult))

            def gu_front(g):
                c = slice(4 * g, 4 * g + 4)
                v = raw[g % 3].rearrange("p (q a b) -> p q a b", a=2, b=P)
                t = mixed.rearrange("p (q a b) -> p q a b", a=2, b=P)
                dve.wait_ge(S["gu_land%d" % (g % 3)], 16 * (g // 3 + 1))
                if g:
                    dve.wait_ge(S["mixB_dve"], g)
                    dve.wait_ge(S["mixB_pool"], g)
                nc.vector.tensor_tensor(t[:, :, 0, :], v[:, :, 0, :], v[:, :, 1, :], ALU.add).then_inc(S["mixA_dve"], 1)
                dve.wait_ge(S["gu_ss"], 4 * g + 4)
                nc.vector.tensor_scalar(ss[:, c], ss[:, c], TINY, None, ALU.max).then_inc(S["gu_rn"], 1)
                dve.wait_ge(S["mixA_dve"], g + 1)
                dve.wait_ge(S["mixA_pool"], g + 1)
                v2 = raw[g % 3].rearrange("p (f a b) -> p f a b", a=2, b=2 * P)
                t2 = mixed.rearrange("p (f a b) -> p f a b", a=2, b=2 * P)
                nc.vector.tensor_tensor(v2[:, :, 0, :], t2[:, :, 0, :], t2[:, :, 1, :], ALU.add).then_inc(S["mixB_dve"], 1)
                dve.wait_ge(S["gu_pow"], g + 1)
                link(power_of_two(rnp[:, c], rn[:, c]))
                nc.vector.reciprocal(inv[:, c], rnp[:, c])
                if g:
                    dve.wait_ge(S["turned"], 4 * g)
                else:
                    dve.wait_ge(S["t_ready"], 16)
                for i in range(4):
                    last = nc.vector.tensor_scalar(diag[:, i, :], ident, rnp[:, 4 * g + i:4 * g + i + 1], None, ALU.mult)
                last.then_inc(S["gu_diag"], 1)

            def down_front():
                link(nc.vector.scalar_tensor_tensor(sc[:, :], inv, 1.0 / (W_TOP * D ** 0.5), ws_g[:, :], ALU.mult, ALU.mult))
                link(nc.vector.tensor_tensor(ebound[:, :], ws_g[:, 0:FT], ws_g[:, FT:2 * FT], ALU.mult))
                link(nc.vector.tensor_scalar(ebound.bitcast(U32), ebound.bitcast(U32), 0x7FFFFFFF, None, ALU.bitwise_and))
                link(nc.vector.scalar_tensor_tensor(ebound[:, :], inv[:, 0:FT], float(D), ebound[:, :], ALU.mult, ALU.mult))
                link(nc.vector.tensor_tensor(ebound[:, :], inv[:, FT:2 * FT], ebound[:, :], ALU.mult))
                link(nc.vector.tensor_scalar(ebound[:, :], ebound[:, :], TINY, None, ALU.max))
                link(nc.vector.reciprocal(ebound[:, :], ebound[:, :]))
                link(power_of_two(ebound[:, :], ebound[:, :]))
                link(nc.vector.reciprocal(einv, ebound[:, :]))
                link(nc.vector.scalar_tensor_tensor(kap[:, :], ebound[:, :], 2.0 ** 15, sc[:, FT:2 * FT], ALU.mult, ALU.mult))
                dve.wait_ge(S["d_ss"], 16)
                dve.wait_ge(S["d_land"], 64)
                dve.wait_ge(S["heads_ready"], QUADS)
                dve.wait_ge(S["pl_done"], H)
                k = 0
                for dt in range(4):
                    bufs = [[raw[2], raw[0], raw[1], mixed][dt], down_tmp]
                    for st in range(4):
                        if k:
                            dve.wait_ge(S["d_mix_dve"], k)
                            dve.wait_ge(S["d_mix_pool"], k)
                        a, c = [bufs[(st + i) % 2].rearrange("p (q a b) -> p q a b", a=2, b=P << st) for i in (0, 1)]
                        nc.vector.tensor_tensor(c[:, :, 0, :], a[:, :, 0, :], a[:, :, 1, :], ALU.add).then_inc(S["d_mix_dve"], 1)
                        k += 1
                link(nc.vector.reduce_sum(st4[:, 12:16], ssd[:, :].rearrange("p (a b) -> p a b", b=4), AX.X))
                for _ in range(2):
                    link(nc.vector.tensor_tensor(st4[:, 12:16], st4[:, 12:16], ws_d[:, :], ALU.mult))
                nc.vector.reduce_sum(st4[:, 8:9], st4[:, 12:16], AX.X)
                nc.vector.reduce_max(st4[:, 9:10], einv, AX.X).then_inc(S["e_ready"], 1)
                dve.wait_ge(S["turned"], GU_UNITS)
                for i in range(4):
                    last = nc.vector.tensor_scalar(diag[:, i, :], ident, ws_d[:, i:i + 1], None, ALU.mult)
                last.then_inc(S["d_diag"], 1)
                dve.wait_ge(S["e_reduced"], 1)
                link(nc.vector.tensor_tensor(red[:, 6:7], red[:, 5:6], red[:, 5:6], ALU.mult))
                nc.vector.scalar_tensor_tensor(red[:, 6:7], red[:, 4:5], TINY, red[:, 6:7], ALU.max, ALU.mult)\
                    .then_inc(S["e_ready"], 1)
                dve.wait_ge(S["e_reduced"], 2)
                link(power_of_two(gl[:, 3:4], red[:, 7:8]))
                link(nc.vector.tensor_scalar(einv, einv, gl[:, 3:4], 2.0 ** 9, ALU.mult, ALU.mult))
                link(nc.vector.tensor_tensor(su_e[:, :], einv, su_d[:, :], ALU.mult))
                link(nc.vector.reciprocal(gl[:, 5:6], gl[:, 3:4]))
                nc.vector.tensor_scalar(k_d, gl[:, 5:6], 2.0 ** -24 / INTER ** 0.5, None, ALU.mult).then_inc(S["e_ready"], 1)

            def unit(u):
                dve.wait_ge(S["w_hi"], u + 1)
                if u < GU_UNITS:
                    nc.vector.scalar_tensor_tensor(wgu[:, 1, u // 4, u % 4, :], HADA[u % 2][:, :], su_u[:, u % 4:u % 4 + 1],
                                                   wgu[:, 0, u // 4, u % 4, :], ALU.mult, ALU.subtract).then_inc(S["w_lo"], 1)
                else:
                    f = u - GU_UNITS
                    nc.vector.scalar_tensor_tensor(wd[:, 1, f, :], HADA[u % 2][:, :], su_e[:, f:f + 1],
                                                   wd[:, 0, f, :], ALU.mult, ALU.subtract).then_inc(S["w_lo"], 1)

            def ids(n):
                dve.wait_ge(S["ids_land"], 16 * (n + 1))
                dve.wait_ge(S["picked"], H * n)
                nc.vector.tensor_scalar(onehotT[:, :], ids_b[:, :], iota_col, None, ALU.is_equal)\
                    .then_inc(S["onehotT_ready"], 1)
                dve.wait_ge(S["idc_land"], 16 * (n + 1))
                dve.wait_ge(S["onehot_ready"], 2 * n)
                nc.vector.tensor_copy(ids_f[:, :], ids_c[:, :]).then_inc(S["onehot_ready"], 1)
                dve.wait_ge(S["onehot_ready"], 2 * n + 1)
                dve.wait_ge(S["count_ready"], n)
                for c in range(4):
                    last = nc.vector.tensor_scalar(onehot[:, c, :], iota_row, ids_f[:, c:c + 1], None, ALU.is_equal)
                last.then_inc(S["onehot_ready"], 1)

            def attend(n, s):
                if s < H:
                    i = H * n + s
                    dve.wait_ge(S["picked"], i + 1)
                    if s == 0:
                        dve.wait_ge(S["count_copied"], n + 1)
                    if not (isinstance(n, int) and i < 2):
                        dve.wait_ge(S["pl_done"], i - 1)
                    nc.vector.tensor_tensor(prod[:, s % 2, :], PICK[s % 2][:, :], cnt[:, :], ALU.mult)\
                        .then_inc(S["p_done"], 1)
                if s in (4, 8, 12, 16):
                    i = QUADS * n + s // 4 - 1
                    dve.wait_ge(S["heads_ready"], i + 1)
                    dve.wait_ge(S["h1_done"], 4 * n)
                    nc.vector.tensor_tensor(den[:, :].rearrange("p (a b) -> p a b", a=2),
                                            NORM[:, :].rearrange("p (a b) -> p a b", a=2),
                                            eps_row.rearrange("p (a b) -> p a b", a=1).broadcast_to([P, 2, SEQ]),
                                            ALU.add).then_inc(S["den_done"], 1)
                    dve.wait_ge(S["den_done"], i + 1)
                    nc.vector.reciprocal(den[:, :], den[:, :]).then_inc(S["rden_done"], 1)
                    dve.wait_ge(S["rden_done"], i + 1)
                    dve.wait_ge(S["ol_done"], i)
                    dve.wait_ge(S["xl_done"], 4 * n)
                    nc.vector.tensor_tensor(wide[:, :], HEADS[:, :], den[:, :], ALU.mult).then_inc(S["o_done"], 1)
                if s in (18, 20, 22, 24):
                    m = (s - 18) // 2
                    i = 4 * n + m
                    dve.wait_ge(S["wo_ready"], i + 1)
                    dve.wait_ge(S["hrow_land"], 16 * (i + 1))
                    row = h1[:, bass.ds(n % 2, 1), m, :].rearrange("p a d -> p (a d)")
                    nc.vector.scalar_tensor_tensor(row, WOUT[m % 2][:, :], k_o, h_row[:, :], ALU.mult, ALU.add)\
                        .then_inc(S["h1_done"], 1)
                    dve.wait_ge(S["par_land"], PARAMS)
                    dve.wait_ge(S["h1_done"], i + 1)
                    nc.vector.bn_stats(bn[:, :], row).then_inc(S["bn_done"], 1)
                    dve.wait_ge(S["par_land"], PARAMS)
                    dve.wait_ge(S["bn_done"], i + 1)
                    nc.vector.bn_aggr(mv[:, :], bn[:, :]).then_inc(S["mv_done"], 1)
                    dve.wait_ge(S["mv_done"], i + 1)
                    nc.vector.tensor_scalar(ve[:, :], mv[:, 1:2], 1e-5, None, ALU.add).then_inc(S["ve_done"], 1)
                    dve.wait_ge(S["rstd_done"], i + 1)
                    dve.wait_ge(S["xl_done"], i)
                    dve.wait_ge(S["ol_done"], QUADS * n + QUADS)
                    nc.vector.tensor_scalar(wide[:, :], row, mv[:, 0:1], rstd[:, :], ALU.subtract, ALU.mult)\
                        .then_inc(S["xn_done"], 1)

            def feed(b, s):
                if s < FT:
                    i = FT * b + s
                    dve.wait_ge(S["silu_done"], i + 1)
                    dve.wait_ge(S["up_ready"], i + 1)
                    if s:
                        dve.wait_ge(S["al_done"], i)
                    nc.vector.scalar_tensor_tensor(a32[:, :], UP[s % 2][:, :], kap[:, s:s + 1], sg[:, :],
                                                   ALU.mult, ALU.mult).then_inc(S["a_done"], 1)

            def finish(b, m):
                i = 4 * b + m
                dve.wait_ge(S["y_ready"], i + 1)
                if m:
                    dve.wait_ge(S["stored"], 16 * i)
                nc.vector.scalar_tensor_tensor(o_out[:, :], Y[m][:, :], k_d,
                                               h1[:, bass.ds(b % 2, 1), m, :].rearrange("p a d -> p (a d)"),
                                               ALU.mult, ALU.add).then_inc(S["y_done" if m < 3 else "y_last_done"], 1)

            gu_front(0)
            for s in range(SLOTS):
                if s == 0:
                    ids(0)
                if s < UNIT_SLOTS and s % 3 == 1 and s // 3 + 1 < GROUPS:
                    gu_front(s // 3 + 1)
                if s == UNIT_SLOTS:
                    down_front()
                for u in units_of_slot(s):
                    unit(u)
                attend(0, s)
            with dve.Fori(0, NB - 1) as b:
                for s in range(SLOTS):
                    if s == 0:
                        ids(b + 1)
                    feed(b, s)
                    if s in (20, 24, 28):
                        finish(b, (s - 20) // 4)
                    attend(b + 1, s)
                finish(b, 3)
                dve.wait_ge(S["stored"], 64 * b + 64)
            for s in range(SLOTS):
                feed(NB - 1, s)
            for m in range(4):
                finish(NB - 1, m)

        @block.scalar
        def _(act):
            for dst, src in ((c16[:, :], c_half), (ccol[:, :], c_column), (gb[:, 0:DH], rows(gamma, DH)),
                             (gb[:, DH:2 * DH], rows(beta, DH)),
                             (su_u[:, :], su_ug.rearrange("(c p) -> p c", p=P)),
                             (su_d[:, :], su_dp.rearrange("(c p) -> p c", p=P)),
                             (ws_g[:, :].rearrange("p (w c) -> p w c", w=2)[:, 0, :], wsc_ug[INTER:2 * INTER].rearrange("(c p) -> p c", p=P)),
                             (ws_g[:, :].rearrange("p (w c) -> p w c", w=2)[:, 1, :], wsc_ug[0:INTER].rearrange("(c p) -> p c", p=P)),
                             (ws_d[:, :], wsc_dp.rearrange("(c p) -> p c", p=P))):
                nc.scalar.dma_start(dst, src).then_inc(S["par_land"], 16)

            squares = {}

            def square_sum(dst, src, name):
                if squares:
                    act.wait_ge(S[squares["last"]], squares[squares["last"]])
                squares[name] = squares.get(name, 0) + 1
                squares["last"] = name
                nc.scalar.activation(a32[:, :], src, ACT.Square, accum_out=dst).then_inc(S[name], 1)

            def copy(dst, src, **kw):
                return nc.scalar.activation(dst, src, ACT.Copy, **kw)

            act.wait_ge(S["e_land"], 32)
            square_sum(stat[:, 10:11], emb_s, "emb_ss")
            act.wait_ge(S["vt_ready"], 1)
            copy(xTf, banks[6][:, :]).then_inc(S["vt_copied"], 1)

            def small_copy(u):
                act.wait_ge(S["t_ready"], u + 1)
                copy(small_t[u // 4][:, u % 4, :], TURN[u % 2][:, :]).then_inc(S["t_copied"], 1)

            for u in range(4):
                small_copy(u)
            act.wait_ge(S["w_land"], 64)
            for rt in range(DC):
                square_sum(vn[:, 12 + rt:13 + rt], small_raw[3][:, rt, :], "wv_sq")
            act.wait_ge(S["proj_ready"], 1)
            square_sum(stat[:, 11:12], banks[7][:, :], "emb_ss")
            for rt in range(DC):
                square_sum(st4[:, rt:rt + 1], small_raw[4][:, rt, :], "wo_sq")
            for u in range(4, 10):
                small_copy(u)
            act.wait_ge(S["tok_ready"], 1)
            nc.scalar.dma_start(h_table, h_tok).then_inc(S["h_stored"], 16)
            for u in range(10, 16):
                small_copy(u)
            act.wait_ge(S["vt_ready"], 2)
            copy(xTf, banks[6][:, :]).then_inc(S["vt_copied"], 1)
            act.wait_ge(S["qkv_ready"], 1)
            copy(val[:, 0, :], banks[4][:, :], scale=V_TOP).then_inc(S["v_hi"], 1)
            act.wait_ge(S["wo_scale"], 5)
            for k in range(DC):
                act.wait_ge(S["t_ready"], 17 + k)
                copy(wo_t[:, 0, k, :], TURN[k % 2][:, :], scale=vn[:, k:k + 1]).then_inc(S["wo_hi"], 1)
            for i in range(2):
                act.wait_ge(S["qk_turned"], i + 1)
                copy(qkT[:, 512 * i:512 * i + 512], banks[6 + i][:, :]).then_inc(S["qk_copied"], 1)
            act.wait_ge(S["score_ready"], 1)
            att_v = att[:, :, :, :].rearrange("p l (q j) v -> p l j q v", j=4)
            for j in range(4):
                nc.scalar.activation(sq[:, j, :], banks[2 + j][:, :], ACT.Square).then_inc(S["a_sq"], 1)
            for j in range(4):
                act.wait_ge(S["a_sq"], j + 1)
                copy(att_v[:, 0, j, :, :], sq[:, j, :].rearrange("p (q v) -> p q v", v=P), scale=32.0).then_inc(S["a_hi"], 1)

            def gu_front(g):
                act.wait_ge(S["gu_land%d" % (g % 3)], 16 * (g // 3 + 1))
                for i in range(4):
                    square_sum(ss[:, 4 * g + i:4 * g + i + 1], raw[g % 3][:, 512 * i:512 * i + 512], "gu_ss")

            def down_front():
                act.wait_ge(S["d_land"], 64)
                for i in range(16):
                    src = [raw[2], raw[0], raw[1], mixed][i // 4]
                    square_sum(ssd[:, i:i + 1], src[:, 512 * (i % 4):512 * (i % 4) + 512], "d_ss")

            def turn_copy(u):
                act.wait_ge(S["turned"], u + 1)
                if u >= 2:
                    act.wait_ge(S["hada_ready"], u - 1)
                copy(wt[:, u % 2, :], TURN[u % 2][:, :]).then_inc(S["turned_copied"], 1)

            def unit(u):
                if u + 1 < UNITS and u + 1 != GU_UNITS:
                    turn_copy(u + 1)
                act.wait_ge(S["hada_ready"], u + 1)
                if u == 0:
                    act.wait_ge(S["a_lo"], 4)
                    act.wait_ge(S["h_stored"], 16)
                if u < GU_UNITS:
                    copy(wgu[:, 0, u // 4, u % 4, :], HADA[u % 2][:, :], scale=su_u[:, u % 4:u % 4 + 1]).then_inc(S["w_hi"], 1)
                else:
                    f = u - GU_UNITS
                    if f == 0:
                        act.wait_ge(S["e_ready"], 3)
                    copy(wd[:, 0, f, :], HADA[u % 2][:, :], scale=su_e[:, f:f + 1]).then_inc(S["w_hi"], 1)

            def attend(n, s):
                if s == 0:
                    act.wait_ge(S["count_ready"], n + 1)
                    act.wait_ge(S["p_done"], H * n)
                    copy(cnt[:, :], NORM[:, :]).then_inc(S["count_copied"], 1)
                if s < H:
                    i = H * n + s
                    act.wait_ge(S["p_done"], i + 1)
                    if s % 4 == 0:
                        act.wait_ge(S["heads_ready"], QUADS * n + s // 4)
                    copy(p16[:, 0, s % 4, :], prod[:, s % 2, :]).then_inc(S["ph_done"], 1)
                if s in (4, 8, 12, 16):
                    q = s // 4 - 1
                    act.wait_ge(S["o_done"], QUADS * n + q + 1)
                    if s == 4:
                        act.wait_ge(S["wo_ready"], 4 * n)
                    copy(oT[:, 0, q, :], wide[:, :]).then_inc(S["oh_done"], 1)
                if s in (20, 22, 24, 26):
                    m = (s - 20) // 2
                    act.wait_ge(S["flip_ready"], 4 * n + m + 1)
                    if s == 20:
                        act.wait_ge(S["up_ready"], FT * n)
                    copy(xT[:, :, :, m * P:(m + 1) * P],
                         PICK[m % 2][:, :].bitcast(F16).rearrange("p (l k t) -> p l k t", l=2, t=P)).then_inc(S["xT_done"], 1)
                if s in (18, 20, 22, 24):
                    m = (s - 18) // 2
                    act.wait_ge(S["xn_done"], 4 * n + m + 1)
                    act.wait_ge(S["flip_ready"], 4 * n + m)
                    copy(x16[:, 0, :], wide[:, :]).then_inc(S["xh_done"], 1)

            def feed(b, s):
                if s < FT:
                    i = FT * b + s
                    act.wait_ge(S["gate_ready"], i + 1)
                    nc.scalar.activation(sg[:, :], GATE[s % 2][:, :], ACT.Silu, scale=sc[:, s:s + 1]).then_inc(S["silu_done"], 1)
                    act.wait_ge(S["a_done"], i + 1)
                    copy(hid[:, 0, s, :], a32[:, :]).then_inc(S["ah_done"], 1)

            gu_front(0)
            turn_copy(0)
            for s in range(SLOTS):
                if s < UNIT_SLOTS and s % 3 == 1 and s // 3 + 1 < GROUPS:
                    gu_front(s // 3 + 1)
                if s == UNIT_SLOTS:
                    down_front()
                    turn_copy(GU_UNITS)
                for u in units_of_slot(s):
                    unit(u)
                attend(0, s)
            with act.Fori(0, NB - 1) as b:
                for s in range(SLOTS):
                    feed(b, s)
                    attend(b + 1, s)
                act.wait_ge(S["y_ready"], 4 * b + 4)
            for s in range(SLOTS):
                feed(NB - 1, s)

        @block.tensor
        def _(pe):
            mm = nc.tensor.matmul

            def turn(bank, pieces, rights, done):
                for i in range(4):
                    last = mm(bank[:, i * P:(i + 1) * P], pieces(i), rights(i), start=True, stop=True)
                last.then_inc(done, 1)

            def split_mm(dst, w, v, first, final):
                mm(dst, w[0], v[0], start=first, stop=False)
                mm(dst, w[0], v[1], start=False, stop=False)
                return mm(dst, w[1], v[0], start=False, stop=final)

            pe.wait_ge(S["c_land"], 16)
            pe.wait_ge(S["emb_n"], 1)
            turn(banks[6], lambda i: embn[:, i * P:(i + 1) * P], lambda i: ident, S["vt_ready"])

            def small_unit(u):
                if u >= 2 and u < 18:
                    pe.wait_ge(S["t_copied"], u - 1)
                if u >= 18:
                    pe.wait_ge(S["wo_lo"], u - 17)
                w = small_raw[u // 4]
                k = u % 4
                r = (lambda i: diag[:, i, :]) if u // 4 == 3 else (lambda i: ident)
                turn(TURN[u % 2], lambda i: w[:, i, k * P:(k + 1) * P], r, S["t_ready"])

            pe.wait_ge(S["p_land"], 16)
            for u in range(4):
                small_unit(u)
            pe.wait_ge(S["vt_copied"], 1)
            pe.wait_ge(S["t_copied"], 4)
            for k in range(DC):
                last = mm(banks[7][:, :], xTf[:, k * P:(k + 1) * P], small_t[0][:, k, :], start=(k == 0), stop=(k == DC - 1))
            last.then_inc(S["proj_ready"], 1)
            pe.wait_ge(S["w_land"], 64)
            for u in range(4, 16):
                if u == 12:
                    pe.wait_ge(S["wv_diag"], 2)
                small_unit(u)
            pe.wait_ge(S["x1_ready"], 1)
            turn(banks[6], lambda i: x1[:, i * P:(i + 1) * P], lambda i: ident, S["vt_ready"])
            pe.wait_ge(S["vt_copied"], 2)
            pe.wait_ge(S["t_copied"], 16)
            for i in range(3):
                for k in range(DC):
                    last = mm(banks[2 + i][:, :], xTf[:, k * P:(k + 1) * P], small_t[1 + i][:, k, :],
                              start=(k == 0), stop=(k == DC - 1))
            last.then_inc(S["qkv_ready"], 1)
            for u in range(16, 20):
                small_unit(u)
            pe.wait_ge(S["feat_ready"], 1)
            for i in range(2):
                turn(banks[6 + i], lambda j: qk2[:, 512 * i + j * P:512 * i + (j + 1) * P], lambda j: ident, S["qk_turned"])
            pe.wait_ge(S["qk_copied"], 2)
            pe.wait_ge(S["v_lo"], 1)
            for q in range(QUADS):
                for j in range(4):
                    r = slice(DH * j, DH * j + DH)
                    last = mm(banks[2 + j][:, q * P:(q + 1) * P], qkT[r, q * P:(q + 1) * P],
                              qkT[r, 512 + q * P:512 + (q + 1) * P], start=True, stop=True)
            last.then_inc(S["score_ready"], 1)

            def turn_unit(u):
                if u >= 2:
                    pe.wait_ge(S["turned_copied"], u - 1)
                else:
                    pe.wait_ge(S["wo_lo"], 3 + u)
                if u < GU_UNITS:
                    g, k = u // 4, u % 4
                    if k == 0:
                        pe.wait_ge(S["gu_diag"], g + 1)
                        pe.wait_ge(S["mixB_dve"], g + 1)
                        pe.wait_ge(S["mixB_pool"], g + 1)
                    turn(TURN[u % 2], lambda i: raw[g % 3][:, 512 * i + k * P:512 * i + (k + 1) * P],
                         lambda i: diag[:, i, :], S["turned"])
                else:
                    f = u - GU_UNITS
                    if f == 0:
                        pe.wait_ge(S["d_diag"], 1)
                        pe.wait_ge(S["d_mix_dve"], 16)
                        pe.wait_ge(S["d_mix_pool"], 16)
                    turn(TURN[u % 2], lambda i: [raw[2], raw[0], raw[1], mixed][i][:, f * P:(f + 1) * P],
                         lambda i: diag[:, i, :], S["turned"])

            def unit(u):
                if u + 1 < UNITS and u + 1 != GU_UNITS:
                    turn_unit(u + 1)
                pe.wait_ge(S["turned_copied"], u + 1)
                if u >= 2:
                    pe.wait_ge(S["w_lo"], u - 1)
                else:
                    pe.wait_ge(S["a_sq"], 4)
                mm(HADA[u % 2][:, :], hada, wt[:, u % 2, :], start=True, stop=True).then_inc(S["hada_ready"], 1)

            def attend(n, s):
                if s == 0:
                    pe.wait_ge(S["onehot_ready"], 2 * n + 2)
                    pe.wait_ge(S["h1_done"], 4 * n)
                    if isinstance(n, int) and n == 0:
                        pe.wait_ge(S["qk_copied"], 2)
                        pe.wait_ge(S["a_sq"], 4)
                    for i in range(2):
                        c = SEQ * i
                        mm(NORM[:, c:c + SEQ], onehot[:, 2 * i, :], cum0, start=True, stop=False)
                        last = mm(NORM[:, c + P:c + SEQ], onehot[:, 2 * i + 1, :], cum1, start=False, stop=True)
                    last.then_inc(S["count_ready"], 1)
                if s < H:
                    i = H * n + s
                    if s == 0:
                        pe.wait_ge(S["onehotT_ready"], n + 1)
                        pe.wait_ge(S["a_lo"], 4)
                    if s < 2:
                        pe.wait_ge(S["xT_done"], 4 * n)
                    if not (isinstance(n, int) and i < 2):
                        pe.wait_ge(S["p_done"], i - 1)
                    mm(PICK[s % 2][:, :], att[:, 0, s, :], onehotT[:, :], start=True, stop=False)
                    mm(PICK[s % 2][:, :], att[:, 1, s, :], onehotT[:, :], start=False, stop=True).then_inc(S["picked"], 1)
                if s in (4, 8, 12, 16):
                    q = s // 4 - 1
                    pe.wait_ge(S["pl_done"], H * n + 4 * q + 4)
                    pe.wait_ge(S["o_done"], QUADS * n + q)
                    if q == 0:
                        pe.wait_ge(S["count_copied"], n + 1)
                    for w, p in ((0, 0), (0, 1), (1, 0)):
                        for j in range(4):
                            h = 4 * q + j
                            last = mm(HEADS[DH * j:DH * j + DH, :], val[:, w, DH * h:DH * h + DH], p16[:, p, j, :],
                                      start=(w == 0 and p == 0), stop=(w == 1))
                    for p in range(2):
                        for j in range(4):
                            last = mm(NORM[DH * j:DH * j + DH, :], ones16, p16[:, p, j, :], start=(p == 0), stop=(p == 1))
                    last.then_inc(S["heads_ready"], 1)
                if s in (20, 22, 24, 26):
                    m = (s - 20) // 2
                    pe.wait_ge(S["xl_done"], 4 * n + m + 1)
                    if m >= 2:
                        pe.wait_ge(S["xT_done"], 4 * n + m - 1)
                    bank = PICK[m % 2][:, :].bitcast(F16)
                    for i in range(2):
                        for k in range(DC):
                            c = (DC * i + k) * P
                            last = nc.tensor.transpose(bank[:, c:c + P], x16[:, i, k * P:(k + 1) * P], ident16)
                    last.then_inc(S["flip_ready"], 1)
                if s in (18, 20, 22, 24):
                    m = (s - 18) // 2
                    if m == 0:
                        pe.wait_ge(S["ol_done"], QUADS * n + QUADS)
                        pe.wait_ge(S["wo_lo"], 4)
                    if m >= 2:
                        pe.wait_ge(S["h1_done"], 4 * n + m - 1)
                    c = slice(m * P, m * P + P)
                    for k in range(DC):
                        last = split_mm(WOUT[m % 2][:, :], [oT[:, i, k, c] for i in range(2)],
                                        [wo_t[:, i, k, :] for i in range(2)], k == 0, k == DC - 1)
                    last.then_inc(S["wo_ready"], 1)

            def feed(b, s):
                if s < FT:
                    i = FT * b + s
                    if s == 0:
                        pe.wait_ge(S["xT_done"], 4 * b + 4)
                        pe.wait_ge(S["w_lo"], UNITS)
                    if s == 1 and isinstance(b, int):
                        pe.wait_ge(S["y_last_done"], b)
                    if s >= 2:
                        pe.wait_ge(S["a_done"], i - 1)
                    for half, bank, done in ((0, GATE[s % 2], S["gate_ready"]), (1, UP[s % 2], S["up_ready"])):
                        f = half * FT + s
                        c = slice(P * (f % 4), P * (f % 4) + P)
                        for k in range(DC):
                            last = split_mm(bank[:, :], [wgu[:, l, f // 4, k, c] for l in range(2)],
                                            [xT[:, l, k, :] for l in range(2)], k == 0, k == DC - 1)
                        last.then_inc(done, 1)
                else:
                    m, part = (s - FT) // 4, (s - FT) % 4
                    if m == 0:
                        pe.wait_ge(S["al_done"], FT * b + 4 * part + 4)
                        if part == 0:
                            pe.wait_ge(S["silu_done"], FT * b + FT - 1)
                    if m == 1 and part == 0:
                        pe.wait_ge(S["a_done"], FT * b + FT)
                    c = slice(m * P, m * P + P)
                    for f in range(4 * part, 4 * part + 4):
                        last = split_mm(Y[m][:, :], [hid[:, l, f, c] for l in range(2)],
                                        [wd[:, l, f, :] for l in range(2)], f == 0, f == FT - 1)
                    if part == 3:
                        last.then_inc(S["y_ready"], 1)

            turn_unit(0)
            for s in range(SLOTS):
                if s == UNIT_SLOTS:
                    turn_unit(GU_UNITS)
                for u in units_of_slot(s):
                    unit(u)
                attend(0, s)
            with pe.Fori(0, NB - 1) as b:
                for s in range(SLOTS):
                    feed(b, s)
                    attend(b + 1, s)
                pe.wait_ge(S["y_done"], 3 * b + 3)
            for s in range(SLOTS):
                feed(NB - 1, s)


_INS = ["x", "L0_tok_emb_table", "L0_tok_norm_weight", "L0_tok_proj_weight", "L0_attn_Wq", "L0_attn_Wk", "L0_attn_Wv",
        "L0_attn_Wo", "L0_attn_gamma", "L0_attn_beta", "L0_ffn_SU_ug", "L0_ffn_SU_dp", "L0_ffn_Wscale_ug",
        "L0_ffn_Wscale_dp", "L0_ffn_W_up", "L0_ffn_W_gate", "L0_ffn_W_down"]


def constants(seq):
    import numpy as np
    hada = np.ones((1, 1), np.float32)
    while hada.shape[0] < P:
        hada = np.block([[hada, hada], [hada, -hada]])
    ident = np.eye(P, dtype=np.float32)
    place = np.arange(seq)
    weight = 2.0 ** -np.ceil(np.log2(place + 1.0))
    causal = (place[:, None] <= place[None, :]) * weight[None, :]
    half = np.concatenate([ident, causal[:P], causal[P:, P:], np.tile(np.arange(P), (P, 1)), np.ones((P, 32))], axis=1)
    column = np.concatenate([np.tile(1e-5 * A_TOP * weight, (P, 1)), np.arange(P)[:, None]], axis=1)
    return {"c_square": np.concatenate([ident, hada], axis=1), "c_half": half.astype(np.float16),
            "c_column": column.astype(np.float32)}


def kernel(**inputs):
    import numpy as np
    from concourse.bacc import Bacc
    from concourse.bass_utils import run_bass_kernel_spmd

    nc = Bacc("TRN2", target_bir_lowering=False, num_devices=1)
    given = {name: np.ascontiguousarray(inputs[name]) for name in _INS}
    batch, seq = given["x"].shape
    given.update(constants(seq))
    arrays, args = {}, []
    for name, a in given.items():
        arrays[f"in_{name}"] = a
        args.append(nc.dram_tensor(f"in_{name}", a.shape, mybir.dt.from_np(a.dtype), kind="ExternalInput").ap())
    shape = (batch, seq, given["L0_tok_emb_table"].shape[1])
    out = nc.dram_tensor("out", shape, F32, kind="ExternalOutput").ap()
    tower(nc, *args, out)
    return run_bass_kernel_spmd(nc, [arrays], core_ids=[0]).results[0]["out"]
```

```python
from contextlib import ExitStack

import concourse.bass as bass
from concourse import mybir

ALU = mybir.AluOpType
ACT = mybir.ActivationFunctionType
AX = mybir.AxisListType
F32 = mybir.dt.float32
F16 = mybir.dt.float16
I32 = mybir.dt.int32
U32 = mybir.dt.uint32

P = 128
SLOTS = 32
UNIT_SLOTS = 24
W_TOP = 2.0 ** 9
V_TOP = 2.0 ** 10
A_TOP = 2.0 ** 10
TINY = 1e-30
EXPONENT = 0x7F800000


def units_of_slot(s):
    if s < UNIT_SLOTS:
        g = s // 3
        return [[4 * g, 4 * g + 1], [4 * g + 2], [4 * g + 3]][s % 3]
    return [32 + 2 * (s - UNIT_SLOTS), 33 + 2 * (s - UNIT_SLOTS)]


SUMS_AT = (4, 8, 12, 15)
O_FLIP_AT = (5, 9, 13, 17)
ROWS_AT = (17, 20, 23, 26)
WO_AT = (18, 21, 24, 27)
X_FLIP_AT = (21, 24, 27, 30)
DOWN_MIX_AT = ((3, 0, 0), (4, 0, 1), (5, 0, 2), (6, 0, 3), (7, 1, 0), (8, 1, 1), (9, 1, 2), (10, 2, 0), (11, 2, 1),
               (12, 3, 0), (13, 3, 1), (18, 1, 3), (19, 3, 2), (20, 3, 3), (21, 2, 2), (22, 2, 3))
DOWN_SQUARES_AT = (3, 6, 9, 12)


def tower(nc, x, emb, norm_w, proj_w, wq, wk, wv, wo, gamma, beta, su_ug, su_dp, wsc_ug, wsc_dp,
          w_up, w_gate, w_down, c_square, c_half, c_column, out):
    VOCAB, D = emb.shape
    BATCH, SEQ = x.shape
    DH = gamma.shape[0]
    H = D // DH
    INTER = w_up.shape[0]
    DC = D // P
    FT = INTER // P
    T = 512
    NB = BATCH * SEQ // T
    QUADS = H // 4
    GROUPS = 2 * INTER // 512
    GU_UNITS = GROUPS * DC
    UNITS = GU_UNITS + FT
    PARAMS = 9 * 16
    assert VOCAB == P and SEQ == 256 and D == 512 and DH == 32 and FT == 16 and T == 2 * SEQ

    x_rows = x.rearrange("(n s) t -> n (s t)", s=2)
    x_cols = x.rearrange("(n s) (c p) -> n p (s c)", s=2, p=P)
    out_rows = out.rearrange("(n s) (c p) d -> n (s c) p d", s=2, p=P)

    def rows(v, n):
        return v.rearrange("(a n) -> a n", a=1).broadcast_to([P, n])

    ctx = ExitStack()
    with ctx:
        def sb(name, shape, dt=F32):
            return ctx.enter_context(nc.sbuf_tensor(name, shape, dt))

        def sem(name):
            return ctx.enter_context(nc.semaphore(name))

        h_table = nc.dram_tensor("h_table", [VOCAB, D], F32, kind="Internal").ap()

        wgu = sb("wgu", [P, 2, GROUPS, DC, 512], F16)
        wd = sb("wd", [P, 2, FT, D], F16)
        att = sb("att", [P, 2, H, P], F16)
        val = sb("val", [P, 2, H, DH + 1], F16)
        wo_t = sb("wo_t", [P, 2, DC, D], F16)
        c16 = sb("c16", [P, 640], F16)
        ident16, cum0, cum1 = c16[:, 0:128], c16[:, 128:384], c16[:, 384:512]
        iota_row = c16[:, 512:640]
        ccol = sb("ccol", [P, 3])
        eps_col, iota_col = ccol[:, 0:2], ccol[:, 2:3]
        hid = sb("hid", [P, 2, FT, T], F16)
        xT = sb("xT", [P, 2, DC, T], F16)
        h1 = sb("h1", [P, 2, 4, D])
        oT = sb("oT", [P, 2, QUADS, T], F16)
        prod = sb("prod", [P, 2, T])
        p16 = sb("p16", [P, 2, 4, T], F16)
        cnt = sb("cnt", [P, T])
        onehotT = sb("onehotT", [P, T], F16)
        onehot = sb("onehot", [P, 4, P], F16)
        ids_b = sb("ids_b", [P, T], I32)
        ids_c = sb("ids_c", [P, 4], I32)
        ids_f = sb("ids_f", [P, 4])
        wide = sb("wide", [P, D])
        sg = sb("sg", [P, T])
        x16 = sg[:, :].bitcast(F16).rearrange("p (l d) -> p l d", l=2)
        a32 = sb("a32", [P, T])
        h_row = sb("h_row", [P, D])
        o_out = [a32, a32, a32, h_row]
        o16 = h_row[:, :].bitcast(F16).rearrange("p (l d) -> p l d", l=2)
        zr = sb("zr", [P, 4, 4])
        bn = sb("bn", [P, 6])
        mv = sb("mv", [P, 2])
        ve = sb("ve", [P, 1])
        rstd = sb("rstd", [P, 1])
        mhalf = sb("mhalf", [P, 64])
        su_u = sb("su_u", [P, DC])
        su_d = sb("su_d", [P, FT])
        ws_g = sb("ws_g", [P, 2 * FT])
        ws_d = sb("ws_d", [P, DC])
        sc = sb("sc", [P, 2 * FT])
        kap = sb("kap", [P, FT])
        vn = sb("vn", [P, 16])
        gl = sb("gl", [P, 8])
        k_o, k_d = gl[:, 0:1], gl[:, 1:2]

        raw = [hid[:, 0, 0:8, :].rearrange("p a b -> p (a b)").bitcast(F32),
               hid[:, 0, 8:16, :].rearrange("p a b -> p (a b)").bitcast(F32),
               hid[:, 1, 0:8, :].rearrange("p a b -> p (a b)").bitcast(F32)]
        mixed = hid[:, 1, 8:16, :].rearrange("p a b -> p (a b)").bitcast(F32)
        late = h1[:, 1, :, :].rearrange("p a b -> p (a b)")
        wt = late[:, 0:1024].rearrange("p (a b) -> p a b", a=2)
        v_diag, gu_diag, d_diag = [x.rearrange("p (a b) -> p a b", a=4) for x in
                                   (late[:, 1024:1536], a32[:, :], prod[:, 0, :])]
        gu_diags = [gu_diag, v_diag]
        ss, rn, rnp, inv = [late[:, 1792 + 32 * i:1824 + 32 * i] for i in range(4)]
        ebound, einv, su_e, ssd, st4, red = [late[:, 1920 + 16 * i:1936 + 16 * i] for i in range(6)]
        ident, hada = late[:, 1536:1664], late[:, 1664:1792]
        g32 = wgu[:, :, :, :, :].rearrange("p a b c d -> p (a b c d)").bitcast(F32)
        d32 = wd[:, :, :, :].rearrange("p a b c -> p (a b c)").bitcast(F32)
        small_raw = [g32[:, 2048 * i:2048 * (i + 1)].rearrange("p (a b) -> p a b", a=4) for i in range(5)]
        small_t = [g32[:, 10240 + 2048 * i:12288 + 2048 * i].rearrange("p (a b) -> p a b", a=4) for i in range(3)]
        small_t.append(d32[:, 0:2048].rearrange("p (a b) -> p a b", a=4))
        emb_s, embn, nw_b = d32[:, 2048:2560], d32[:, 2560:3072], d32[:, 3072:3584]
        h_tok, x1 = d32[:, 3584:4096], d32[:, 4096:4608]
        xTf = d32[:, 4608:5120]
        qk = d32[:, 5120:6144]
        qk2 = d32[:, 6144:7168]
        gb = d32[:, 7168:7232]
        stat = d32[:, 7232:7360]
        quarter = [d32[:, 2048 * i:2048 * i + 2048] for i in range(4)]
        spare = xT[:, :, :, :].rearrange("p a b c -> p (a b c)").bitcast(F32)
        down_path = [[quarter[0], quarter[1], quarter[0], quarter[1], quarter[3]],
                     [quarter[2], quarter[1], quarter[2], quarter[1], raw[2]],
                     [quarter[0], spare, quarter[0], quarter[1], raw[0]],
                     [quarter[2], spare, quarter[2], quarter[1], mixed]]
        qkT = d32[:, 2048:3072]
        sq = small_raw[0]

        banks = [ctx.enter_context(nc.psum_tensor(f"bank{i}", [P, 512], F32)) for i in range(8)]
        GATE, UP = banks[0:2], banks[2:4]
        Y = banks[0:4]
        PICK = banks[4:6]
        COUNT = banks[7]
        HEADS = [banks[6 + i][:, 0:8 * (DH + 1)].rearrange("p (i d) -> p i d", d=DH + 1) for i in range(2)]
        WOUT = banks[6:8]
        TURN, HADA = banks[0:2], banks[2:4]

        names = """c_land e_land p_land w_land gb_land gu_land0 gu_land1 gu_land2 par_land h_stored
        ids_land idc_land hrow_land stored
        dve_step pool_step act_step
        emb_ss emb_n t_ready t_copied vt_ready vt_copied proj_ready tok_ready x1_ready qkv_ready
        feat_ready score_ready a_sq a_hi a_lo v_hi v_lo wo_hi wo_lo wo_scale
        wv_sq wv_ss wv_diag wo_sq pow_asked pow_given qk_turned qk_copied
        gu_ss gu_rn gu_pow gu_diag mixA_dve mixA_pool mixB_dve mixB_pool
        su_ready turned turned_copied hada_ready w_hi w_lo
        d_land0 d_land1 d_land2 d_land3 d_ss d_mix_dve d_mix_pool d_diag e_ready e_reduced
        onehotT_ready onehot_ready count_ready count_copied picked p_done ph_done pl_done
        heads_ready den_done rden_done o_done oh_done ol_done o_flipped oT_done
        wo_ready h1_done bn_done mv_done ve_done rstd_done xn_done xh_done xl_done
        flip_ready xT_done
        gate_ready up_ready silu_done a_done ah_done al_done y_ready y_done y_last_done""".split()
        S = {n: sem(n) for n in names}

        ctx.enter_context(nc.allow_non_contiguous_dma(reason="short columns"))
        block = ctx.enter_context(nc.Block())

        @block.sync
        def _(sp):
            nc.sync.dma_start(emb_s, emb).then_inc(S["e_land"], 16)
            nc.sync.dma_start(nw_b, rows(norm_w, D)).then_inc(S["e_land"], 16)
            nc.sync.dma_start(late[:, 1536:1792], c_square).then_inc(S["c_land"], 16)
            nc.sync.dma_start(small_raw[0], proj_w.rearrange("(c p) d -> p c d", p=P)).then_inc(S["p_land"], 16)
            for i, w in enumerate((wq, wk, wv)):
                nc.sync.dma_start(small_raw[1 + i], w.rearrange("(c p) d -> p c d", p=P)).then_inc(S["w_land"], 16)
            nc.sync.dma_start(small_raw[4], wo.rearrange("(c p) d -> p c d", p=P)).then_inc(S["w_land"], 16)

            def gu_load(g):
                if g >= 3:
                    sp.wait_ge(S["turned"], 4 * (g - 2))
                src = (w_gate if g < GROUPS // 2 else w_up)[512 * (g % (GROUPS // 2)):512 * (g % (GROUPS // 2)) + 512, :]
                nc.sync.dma_start(raw[g % 3].rearrange("p (a b) -> p a b", a=4),
                                  src.rearrange("(c p) d -> p c d", p=P)).then_inc(S[f"gu_land{g % 3}"], 16)

            def down_load(dt):
                if dt == 0:
                    sp.wait_ge(S["score_ready"], 1)
                    sp.wait_ge(S["feat_ready"], 1)
                    sp.wait_ge(S["v_lo"], 2)
                    sp.wait_ge(S["h_stored"], 16)
                if dt >= 2:
                    for who in ("d_mix_dve", "d_mix_pool"):
                        sp.wait_ge(S[who], 3 if dt == 2 else 7)
                nc.sync.dma_start(down_path[dt][0], w_down[dt * P:(dt + 1) * P, :]).then_inc(S[f"d_land{dt}"], 16)

            for g in range(3):
                gu_load(g)
            nc.sync.dma_start(ids_b[:, :], x_rows[0:1, :].broadcast_to([P, T])).then_inc(S["ids_land"], 16)
            nc.sync.dma_start(ids_c[:, :], x_cols[0, :, :]).then_inc(S["idc_land"], 16)
            down_load(0)
            down_load(1)
            gu_load(3)
            gu_load(4)
            down_load(2)
            gu_load(5)
            down_load(3)
            gu_load(6)
            gu_load(7)

            def load_ids_rows(n):
                sp.wait_ge(S["c_land"], 16)
                sp.wait_ge(S["onehotT_ready"], n)
                nc.sync.dma_start(ids_b[:, :], x_rows[bass.ds(n, 1), :].broadcast_to([P, T])).then_inc(S["ids_land"], 16)

            def load_ids_columns(n):
                sp.wait_ge(S["c_land"], 16)
                sp.wait_ge(S["hrow_land"], 64 * n)
                nc.sync.dma_start(ids_c[:, :], x_cols[bass.ds(n, 1), :, :].rearrange("a p c -> (a p) c"))\
                    .then_inc(S["idc_land"], 16)

            def block_io(b, n):
                for m in range(4):
                    if n is not None and m == 2:
                        load_ids_rows(n)
                    if n is not None and m == 3:
                        load_ids_columns(n)
                    sp.wait_ge(S["c_land"], 16)
                    if m < 3:
                        sp.wait_ge(S["y_done"], 3 * b + m + 1)
                    else:
                        sp.wait_ge(S["y_last_done"], b + 1)
                    nc.sync.dma_start(out_rows[bass.ds(b, 1), m, :, :].rearrange("a p d -> (a p) d"), o_out[m][:, :])\
                        .then_inc(S["stored"], 16)

            load_ids_rows(1)
            load_ids_columns(1)
            with sp.Fori(0, NB - 2) as b:
                block_io(b, b + 2)
            block_io(NB - 2, None)
            block_io(NB - 1, None)
            sp.wait_ge(S["stored"], 16 * 4 * NB)
            sp.wait_ge(S["h_stored"], 16)

        @block.gpsimd
        def _(pool):
            steps = [0]

            def link(ins):
                steps[0] += 1
                ins.then_inc(S["pool_step"], 1)
                pool.wait_ge(S["pool_step"], steps[0])

            link(nc.gpsimd.memset(mhalf[:, :], -0.5))

            def power(dst, src):
                return nc.gpsimd.tensor_tensor(dst, src, mhalf[:, 0:src.shape[1]], ALU.pow)

            def part(v):
                return v[:, :, 0:v.shape[2] * 5 // 8]

            def gu_mix(g, st):
                src, dst = (raw[g % 3], mixed) if st == 0 else (mixed, raw[g % 3])
                v, t = [x.rearrange("p (q a b) -> p q a b", a=2, b=P << st) for x in (src, dst)]
                if st == 0:
                    pool.wait_ge(S["gu_land%d" % (g % 3)], 16 * (g // 3 + 1))
                    if g:
                        pool.wait_ge(S["mixB_dve"], g)
                        pool.wait_ge(S["mixB_pool"], g)
                else:
                    pool.wait_ge(S["gu_rn"], g + 1)
                    pool.wait_ge(S["mixA_dve"], g + 1)
                    pool.wait_ge(S["mixA_pool"], g + 1)
                nc.gpsimd.tensor_tensor(part(t[:, :, 1, :]), part(v[:, :, 0, :]), part(v[:, :, 1, :]), ALU.subtract)\
                    .then_inc(S["mixA_pool" if st == 0 else "mixB_pool"], 1)
                if st == 1:
                    power(rn[:, 4 * g:4 * g + 4], ss[:, 4 * g:4 * g + 4]).then_inc(S["gu_pow"], 1)

            pool.wait_ge(S["pow_asked"], 1)
            power(stat[:, 1:2], stat[:, 0:1]).then_inc(S["pow_given"], 1)
            pool.wait_ge(S["wv_ss"], 1)
            power(vn[:, 4:8], vn[:, 0:4]).then_inc(S["wv_diag"], 1)
            pool.wait_ge(S["pow_asked"], 2)
            power(stat[:, 3:4], stat[:, 2:3]).then_inc(S["pow_given"], 1)
            pool.wait_ge(S["pow_asked"], 3)
            power(stat[:, 5:6], stat[:, 4:5]).then_inc(S["pow_given"], 1)
            pool.wait_ge(S["wo_scale"], 1)
            link(nc.gpsimd.partition_all_reduce(red[:, 0:1], st4[:, 4:5], P, bass.bass_isa.ReduceOp.add))
            nc.gpsimd.partition_all_reduce(red[:, 1:2], st4[:, 5:6], P, bass.bass_isa.ReduceOp.max)\
                .then_inc(S["wo_scale"], 1)
            pool.wait_ge(S["wo_scale"], 3)
            power(red[:, 3:4], red[:, 2:3]).then_inc(S["wo_scale"], 1)
            gu_mix(0, 0)
            gu_mix(0, 1)
            pool.wait_ge(S["pow_asked"], 4)
            power(stat[:, 96:128], stat[:, 64:96]).then_inc(S["pow_given"], 1)
            gu_mix(1, 0)

            def down_mix(k):
                _, dt, st = DOWN_MIX_AT[k]
                if st == 0:
                    pool.wait_ge(S[f"d_land{dt}"], 16)
                if st == 1:
                    pool.wait_ge(S["d_ss"], 4 * dt + 4)
                if k:
                    pool.wait_ge(S["d_mix_dve"], k)
                    pool.wait_ge(S["d_mix_pool"], k)
                if k >= 11:
                    pool.wait_ge(S["turned"], 4 * (7 if (dt, st) == (2, 3) else 6))
                if (dt, st) == (3, 3):
                    pool.wait_ge(S["mixB_dve"], GROUPS)
                    pool.wait_ge(S["mixB_pool"], GROUPS)
                a, c = [x.rearrange("p (q a b) -> p q a b", a=2, b=P << st) for x in down_path[dt][st:st + 2]]
                nc.gpsimd.tensor_tensor(part(c[:, :, 1, :]), part(a[:, :, 0, :]), part(a[:, :, 1, :]), ALU.subtract)\
                    .then_inc(S["d_mix_pool"], 1)

            def down_scale(step):
                if step == 0:
                    pool.wait_ge(S["e_ready"], 1)
                    link(nc.gpsimd.partition_all_reduce(red[:, 4:5], st4[:, 8:9], P, bass.bass_isa.ReduceOp.add))
                    nc.gpsimd.partition_all_reduce(red[:, 5:6], st4[:, 9:10], P, bass.bass_isa.ReduceOp.max)\
                        .then_inc(S["e_reduced"], 1)
                else:
                    pool.wait_ge(S["e_ready"], 2)
                    power(red[:, 7:8], red[:, 6:7]).then_inc(S["e_reduced"], 1)

            def prepare(s):
                g, step = (s + 1) // 3 + 1, (s + 1) % 3
                if g < GROUPS and step < 2:
                    gu_mix(g, step)
                for k in range(len(DOWN_MIX_AT)):
                    if DOWN_MIX_AT[k][0] == s:
                        down_mix(k)
                if s in (21, 22):
                    down_scale(s - 21)

            def product(n, h):
                if h < H:
                    pool.wait_ge(S["ph_done"], H * n + h + 1)
                    nc.gpsimd.tensor_tensor(p16[:, 1, h % 4, :], prod[:, h % 2, :], p16[:, 0, h % 4, :], ALU.subtract)\
                        .then_inc(S["pl_done"], 1)

            def attend(n, s):
                if s in SUMS_AT:
                    q = SUMS_AT.index(s)
                    pool.wait_ge(S["oh_done"], QUADS * n + q + 1)
                    nc.gpsimd.tensor_tensor(o16[:, 1, :], wide[:, :], o16[:, 0, :], ALU.subtract)\
                        .then_inc(S["ol_done"], 1)
                if s in ROWS_AT:
                    m = ROWS_AT.index(s)
                    pool.wait_ge(S["h_stored"], 16)
                    pool.wait_ge(S["o_flipped"], QUADS * n + QUADS)
                    pool.wait_ge(S["h1_done"], 4 * n + m)
                    nc.gpsimd.indirect_dma_start(h_row[:, :], None, h_table,
                                                 bass.IndirectOffsetOnAxis(ids_c[:, m:m + 1].bitcast(U32), axis=0))\
                        .then_inc(S["hrow_land"], 16)
                if s in WO_AT:
                    m = WO_AT.index(s)
                    pool.wait_ge(S["ve_done"], 4 * n + m + 1)
                    power(rstd[:, :], ve[:, :]).then_inc(S["rstd_done"], 1)
                    pool.wait_ge(S["xh_done"], 4 * n + m + 1)
                    nc.gpsimd.tensor_tensor(x16[:, 1, :], wide[:, :], x16[:, 0, :], ALU.subtract)\
                        .then_inc(S["xl_done"], 1)

            def feed(b, s):
                if s < FT:
                    pool.wait_ge(S["ah_done"], FT * b + s + 1)
                    nc.gpsimd.tensor_tensor(hid[:, 1, s, :], a32[:, :], hid[:, 0, s, :], ALU.subtract)\
                        .then_inc(S["al_done"], 1)

            for s in range(SLOTS):
                product(0, s)
                attend(0, s)
                prepare(s)
            with pool.Fori(0, NB - 1) as b:
                for s in range(SLOTS):
                    if s:
                        product(b + 1, s)
                    feed(b, s)
                    if s == 0:
                        product(b + 1, s)
                    attend(b + 1, s)
            for s in range(SLOTS):
                feed(NB - 1, s)

        @block.vector
        def _(dve):
            steps = [0]

            def link(ins):
                steps[0] += 1
                ins.then_inc(S["dve_step"], 1)
                dve.wait_ge(S["dve_step"], steps[0])

            def power_of_two(dst, src):
                return nc.vector.tensor_scalar(dst.bitcast(U32), src.bitcast(U32), EXPONENT, None, ALU.bitwise_and)

            def butterfly(t, v, done):
                k = v.shape[3] * 5 // 8
                nc.vector.tensor_tensor(t[:, :, 0, :], v[:, :, 0, :], v[:, :, 1, :], ALU.add)
                nc.vector.tensor_tensor(t[:, :, 1, k:], v[:, :, 0, k:], v[:, :, 1, k:], ALU.subtract).then_inc(done, 1)

            def gu_mix(g, st):
                src, dst = (raw[g % 3], mixed) if st == 0 else (mixed, raw[g % 3])
                v, t = [x.rearrange("p (q a b) -> p q a b", a=2, b=P << st) for x in (src, dst)]
                if st == 0:
                    dve.wait_ge(S["gu_land%d" % (g % 3)], 16 * (g // 3 + 1))
                    if g:
                        dve.wait_ge(S["mixB_dve"], g)
                        dve.wait_ge(S["mixB_pool"], g)
                    butterfly(t, v, S["mixA_dve"])
                else:
                    c = slice(4 * g, 4 * g + 4)
                    dve.wait_ge(S["gu_ss"], 4 * g + 4)
                    nc.vector.tensor_scalar(ss[:, c], ss[:, c], TINY, None, ALU.max).then_inc(S["gu_rn"], 1)
                    dve.wait_ge(S["mixA_dve"], g + 1)
                    dve.wait_ge(S["mixA_pool"], g + 1)
                    butterfly(t, v, S["mixB_dve"])

            def gu_scale(g):
                c = slice(4 * g, 4 * g + 4)
                dve.wait_ge(S["gu_pow"], g + 1)
                link(power_of_two(rnp[:, c], rn[:, c]))
                nc.vector.reciprocal(inv[:, c], rnp[:, c])
                if g > 1:
                    dve.wait_ge(S["turned"], 4 * (g - 1))
                elif g == 1:
                    dve.wait_ge(S["t_ready"], 16)
                for i in range(4):
                    last = nc.vector.tensor_scalar(gu_diags[g % 2][:, i, :], ident, rnp[:, 4 * g + i:4 * g + i + 1], None, ALU.mult)
                last.then_inc(S["gu_diag"], 1)

            dve.wait_ge(S["emb_ss"], 1)
            nc.vector.tensor_scalar(stat[:, 0:1], stat[:, 10:11], 1.0 / D, 1e-6, ALU.mult, ALU.add).then_inc(S["pow_asked"], 1)
            dve.wait_ge(S["pow_given"], 1)
            nc.vector.scalar_tensor_tensor(embn, emb_s, stat[:, 1:2], nw_b, ALU.mult, ALU.mult).then_inc(S["emb_n"], 1)
            dve.wait_ge(S["wv_sq"], 4)
            nc.vector.tensor_scalar(vn[:, 0:4], vn[:, 12:16], TINY, None, ALU.max).then_inc(S["wv_ss"], 1)
            dve.wait_ge(S["wv_diag"], 1)
            link(power_of_two(vn[:, 4:8], vn[:, 4:8]))
            link(nc.vector.reciprocal(vn[:, 8:12], vn[:, 4:8]))
            dve.wait_ge(S["c_land"], 16)
            for rt in range(DC):
                last = nc.vector.tensor_scalar(v_diag[:, rt, :], ident, vn[:, 4 + rt:5 + rt], None, ALU.mult)
            last.then_inc(S["wv_diag"], 1)
            dve.wait_ge(S["emb_ss"], 2)
            nc.vector.tensor_scalar(stat[:, 2:3], stat[:, 11:12], 1.0 / D, 1e-6, ALU.mult, ALU.add).then_inc(S["pow_asked"], 1)
            dve.wait_ge(S["pow_given"], 2)
            nc.vector.tensor_scalar(h_tok, banks[7][:, :], stat[:, 3:4], None, ALU.mult).then_inc(S["tok_ready"], 1)
            dve.wait_ge(S["tok_ready"], 1)
            link(nc.vector.bn_stats(bn[:, :], h_tok))
            link(nc.vector.bn_aggr(mv[:, :], bn[:, :]))
            nc.vector.tensor_scalar(stat[:, 4:5], mv[:, 1:2], 1e-5, None, ALU.add).then_inc(S["pow_asked"], 1)
            dve.wait_ge(S["pow_given"], 3)
            nc.vector.tensor_scalar(x1, h_tok, mv[:, 0:1], stat[:, 5:6], ALU.subtract, ALU.mult).then_inc(S["x1_ready"], 1)
            dve.wait_ge(S["wo_sq"], 4)
            nc.vector.reduce_sum(st4[:, 4:5], st4[:, 0:4], AX.X)
            nc.vector.reduce_max(st4[:, 5:6], vn[:, 8:12], AX.X).then_inc(S["wo_scale"], 1)
            dve.wait_ge(S["wo_scale"], 2)
            link(nc.vector.tensor_tensor(red[:, 2:3], red[:, 1:2], red[:, 1:2], ALU.mult))
            nc.vector.scalar_tensor_tensor(red[:, 2:3], red[:, 0:1], TINY, red[:, 2:3], ALU.max, ALU.mult).then_inc(S["wo_scale"], 1)
            dve.wait_ge(S["wo_scale"], 4)
            link(power_of_two(gl[:, 2:3], red[:, 3:4]))
            link(nc.vector.tensor_scalar(vn[:, 0:4], vn[:, 8:12], gl[:, 2:3], 2.0 ** 15, ALU.mult, ALU.mult))
            link(nc.vector.reciprocal(gl[:, 4:5], gl[:, 2:3]))
            nc.vector.tensor_scalar(k_o, gl[:, 4:5], 2.0 ** -15 / V_TOP, None, ALU.mult).then_inc(S["wo_scale"], 1)
            nc.vector.memset(val[:, 0, :, DH:DH + 1], 1.0)
            nc.vector.memset(val[:, 1, :, DH:DH + 1], 0.0).then_inc(S["v_lo"], 1)
            gu_mix(0, 0)
            gu_mix(0, 1)
            dve.wait_ge(S["par_land"], PARAMS)
            nc.vector.tensor_scalar(su_u[:, :], su_u[:, :], W_TOP, None, ALU.mult).then_inc(S["su_ready"], 1)
            dve.wait_ge(S["qkv_ready"], 1)

            def heads(v, n=2 * H):
                return v.rearrange("p (h d) -> p h d", d=DH)

            def wide_row(v, n):
                return v.rearrange("p (a d) -> p a d", a=1).broadcast_to([P, n, DH])

            for i in range(2):
                last = nc.vector.tensor_tensor(heads(qk[:, 512 * i:512 * i + 512]), heads(banks[2 + i][:, :]),
                                               wide_row(gb[:, 0:32], H), ALU.mult)
            link(last)
            link(nc.vector.tensor_tensor(heads(qk2), heads(qk), wide_row(gb[:, 32:64], 2 * H), ALU.add))
            link(nc.vector.reduce_sum(stat[:, 32:64], heads(qk2), AX.X))
            link(nc.vector.tensor_scalar(stat[:, 32:64], stat[:, 32:64], 1.0 / DH, None, ALU.mult))

            def per_head(v):
                return v.rearrange("p (h a) -> p h a", a=1).broadcast_to([P, 2 * H, DH])

            link(nc.vector.tensor_tensor(heads(qk), heads(qk2), per_head(stat[:, 32:64]), ALU.subtract))
            link(nc.vector.tensor_tensor(qk2, qk, qk, ALU.mult))
            link(nc.vector.reduce_sum(stat[:, 64:96], heads(qk2), AX.X))
            nc.vector.tensor_scalar(stat[:, 64:96], stat[:, 64:96], 1.0 / DH, 1e-5, ALU.mult, ALU.add)\
                .then_inc(S["pow_asked"], 1)
            dve.wait_ge(S["v_hi"], 1)
            nc.vector.scalar_tensor_tensor(val[:, 1, :, 0:DH], heads(banks[4][:, :]), V_TOP, val[:, 0, :, 0:DH],
                                           ALU.mult, ALU.subtract)\
                .then_inc(S["v_lo"], 1)
            dve.wait_ge(S["pow_given"], 4)
            nc.vector.tensor_tensor(heads(qk2), heads(qk), per_head(stat[:, 96:128]), ALU.mult).then_inc(S["feat_ready"], 1)
            gu_scale(0)
            gu_mix(1, 0)
            for k in range(DC):
                dve.wait_ge(S["wo_hi"], k + 1)
                nc.vector.scalar_tensor_tensor(wo_t[:, 1, k, :], TURN[k % 2][:, :], vn[:, k:k + 1], wo_t[:, 0, k, :],
                                               ALU.mult, ALU.subtract).then_inc(S["wo_lo"], 1)
            att_v = att[:, :, :, :].rearrange("p l (q j) v -> p l j q v", j=4)
            for j in range(4):
                dve.wait_ge(S["a_hi"], j + 1)
                nc.vector.scalar_tensor_tensor(att_v[:, 1, j, :, :], sq[:, j, :].rearrange("p (q v) -> p q v", v=P), 32.0,
                                               att_v[:, 0, j, :, :], ALU.mult, ALU.subtract).then_inc(S["a_lo"], 1)

            def down_bound():
                link(nc.vector.scalar_tensor_tensor(sc[:, :], inv, 1.0 / (W_TOP * D ** 0.5), ws_g[:, :], ALU.mult, ALU.mult))
                link(nc.vector.tensor_tensor(ebound, ws_g[:, 0:FT], ws_g[:, FT:2 * FT], ALU.mult))
                link(nc.vector.tensor_scalar(ebound.bitcast(U32), ebound.bitcast(U32), 0x7FFFFFFF, None, ALU.bitwise_and))
                link(nc.vector.scalar_tensor_tensor(ebound, inv[:, 0:FT], float(D), ebound, ALU.mult, ALU.mult))
                link(nc.vector.tensor_tensor(ebound, inv[:, FT:2 * FT], ebound, ALU.mult))
                link(nc.vector.tensor_scalar(ebound, ebound, TINY, None, ALU.max))
                link(nc.vector.reciprocal(ebound, ebound))
                link(power_of_two(ebound, ebound))
                link(nc.vector.reciprocal(einv, ebound))
                link(nc.vector.scalar_tensor_tensor(kap[:, :], ebound, 2.0 ** 15, sc[:, FT:2 * FT], ALU.mult, ALU.mult))

            def down_mix(k):
                _, dt, st = DOWN_MIX_AT[k]
                if st == 0:
                    dve.wait_ge(S[f"d_land{dt}"], 16)
                if st == 1:
                    dve.wait_ge(S["d_ss"], 4 * dt + 4)
                if k:
                    dve.wait_ge(S["d_mix_dve"], k)
                    dve.wait_ge(S["d_mix_pool"], k)
                if k >= 11:
                    dve.wait_ge(S["turned"], 4 * (7 if (dt, st) == (2, 3) else 6))
                if (dt, st) == (3, 3):
                    dve.wait_ge(S["mixB_dve"], GROUPS)
                    dve.wait_ge(S["mixB_pool"], GROUPS)
                a, c = [x.rearrange("p (q a b) -> p q a b", a=2, b=P << st) for x in down_path[dt][st:st + 2]]
                butterfly(c, a, S["d_mix_dve"])

            def down_scale(step):
                if step == 0:
                    dve.wait_ge(S["d_ss"], 4 * DC)
                    link(nc.vector.reduce_sum(st4[:, 12:16], ssd.rearrange("p (a b) -> p a b", b=4), AX.X))
                    for _ in range(2):
                        link(nc.vector.tensor_tensor(st4[:, 12:16], st4[:, 12:16], ws_d[:, :], ALU.mult))
                    nc.vector.reduce_sum(st4[:, 8:9], st4[:, 12:16], AX.X)
                    nc.vector.reduce_max(st4[:, 9:10], einv, AX.X).then_inc(S["e_ready"], 1)
                    dve.wait_ge(S["pl_done"], H)
                    for i in range(4):
                        last = nc.vector.tensor_scalar(d_diag[:, i, :], ident, ws_d[:, i:i + 1], None, ALU.mult)
                    last.then_inc(S["d_diag"], 1)
                elif step == 1:
                    dve.wait_ge(S["e_reduced"], 1)
                    link(nc.vector.tensor_tensor(red[:, 6:7], red[:, 5:6], red[:, 5:6], ALU.mult))
                    nc.vector.scalar_tensor_tensor(red[:, 6:7], red[:, 4:5], TINY, red[:, 6:7], ALU.max, ALU.mult)\
                        .then_inc(S["e_ready"], 1)
                else:
                    dve.wait_ge(S["e_reduced"], 2)
                    link(power_of_two(gl[:, 3:4], red[:, 7:8]))
                    link(nc.vector.tensor_scalar(einv, einv, gl[:, 3:4], 2.0 ** 9, ALU.mult, ALU.mult))
                    link(nc.vector.tensor_tensor(su_e, einv, su_d[:, :], ALU.mult))
                    link(nc.vector.reciprocal(gl[:, 5:6], gl[:, 3:4]))
                    nc.vector.tensor_scalar(k_d, gl[:, 5:6], 2.0 ** -24 / INTER ** 0.5, None, ALU.mult).then_inc(S["e_ready"], 1)

            def prepare(s):
                g, step = (s + 1) // 3 + 1, (s + 1) % 3
                if g < GROUPS:
                    if step < 2:
                        gu_mix(g, step)
                    else:
                        gu_scale(g)
                for k in range(len(DOWN_MIX_AT)):
                    if DOWN_MIX_AT[k][0] == s:
                        down_mix(k)
                if s == 20:
                    down_bound()
                if s in (21, 22, 23):
                    down_scale(s - 21)

            def unit(u):
                dve.wait_ge(S["w_hi"], u + 1)
                if u < GU_UNITS:
                    nc.vector.scalar_tensor_tensor(wgu[:, 1, u // 4, u % 4, :], HADA[u % 2][:, :], su_u[:, u % 4:u % 4 + 1],
                                                   wgu[:, 0, u // 4, u % 4, :], ALU.mult, ALU.subtract).then_inc(S["w_lo"], 1)
                else:
                    f = u - GU_UNITS
                    nc.vector.scalar_tensor_tensor(wd[:, 1, f, :], HADA[u % 2][:, :], su_e[:, f:f + 1],
                                                   wd[:, 0, f, :], ALU.mult, ALU.subtract).then_inc(S["w_lo"], 1)

            def ids(n):
                dve.wait_ge(S["ids_land"], 16 * (n + 1))
                dve.wait_ge(S["picked"], H * n)
                nc.vector.tensor_scalar(onehotT[:, :], ids_b[:, :], iota_col, None, ALU.is_equal)\
                    .then_inc(S["onehotT_ready"], 1)
                dve.wait_ge(S["idc_land"], 16 * (n + 1))
                dve.wait_ge(S["onehot_ready"], 2 * n)
                nc.vector.tensor_copy(ids_f[:, :], ids_c[:, :]).then_inc(S["onehot_ready"], 1)
                dve.wait_ge(S["onehot_ready"], 2 * n + 1)
                dve.wait_ge(S["count_ready"], n)
                for c in range(4):
                    last = nc.vector.tensor_scalar(onehot[:, c, :], iota_row, ids_f[:, c:c + 1], None, ALU.is_equal)
                last.then_inc(S["onehot_ready"], 1)

            def product(n, s):
                if s < H:
                    i = H * n + s
                    dve.wait_ge(S["picked"], i + 1)
                    if s == 0:
                        dve.wait_ge(S["count_copied"], n + 1)
                    if not (isinstance(n, int) and i < 2):
                        dve.wait_ge(S["pl_done"], i - 1)
                    nc.vector.tensor_tensor(prod[:, s % 2, :], PICK[s % 2][:, :], cnt[:, :], ALU.mult)\
                        .then_inc(S["p_done"], 1)

            def attend(n, s):
                if s in SUMS_AT:
                    i = QUADS * n + SUMS_AT.index(s)
                    dve.wait_ge(S["heads_ready"], i + 1)
                    for k in range(2):
                        z = HEADS[k][:, :, DH:DH + 1].rearrange("p (m h) a -> p m (h a)", m=2)
                        last = nc.vector.tensor_tensor(zr[:, 2 * k:2 * k + 2, :], z,
                                                       eps_col.rearrange("p (m a) -> p m a", a=1).broadcast_to([P, 2, 4]),
                                                       ALU.add)
                    last.then_inc(S["den_done"], 1)
                    dve.wait_ge(S["den_done"], i + 1)
                    nc.vector.reciprocal(zr[:, :, :], zr[:, :, :]).then_inc(S["rden_done"], 1)
                    dve.wait_ge(S["rden_done"], i + 1)
                    dve.wait_ge(S["ol_done"], i)
                    dve.wait_ge(S["xl_done"], 4 * n)
                    for k in range(2):
                        last = nc.vector.tensor_tensor(
                            wide[:, 256 * k:256 * k + 256].rearrange("p (i d) -> p i d", d=DH), HEADS[k][:, :, 0:DH],
                            zr[:, 2 * k:2 * k + 2, :].rearrange("p m (h a) -> p (m h) a", a=1).broadcast_to([P, 8, DH]),
                            ALU.mult)
                    last.then_inc(S["o_done"], 1)
                if s in WO_AT:
                    m = WO_AT.index(s)
                    i = 4 * n + m
                    dve.wait_ge(S["wo_ready"], i + 1)
                    dve.wait_ge(S["hrow_land"], 16 * (i + 1))
                    row = h1[:, bass.ds(n % 2, 1), m, :].rearrange("p a d -> p (a d)")
                    nc.vector.scalar_tensor_tensor(row, WOUT[m % 2][:, :], k_o, h_row[:, :], ALU.mult, ALU.add)\
                        .then_inc(S["h1_done"], 1)
                    dve.wait_ge(S["par_land"], PARAMS)
                    dve.wait_ge(S["h1_done"], i + 1)
                    nc.vector.bn_stats(bn[:, :], row).then_inc(S["bn_done"], 1)
                    dve.wait_ge(S["par_land"], PARAMS)
                    dve.wait_ge(S["bn_done"], i + 1)
                    nc.vector.bn_aggr(mv[:, :], bn[:, :]).then_inc(S["mv_done"], 1)
                    dve.wait_ge(S["mv_done"], i + 1)
                    nc.vector.tensor_scalar(ve[:, :], mv[:, 1:2], 1e-5, None, ALU.add).then_inc(S["ve_done"], 1)
                    dve.wait_ge(S["rstd_done"], i + 1)
                    dve.wait_ge(S["xl_done"], i)
                    dve.wait_ge(S["ol_done"], QUADS * n + QUADS)
                    nc.vector.tensor_scalar(wide[:, :], row, mv[:, 0:1], rstd[:, :], ALU.subtract, ALU.mult)\
                        .then_inc(S["xn_done"], 1)

            def feed(b, s):
                if s < FT:
                    i = FT * b + s
                    dve.wait_ge(S["silu_done"], i + 1)
                    dve.wait_ge(S["up_ready"], i + 1)
                    if s:
                        dve.wait_ge(S["al_done"], i)
                    nc.vector.scalar_tensor_tensor(a32[:, :], UP[s % 2][:, :], kap[:, s:s + 1], sg[:, :],
                                                   ALU.mult, ALU.mult).then_inc(S["a_done"], 1)

            def finish(b, m):
                i = 4 * b + m
                dve.wait_ge(S["y_ready"], i + 1)
                if m:
                    dve.wait_ge(S["stored"], 16 * i)
                nc.vector.scalar_tensor_tensor(o_out[m][:, :], Y[m][:, :], k_d,
                                               h1[:, bass.ds(b % 2, 1), m, :].rearrange("p a d -> p (a d)"),
                                               ALU.mult, ALU.add).then_inc(S["y_done" if m < 3 else "y_last_done"], 1)

            ids(0)
            for s in range(SLOTS):
                product(0, s)
                us = units_of_slot(s)
                unit(us[0])
                attend(0, s)
                prepare(s)
                for u in us[1:]:
                    unit(u)
            with dve.Fori(0, NB - 1) as b:
                for s in range(SLOTS):
                    if s == 0:
                        ids(b + 1)
                    else:
                        product(b + 1, s)
                    feed(b, s)
                    if s == 0:
                        product(b + 1, s)
                    if s in (20, 24, 28):
                        finish(b, (s - 20) // 4)
                    attend(b + 1, s)
                finish(b, 3)
            for s in range(SLOTS):
                feed(NB - 1, s)
            for m in range(4):
                finish(NB - 1, m)

        @block.scalar
        def _(act):
            for dst, src in ((c16[:, :], c_half), (ccol[:, :], c_column), (gb[:, 0:DH], rows(gamma, DH)),
                             (gb[:, DH:2 * DH], rows(beta, DH)),
                             (su_u[:, :], su_ug.rearrange("(c p) -> p c", p=P)),
                             (su_d[:, :], su_dp.rearrange("(c p) -> p c", p=P)),
                             (ws_g[:, :].rearrange("p (w c) -> p w c", w=2)[:, 0, :], wsc_ug[INTER:2 * INTER].rearrange("(c p) -> p c", p=P)),
                             (ws_g[:, :].rearrange("p (w c) -> p w c", w=2)[:, 1, :], wsc_ug[0:INTER].rearrange("(c p) -> p c", p=P)),
                             (ws_d[:, :], wsc_dp.rearrange("(c p) -> p c", p=P))):
                nc.scalar.dma_start(dst, src).then_inc(S["par_land"], 16)

            squares = {}

            def square_sum(dst, src, name):
                if squares:
                    act.wait_ge(S[squares["last"]], squares[squares["last"]])
                squares[name] = squares.get(name, 0) + 1
                squares["last"] = name
                nc.scalar.activation(sg[:, :], src, ACT.Square, accum_out=dst).then_inc(S[name], 1)

            def copy(dst, src, **kw):
                return nc.scalar.activation(dst, src, ACT.Copy, **kw)

            def gu_squares(g):
                act.wait_ge(S["gu_land%d" % (g % 3)], 16 * (g // 3 + 1))
                for i in range(4):
                    square_sum(ss[:, 4 * g + i:4 * g + i + 1], raw[g % 3][:, 512 * i:512 * i + 512], "gu_ss")

            def down_squares(dt):
                act.wait_ge(S[f"d_land{dt}"], 16)
                for i in range(4):
                    src = down_path[dt][0]
                    square_sum(ssd[:, 4 * dt + i:4 * dt + i + 1], src[:, 512 * i:512 * i + 512], "d_ss")

            act.wait_ge(S["e_land"], 32)
            square_sum(stat[:, 10:11], emb_s, "emb_ss")
            act.wait_ge(S["vt_ready"], 1)
            copy(xTf, banks[6][:, :]).then_inc(S["vt_copied"], 1)

            def small_copy(u):
                act.wait_ge(S["t_ready"], u + 1)
                copy(small_t[u // 4][:, u % 4, :], TURN[u % 2][:, :]).then_inc(S["t_copied"], 1)

            for u in range(4):
                small_copy(u)
            act.wait_ge(S["w_land"], 64)
            for rt in range(DC):
                square_sum(vn[:, 12 + rt:13 + rt], small_raw[3][:, rt, :], "wv_sq")
            act.wait_ge(S["proj_ready"], 1)
            square_sum(stat[:, 11:12], banks[7][:, :], "emb_ss")
            for rt in range(DC):
                square_sum(st4[:, rt:rt + 1], small_raw[4][:, rt, :], "wo_sq")
            for u in range(4, 10):
                small_copy(u)
            act.wait_ge(S["tok_ready"], 1)
            nc.scalar.dma_start(h_table, h_tok).then_inc(S["h_stored"], 16)
            for u in range(10, 16):
                small_copy(u)
            act.wait_ge(S["vt_ready"], 2)
            copy(xTf, banks[6][:, :]).then_inc(S["vt_copied"], 1)
            gu_squares(0)
            gu_squares(1)
            act.wait_ge(S["qkv_ready"], 1)
            copy(val[:, 0, :, 0:DH], banks[4][:, :].rearrange("p (h d) -> p h d", d=DH), scale=V_TOP).then_inc(S["v_hi"], 1)
            act.wait_ge(S["wo_scale"], 5)
            for k in range(DC):
                act.wait_ge(S["t_ready"], 17 + k)
                copy(wo_t[:, 0, k, :], TURN[k % 2][:, :], scale=vn[:, k:k + 1]).then_inc(S["wo_hi"], 1)
            for i in range(2):
                act.wait_ge(S["qk_turned"], i + 1)
                copy(qkT[:, 512 * i:512 * i + 512], banks[6 + i][:, :]).then_inc(S["qk_copied"], 1)
            act.wait_ge(S["score_ready"], 1)
            att_v = att[:, :, :, :].rearrange("p l (q j) v -> p l j q v", j=4)
            for j in range(4):
                nc.scalar.activation(sq[:, j, :], banks[2 + j][:, :], ACT.Square).then_inc(S["a_sq"], 1)
            for j in range(4):
                act.wait_ge(S["a_sq"], j + 1)
                copy(att_v[:, 0, j, :, :], sq[:, j, :].rearrange("p (q v) -> p q v", v=P), scale=32.0).then_inc(S["a_hi"], 1)

            def turn_copy(u):
                act.wait_ge(S["turned"], u + 1)
                if u >= 2:
                    act.wait_ge(S["hada_ready"], u - 1)
                copy(wt[:, u % 2, :], TURN[u % 2][:, :]).then_inc(S["turned_copied"], 1)

            def unit(u):
                if u + 1 < UNITS:
                    turn_copy(u + 1)
                act.wait_ge(S["hada_ready"], u + 1)
                if u == 0:
                    act.wait_ge(S["a_lo"], 4)
                    act.wait_ge(S["h_stored"], 16)
                    act.wait_ge(S["su_ready"], 1)
                if u < GU_UNITS:
                    copy(wgu[:, 0, u // 4, u % 4, :], HADA[u % 2][:, :], scale=su_u[:, u % 4:u % 4 + 1]).then_inc(S["w_hi"], 1)
                else:
                    f = u - GU_UNITS
                    if f == 0:
                        act.wait_ge(S["e_ready"], 3)
                    copy(wd[:, 0, f, :], HADA[u % 2][:, :], scale=su_e[:, f:f + 1]).then_inc(S["w_hi"], 1)

            def product(n, s):
                if s == 0:
                    act.wait_ge(S["count_ready"], n + 1)
                    act.wait_ge(S["p_done"], H * n)
                    copy(cnt[:, :], COUNT[:, :]).then_inc(S["count_copied"], 1)
                if s < H:
                    i = H * n + s
                    act.wait_ge(S["p_done"], i + 1)
                    if s % 4 == 0:
                        act.wait_ge(S["heads_ready"], QUADS * n + s // 4)
                    copy(p16[:, 0, s % 4, :], prod[:, s % 2, :]).then_inc(S["ph_done"], 1)

            def attend(n, s):
                if s in SUMS_AT:
                    q = SUMS_AT.index(s)
                    act.wait_ge(S["o_done"], QUADS * n + q + 1)
                    copy(o16[:, 0, :], wide[:, :]).then_inc(S["oh_done"], 1)
                if s in O_FLIP_AT:
                    q = O_FLIP_AT.index(s)
                    act.wait_ge(S["o_flipped"], QUADS * n + q + 1)
                    if q == 0:
                        act.wait_ge(S["wo_ready"], 4 * n)
                    copy(oT[:, :, q, :], banks[6][:, :].bitcast(F16).rearrange("p (l t) -> p l t", l=2))\
                        .then_inc(S["oT_done"], 1)
                if s in X_FLIP_AT:
                    m = X_FLIP_AT.index(s)
                    act.wait_ge(S["flip_ready"], 4 * n + m + 1)
                    if m == 0:
                        act.wait_ge(S["up_ready"], FT * n)
                    copy(xT[:, :, :, m * P:(m + 1) * P],
                         PICK[m % 2][:, :].bitcast(F16).rearrange("p (l k t) -> p l k t", l=2, t=P)).then_inc(S["xT_done"], 1)
                if s in WO_AT:
                    m = WO_AT.index(s)
                    act.wait_ge(S["xn_done"], 4 * n + m + 1)
                    act.wait_ge(S["flip_ready"], 4 * n + m)
                    copy(x16[:, 0, :], wide[:, :]).then_inc(S["xh_done"], 1)

            def feed(b, s):
                if s < FT:
                    i = FT * b + s
                    act.wait_ge(S["gate_ready"], i + 1)
                    nc.scalar.activation(sg[:, :], GATE[s % 2][:, :], ACT.Silu, scale=sc[:, s:s + 1]).then_inc(S["silu_done"], 1)
                    act.wait_ge(S["a_done"], i + 1)
                    copy(hid[:, 0, s, :], a32[:, :]).then_inc(S["ah_done"], 1)

            turn_copy(0)
            for s in range(SLOTS):
                us = units_of_slot(s)
                unit(us[0])
                if s == WO_AT[0]:
                    act.wait_ge(S["d_ss"], 4 * DC)
                    act.wait_ge(S["gu_ss"], 4 * GROUPS)
                product(0, s)
                attend(0, s)
                for u in us[1:]:
                    unit(u)
                if s % 3 == 2 and (s + 1) // 3 + 1 < GROUPS:
                    gu_squares((s + 1) // 3 + 1)
                if s in DOWN_SQUARES_AT:
                    down_squares(DOWN_SQUARES_AT.index(s))
            with act.Fori(0, NB - 1) as b:
                for s in range(SLOTS):
                    if s:
                        product(b + 1, s)
                    feed(b, s)
                    if s == 0:
                        product(b + 1, s)
                    attend(b + 1, s)
                act.wait_ge(S["y_ready"], 4 * b + 4)
                act.wait_ge(S["stored"], 64 * b + 64)
            for s in range(SLOTS):
                feed(NB - 1, s)

        @block.tensor
        def _(pe):
            mm = nc.tensor.matmul

            def turn(bank, pieces, rights, done):
                for i in range(4):
                    if rights is None:
                        last = nc.tensor.transpose(bank[:, i * P:(i + 1) * P], pieces(i), ident)
                    else:
                        last = mm(bank[:, i * P:(i + 1) * P], pieces(i), rights(i), start=True, stop=True)
                last.then_inc(done, 1)

            def split_mm(dst, w, v, first, final):
                mm(dst, w[0], v[0], start=first, stop=False)
                mm(dst, w[0], v[1], start=False, stop=False)
                return mm(dst, w[1], v[0], start=False, stop=final)

            pe.wait_ge(S["c_land"], 16)
            pe.wait_ge(S["emb_n"], 1)
            turn(banks[6], lambda i: embn[:, i * P:(i + 1) * P], None, S["vt_ready"])

            def small_unit(u):
                if u >= 2 and u < 18:
                    pe.wait_ge(S["t_copied"], u - 1)
                if u >= 18:
                    pe.wait_ge(S["wo_lo"], u - 17)
                w = small_raw[u // 4]
                k = u % 4
                r = (lambda i: v_diag[:, i, :]) if u // 4 == 3 else None
                turn(TURN[u % 2], lambda i: w[:, i, k * P:(k + 1) * P], r, S["t_ready"])

            pe.wait_ge(S["p_land"], 16)
            for u in range(4):
                small_unit(u)
            pe.wait_ge(S["vt_copied"], 1)
            pe.wait_ge(S["t_copied"], 4)
            for k in range(DC):
                last = mm(banks[7][:, :], xTf[:, k * P:(k + 1) * P], small_t[0][:, k, :], start=(k == 0), stop=(k == DC - 1))
            last.then_inc(S["proj_ready"], 1)
            pe.wait_ge(S["w_land"], 64)
            for u in range(4, 16):
                if u == 12:
                    pe.wait_ge(S["wv_diag"], 2)
                small_unit(u)
            pe.wait_ge(S["x1_ready"], 1)
            turn(banks[6], lambda i: x1[:, i * P:(i + 1) * P], None, S["vt_ready"])
            pe.wait_ge(S["vt_copied"], 2)
            pe.wait_ge(S["t_copied"], 16)
            for i in range(3):
                for k in range(DC):
                    last = mm(banks[2 + i][:, :], xTf[:, k * P:(k + 1) * P], small_t[1 + i][:, k, :],
                              start=(k == 0), stop=(k == DC - 1))
            last.then_inc(S["qkv_ready"], 1)
            for u in range(16, 20):
                small_unit(u)
            pe.wait_ge(S["feat_ready"], 1)
            for i in range(2):
                turn(banks[6 + i], lambda j: qk2[:, 512 * i + j * P:512 * i + (j + 1) * P], None, S["qk_turned"])
            pe.wait_ge(S["qk_copied"], 2)
            pe.wait_ge(S["v_lo"], 2)
            for q in range(QUADS):
                for j in range(4):
                    r = slice(DH * j, DH * j + DH)
                    last = mm(banks[2 + j][:, q * P:(q + 1) * P], qkT[r, q * P:(q + 1) * P],
                              qkT[r, 512 + q * P:512 + (q + 1) * P], start=True, stop=True)
            last.then_inc(S["score_ready"], 1)

            def turn_unit(u):
                if u >= 2:
                    pe.wait_ge(S["turned_copied"], u - 1)
                else:
                    pe.wait_ge(S["wo_lo"], 3 + u)
                if u < GU_UNITS:
                    g, k = u // 4, u % 4
                    if k == 0:
                        pe.wait_ge(S["gu_diag"], g + 1)
                        pe.wait_ge(S["mixB_dve"], g + 1)
                        pe.wait_ge(S["mixB_pool"], g + 1)
                    turn(TURN[u % 2], lambda i: raw[g % 3][:, 512 * i + k * P:512 * i + (k + 1) * P],
                         lambda i: gu_diags[g % 2][:, i, :], S["turned"])
                else:
                    f = u - GU_UNITS
                    if f == 0:
                        pe.wait_ge(S["d_diag"], 1)
                        pe.wait_ge(S["d_mix_dve"], 16)
                        pe.wait_ge(S["d_mix_pool"], 16)
                    turn(TURN[u % 2], lambda i: down_path[i][-1][:, f * P:(f + 1) * P],
                         lambda i: d_diag[:, i, :], S["turned"])

            def unit(u):
                if u + 1 < UNITS:
                    turn_unit(u + 1)
                pe.wait_ge(S["turned_copied"], u + 1)
                if u >= 2:
                    pe.wait_ge(S["w_lo"], u - 1)
                else:
                    pe.wait_ge(S["a_sq"], 4)
                mm(HADA[u % 2][:, :], hada, wt[:, u % 2, :], start=True, stop=True).then_inc(S["hada_ready"], 1)

            def attend(n, s):
                if s == 0:
                    pe.wait_ge(S["onehot_ready"], 2 * n + 2)
                    pe.wait_ge(S["h1_done"], 4 * n)
                    if isinstance(n, int) and n == 0:
                        pe.wait_ge(S["qk_copied"], 2)
                        pe.wait_ge(S["a_sq"], 4)
                    for i in range(2):
                        c = SEQ * i
                        mm(COUNT[:, c:c + SEQ], onehot[:, 2 * i, :], cum0, start=True, stop=False)
                        last = mm(COUNT[:, c + P:c + SEQ], onehot[:, 2 * i + 1, :], cum1, start=False, stop=True)
                    last.then_inc(S["count_ready"], 1)
                for h in (0, 1) if s == 0 else (s + 1,) if s + 1 < H else ():
                    i = H * n + h
                    if h == 0:
                        pe.wait_ge(S["onehotT_ready"], n + 1)
                        pe.wait_ge(S["a_lo"], 4)
                    if h < 2:
                        pe.wait_ge(S["xT_done"], 4 * n)
                    if not (isinstance(n, int) and i < 2):
                        pe.wait_ge(S["p_done"], i - 1)
                    mm(PICK[h % 2][:, :], att[:, 0, h, :], onehotT[:, :], start=True, stop=False)
                    mm(PICK[h % 2][:, :], att[:, 1, h, :], onehotT[:, :], start=False, stop=True).then_inc(S["picked"], 1)
                if s in SUMS_AT:
                    q = SUMS_AT.index(s)
                    pe.wait_ge(S["pl_done"], H * n + 4 * q + 4)
                    pe.wait_ge(S["oT_done"], QUADS * n + q)
                    if q == 0:
                        pe.wait_ge(S["count_copied"], n + 1)
                    for m in range(4):
                        for j in range(4):
                            for w, p in ((0, 0), (1, 0), (0, 1)):
                                first = m % 2 == 0 and j == 0 and w == 0 and p == 0
                                final = m % 2 == 1 and j == 3 and p == 1
                                last = mm(HEADS[m // 2][:, 4 * (m % 2) + j, :], p16[:, p, j, m * P:(m + 1) * P],
                                          val[:, w, 4 * q + j, :], start=first, stop=final, skip_group_check=True)
                    last.then_inc(S["heads_ready"], 1)
                if s in O_FLIP_AT:
                    q = O_FLIP_AT.index(s)
                    pe.wait_ge(S["ol_done"], QUADS * n + q + 1)
                    bank = banks[6][:, :].bitcast(F16)
                    for l in range(2):
                        for m in range(4):
                            c = (4 * l + m) * P
                            last = nc.tensor.transpose(bank[:, c:c + P], o16[:, l, m * P:(m + 1) * P], ident16)
                    last.then_inc(S["o_flipped"], 1)
                if s in X_FLIP_AT:
                    m = X_FLIP_AT.index(s)
                    pe.wait_ge(S["xl_done"], 4 * n + m + 1)
                    if m >= 2:
                        pe.wait_ge(S["xT_done"], 4 * n + m - 1)
                    bank = PICK[m % 2][:, :].bitcast(F16)
                    for i in range(2):
                        for k in range(DC):
                            c = (DC * i + k) * P
                            last = nc.tensor.transpose(bank[:, c:c + P], x16[:, i, k * P:(k + 1) * P], ident16)
                    last.then_inc(S["flip_ready"], 1)
                if s in WO_AT:
                    m = WO_AT.index(s)
                    if m == 0:
                        pe.wait_ge(S["oT_done"], QUADS * n + QUADS)
                        pe.wait_ge(S["wo_lo"], 4)
                    if m >= 2:
                        pe.wait_ge(S["h1_done"], 4 * n + m - 1)
                    c = slice(m * P, m * P + P)
                    for k in range(DC):
                        last = split_mm(WOUT[m % 2][:, :], [oT[:, i, k, c] for i in range(2)],
                                        [wo_t[:, i, k, :] for i in range(2)], k == 0, k == DC - 1)
                    last.then_inc(S["wo_ready"], 1)

            def feed(b, s):
                if s < FT:
                    i = FT * b + s
                    if s == 0:
                        pe.wait_ge(S["xT_done"], 4 * b + 4)
                        pe.wait_ge(S["w_lo"], UNITS)
                    if s == 1 and isinstance(b, int):
                        pe.wait_ge(S["y_last_done"], b)
                    if s >= 2:
                        pe.wait_ge(S["a_done"], i - 1)
                    for half, bank, done in ((0, GATE[s % 2], S["gate_ready"]), (1, UP[s % 2], S["up_ready"])):
                        f = half * FT + s
                        c = slice(P * (f % 4), P * (f % 4) + P)
                        for k in range(DC):
                            last = split_mm(bank[:, :], [wgu[:, l, f // 4, k, c] for l in range(2)],
                                            [xT[:, l, k, :] for l in range(2)], k == 0, k == DC - 1)
                        last.then_inc(done, 1)
                else:
                    m, part = (s - FT) // 4, (s - FT) % 4
                    if m == 0:
                        pe.wait_ge(S["al_done"], FT * b + 4 * part + 4)
                        if part == 0:
                            pe.wait_ge(S["silu_done"], FT * b + FT - 1)
                    if m == 1 and part == 0:
                        pe.wait_ge(S["a_done"], FT * b + FT)
                    c = slice(m * P, m * P + P)
                    for f in range(4 * part, 4 * part + 4):
                        last = split_mm(Y[m][:, :], [hid[:, l, f, c] for l in range(2)],
                                        [wd[:, l, f, :] for l in range(2)], f == 0, f == FT - 1)
                    if part == 3:
                        last.then_inc(S["y_ready"], 1)

            turn_unit(0)
            for s in range(SLOTS):
                us = units_of_slot(s)
                unit(us[0])
                attend(0, s)
                for u in us[1:]:
                    unit(u)
            with pe.Fori(0, NB - 1) as b:
                for s in range(SLOTS):
                    feed(b, s)
                    attend(b + 1, s)
                pe.wait_ge(S["y_done"], 3 * b + 3)
            for s in range(SLOTS):
                feed(NB - 1, s)


_INS = ["x", "L0_tok_emb_table", "L0_tok_norm_weight", "L0_tok_proj_weight", "L0_attn_Wq", "L0_attn_Wk", "L0_attn_Wv",
        "L0_attn_Wo", "L0_attn_gamma", "L0_attn_beta", "L0_ffn_SU_ug", "L0_ffn_SU_dp", "L0_ffn_Wscale_ug",
        "L0_ffn_Wscale_dp", "L0_ffn_W_up", "L0_ffn_W_gate", "L0_ffn_W_down"]


def constants(seq):
    import numpy as np
    hada = np.ones((1, 1), np.float32)
    while hada.shape[0] < P:
        hada = np.block([[hada, hada], [hada, -hada]])
    ident = np.eye(P, dtype=np.float32)
    place = np.arange(seq)
    weight = 2.0 ** -np.ceil(np.log2(place + 1.0))
    causal = (place[:, None] <= place[None, :]) * weight[None, :]
    half = np.concatenate([ident, causal[:P], causal[P:, P:], np.tile(np.arange(P), (P, 1))], axis=1)
    column = np.concatenate([(1e-5 * A_TOP * weight).reshape(-1, P).T, np.arange(P)[:, None]], axis=1)
    return {"c_square": np.concatenate([ident, hada], axis=1), "c_half": half.astype(np.float16),
            "c_column": column.astype(np.float32)}


def kernel(**inputs):
    import numpy as np
    from concourse.bacc import Bacc
    from concourse.bass_utils import run_bass_kernel_spmd

    nc = Bacc("TRN2", target_bir_lowering=False, num_devices=1)
    given = {name: np.ascontiguousarray(inputs[name]) for name in _INS}
    batch, seq = given["x"].shape
    given.update(constants(seq))
    arrays, args = {}, []
    for name, a in given.items():
        arrays[f"in_{name}"] = a
        args.append(nc.dram_tensor(f"in_{name}", a.shape, mybir.dt.from_np(a.dtype), kind="ExternalInput").ap())
    shape = (batch, seq, given["L0_tok_emb_table"].shape[1])
    out = nc.dram_tensor("out", shape, F32, kind="ExternalOutput").ap()
    tower(nc, *args, out)
    return run_bass_kernel_spmd(nc, [arrays], core_ids=[0]).results[0]["out"]
```

```python
from contextlib import ExitStack

import concourse.bass as bass
from concourse import mybir

ALU = mybir.AluOpType
ACT = mybir.ActivationFunctionType
AX = mybir.AxisListType
F32 = mybir.dt.float32
F16 = mybir.dt.float16
I32 = mybir.dt.int32
U32 = mybir.dt.uint32

P = 128
SLOTS = 32
EARLY = 12
W_TOP = 2.0 ** 9
V_TOP = 2.0 ** 10
A_TOP = 2.0 ** 10
TINY = 1e-30
EXPONENT = 0x7F800000


UNITS_IN_SLOT = (1, 1, 1, 1, 1, 1, 1, 1, 1, 1, 1, 1, 1, 1, 1, 2, 1, 1, 1, 1, 1, 1, 2, 1, 1, 2, 1, 1, 2, 1, 1, 1)


def units_of_slot(s):
    first = EARLY + sum(UNITS_IN_SLOT[:s])
    return list(range(first, first + UNITS_IN_SLOT[s]))


def ahead(s):
    return 1 if s < 15 else 4


SUMS_AT = (4, 8, 12, 15)
O_FLIP_AT = (5, 9, 13, 17)
ROWS_AT = (17, 20, 23, 26)
WO_AT = (18, 21, 24, 27)
X_FLIP_AT = (21, 24, 27, 30)
DOWN_MIX_AT = ((8, 0, 0), (9, 0, 1), (10, 0, 2), (12, 0, 3), (13, 1, 0), (14, 1, 1), (15, 1, 2), (16, 2, 0),
               (17, 2, 1), (18, 3, 0), (19, 3, 1), (20, 3, 2), (21, 2, 2), (24, 1, 3), (25, 3, 3), (26, 2, 3))
DOWN_SQUARES_AT = {12: (1, (0, 1)), 13: (1, (2, 3)), 14: (2, (0,)), 15: (2, (1,)), 16: (2, (2, 3)),
                   17: (3, (0, 1)), 18: (3, (2, 3))}
DOWN_SCALE_AT = (26, 27, 28, 29)


def tower(nc, x, emb, norm_w, proj_w, wq, wk, wv, wo, gamma, beta, su_ug, su_dp, wsc_ug, wsc_dp,
          w_up, w_gate, w_down, c_square, c_half, c_column, out):
    VOCAB, D = emb.shape
    BATCH, SEQ = x.shape
    DH = gamma.shape[0]
    H = D // DH
    INTER = w_up.shape[0]
    DC = D // P
    FT = INTER // P
    T = 512
    NB = BATCH * SEQ // T
    QUADS = H // 4
    GROUPS = 2 * INTER // 512
    GU_UNITS = GROUPS * DC
    UNITS = GU_UNITS + FT
    PARAMS = 9 * 16
    assert VOCAB == P and SEQ == 256 and D == 512 and DH == 32 and FT == 16 and T == 2 * SEQ

    x_rows = x.rearrange("(n s) t -> n (s t)", s=2)
    x_cols = x.rearrange("(n s) (c p) -> n p (s c)", s=2, p=P)
    out_rows = out.rearrange("(n s) (c p) d -> n (s c) p d", s=2, p=P)

    def rows(v, n):
        return v.rearrange("(a n) -> a n", a=1).broadcast_to([P, n])

    ctx = ExitStack()
    with ctx:
        def sb(name, shape, dt=F32):
            return ctx.enter_context(nc.sbuf_tensor(name, shape, dt))

        def sem(name):
            return ctx.enter_context(nc.semaphore(name))

        h_table = nc.dram_tensor("h_table", [VOCAB, D], F32, kind="Internal").ap()

        wgu = sb("wgu", [P, 2, GROUPS, DC, 512], F16)
        wd = sb("wd", [P, 2, FT, D], F16)
        att = sb("att", [P, 2, H, P], F16)
        val = sb("val", [P, 2, H, DH + 1], F16)
        wo_t = sb("wo_t", [P, 2, DC, D], F16)
        c16 = sb("c16", [P, 640], F16)
        ident16, cum0, cum1 = c16[:, 0:128], c16[:, 128:384], c16[:, 384:512]
        iota_row = c16[:, 512:640]
        ccol = sb("ccol", [P, 3])
        eps_col, iota_col = ccol[:, 0:2], ccol[:, 2:3]
        hid = sb("hid", [P, 2, FT, T], F16)
        xT = sb("xT", [P, 2, DC, T], F16)
        h1 = sb("h1", [P, 2, 4, D])
        oT = sb("oT", [P, 2, QUADS, T], F16)
        prod = sb("prod", [P, 2, T])
        p16 = sb("p16", [P, 2, 4, T], F16)
        cnt = sb("cnt", [P, T])
        onehotT = sb("onehotT", [P, T], F16)
        onehot = sb("onehot", [P, 4, P], F16)
        ids_b = sb("ids_b", [P, T], I32)
        ids_c = sb("ids_c", [P, 4], I32)
        ids_f = sb("ids_f", [P, 4])
        wide = sb("wide", [P, D])
        sg = sb("sg", [P, T])
        x16 = sg[:, :].bitcast(F16).rearrange("p (l d) -> p l d", l=2)
        a32 = sb("a32", [P, T])
        h_row = sb("h_row", [P, D])
        o_out = [a32, a32, a32, h_row]
        o16 = h_row[:, :].bitcast(F16).rearrange("p (l d) -> p l d", l=2)
        zr = sb("zr", [P, 4, 4])
        bn = sb("bn", [P, 6])
        mv = sb("mv", [P, 2])
        ve = sb("ve", [P, 1])
        rstd = sb("rstd", [P, 1])
        mhalf = sb("mhalf", [P, 64])
        su_u = sb("su_u", [P, DC])
        su_d = sb("su_d", [P, FT])
        ws_g = sb("ws_g", [P, 2 * FT])
        ws_d = sb("ws_d", [P, DC])
        sc = sb("sc", [P, 2 * FT])
        kap = sb("kap", [P, FT])
        vn = sb("vn", [P, 16])
        gl = sb("gl", [P, 8])
        k_o, k_d = gl[:, 0:1], gl[:, 1:2]

        raw = [hid[:, 0, 0:8, :].rearrange("p a b -> p (a b)").bitcast(F32),
               hid[:, 0, 8:16, :].rearrange("p a b -> p (a b)").bitcast(F32),
               hid[:, 1, 0:8, :].rearrange("p a b -> p (a b)").bitcast(F32)]
        mixed = hid[:, 1, 8:16, :].rearrange("p a b -> p (a b)").bitcast(F32)
        late = h1[:, 1, :, :].rearrange("p a b -> p (a b)")
        wt = late[:, 0:1024].rearrange("p (a b) -> p a b", a=2)
        v_diag, gu_diag = [x.rearrange("p (a b) -> p a b", a=4) for x in (late[:, 1024:1536], a32[:, :])]
        gu_diags = [gu_diag, v_diag]
        d_diag = gu_diag
        ss, rn, rnp, inv = [late[:, 1792 + 32 * i:1824 + 32 * i] for i in range(4)]
        ebound, einv, su_e, ssd, st4, red = [late[:, 1920 + 16 * i:1936 + 16 * i] for i in range(6)]
        ident, hada = late[:, 1536:1664], late[:, 1664:1792]
        g32 = wgu[:, :, :, :, :].rearrange("p a b c d -> p (a b c d)").bitcast(F32)
        d32 = wd[:, :, :, :].rearrange("p a b c -> p (a b c)").bitcast(F32)
        spare = xT[:, :, :, :].rearrange("p a b c -> p (a b c)").bitcast(F32)
        small_raw, small_t = [[v.rearrange("p (a b) -> p a b", a=4) for v in vs] for vs in (
            [spare, p16[:, :, :, :].rearrange("p a b c -> p (a b c)").bitcast(F32), g32[:, 4096:6144], g32[:, 6144:8192],
             h1[:, 0, :, :].rearrange("p a b -> p (a b)")],
            [oT[:, :, :, :].rearrange("p a b c -> p (a b c)").bitcast(F32), g32[:, 12288:14336], g32[:, 14336:16384],
             d32[:, 0:2048]])]
        emb_s, embn, nw_b = d32[:, 2048:2560], d32[:, 2560:3072], d32[:, 3072:3584]
        h_tok, x1 = d32[:, 3584:4096], d32[:, 4096:4608]
        xTf = d32[:, 4608:5120]
        qk = d32[:, 5120:6144]
        qk2 = d32[:, 6144:7168]
        gb = d32[:, 7168:7232]
        stat = d32[:, 7232:7360]
        quarter = [d32[:, 2048 * i:2048 * i + 2048] for i in range(4)]
        table_raw, table_t1, table_t2 = g32[:, 6144:8192], g32[:, 12288:14336], g32[:, 14336:16384]
        down_path = [[table_t1, table_t2, table_t1, table_t2, quarter[3]],
                     [table_raw, table_t2, table_raw, quarter[1], raw[2]],
                     [quarter[0], spare, quarter[0], quarter[2], raw[0]],
                     [quarter[2], spare, quarter[2], spare, mixed]]
        qkT = d32[:, 2048:3072]
        sq = small_raw[2]

        banks = [ctx.enter_context(nc.psum_tensor(f"bank{i}", [P, 512], F32)) for i in range(8)]
        GATE, UP = banks[0:2], banks[2:4]
        Y = banks[0:4]
        PICK = banks[4:6]
        COUNT = banks[7]
        HEADS = [banks[6 + i][:, 0:8 * (DH + 1)].rearrange("p (i d) -> p i d", d=DH + 1) for i in range(2)]
        WOUT = banks[6:8]
        TURN, HADA = banks[0:2], banks[2:4]
        TURN_SMALL, VT, PROJ, QKV, SCORE = banks[4:6], banks[6], banks[7], [banks[7], banks[6], banks[5]], banks[4:8]

        names = """c_land e_land p_land w_land0 w_land1 w_land2 w_land3 gu_land0 gu_land1 gu_land2 par_land h_stored
        ids_land idc_land hrow_land stored
        dve_step pool_step act_step
        emb_ss emb_n t_ready t_copied vt_ready vt_copied proj_ready tok_ready x1_ready qkv_ready
        feat_ready score_ready a_sq a_hi a_lo v_hi v_lo wo_hi wo_lo wo_scale
        wv_sq wv_ss wv_diag wo_sq pow_asked pow_given qk_turned qk_copied
        gu_ss gu_rn gu_pow gu_diag mixA_dve mixA_pool mixB_dve mixB_pool
        su_ready turned turned_copied hada_ready w_hi w_lo
        d_land0 d_land1 d_land2 d_land3 d_ss d_mix_dve d_mix_pool d_diag e_ready e_reduced
        onehotT_ready onehot_ready count_ready count_copied picked p_done ph_done pl_done
        heads_ready den_done rden_done o_done oh_done ol_done o_flipped oT_done
        wo_ready h1_done bn_done mv_done ve_done rstd_done xn_done xh_done xl_done
        flip_ready xT_done
        gate_ready up_ready silu_done a_done ah_done al_done y_ready y_done y_last_done""".split()
        S = {n: sem(n) for n in names}

        ctx.enter_context(nc.allow_non_contiguous_dma(reason="short columns"))
        block = ctx.enter_context(nc.Block())

        @block.sync
        def _(sp):
            nc.sync.dma_start(late[:, 1536:1792], c_square).then_inc(S["c_land"], 16)
            nc.sync.dma_start(emb_s, emb).then_inc(S["e_land"], 16)
            nc.sync.dma_start(nw_b, rows(norm_w, D)).then_inc(S["e_land"], 16)
            nc.sync.dma_start(small_raw[0], proj_w.rearrange("(c p) d -> p c d", p=P)).then_inc(S["p_land"], 16)
            for i, w in ((2, wv), (0, wq), (1, wk), (3, wo)):
                nc.sync.dma_start(small_raw[1 + i], w.rearrange("(c p) d -> p c d", p=P)).then_inc(S[f"w_land{i}"], 16)

            def gu_load(g):
                if g >= 3:
                    sp.wait_ge(S["turned"], 4 * (g - 2))
                src = (w_gate if g < GROUPS // 2 else w_up)[512 * (g % (GROUPS // 2)):512 * (g % (GROUPS // 2)) + 512, :]
                nc.sync.dma_start(raw[g % 3].rearrange("p (a b) -> p a b", a=4),
                                  src.rearrange("(c p) d -> p c d", p=P)).then_inc(S[f"gu_land{g % 3}"], 16)

            def down_load(dt):
                if dt == 0:
                    sp.wait_ge(S["qkv_ready"], 1)
                if dt == 2:
                    sp.wait_ge(S["score_ready"], 1)
                    sp.wait_ge(S["feat_ready"], 1)
                    sp.wait_ge(S["v_lo"], 2)
                    sp.wait_ge(S["h_stored"], 16)
                nc.sync.dma_start(down_path[dt][0], w_down[dt * P:(dt + 1) * P, :]).then_inc(S[f"d_land{dt}"], 16)

            for g in range(3):
                gu_load(g)
            nc.sync.dma_start(ids_b[:, :], x_rows[0:1, :].broadcast_to([P, T])).then_inc(S["ids_land"], 16)
            nc.sync.dma_start(ids_c[:, :], x_cols[0, :, :]).then_inc(S["idc_land"], 16)
            down_load(0)
            gu_load(3)
            gu_load(4)
            down_load(1)
            gu_load(5)
            down_load(2)
            down_load(3)
            gu_load(6)
            gu_load(7)

            def load_ids_rows(n):
                sp.wait_ge(S["c_land"], 16)
                sp.wait_ge(S["onehotT_ready"], n)
                nc.sync.dma_start(ids_b[:, :], x_rows[bass.ds(n, 1), :].broadcast_to([P, T])).then_inc(S["ids_land"], 16)

            def load_ids_columns(n):
                sp.wait_ge(S["c_land"], 16)
                sp.wait_ge(S["hrow_land"], 64 * n)
                nc.sync.dma_start(ids_c[:, :], x_cols[bass.ds(n, 1), :, :].rearrange("a p c -> (a p) c"))\
                    .then_inc(S["idc_land"], 16)

            def block_io(b, n):
                for m in range(4):
                    if n is not None and m == 2:
                        load_ids_rows(n)
                    if n is not None and m == 3:
                        load_ids_columns(n)
                    sp.wait_ge(S["c_land"], 16)
                    if m < 3:
                        sp.wait_ge(S["y_done"], 3 * b + m + 1)
                    else:
                        sp.wait_ge(S["y_last_done"], b + 1)
                    nc.sync.dma_start(out_rows[bass.ds(b, 1), m, :, :].rearrange("a p d -> (a p) d"), o_out[m][:, :])\
                        .then_inc(S["stored"], 16)

            load_ids_rows(1)
            load_ids_columns(1)
            with sp.Fori(0, NB - 2) as b:
                block_io(b, b + 2)
            block_io(NB - 2, None)
            block_io(NB - 1, None)
            sp.wait_ge(S["stored"], 16 * 4 * NB)
            sp.wait_ge(S["h_stored"], 16)

        @block.gpsimd
        def _(pool):
            steps = [0]

            def link(ins):
                steps[0] += 1
                ins.then_inc(S["pool_step"], 1)
                pool.wait_ge(S["pool_step"], steps[0])

            link(nc.gpsimd.memset(mhalf[:, :], -0.5))

            def power(dst, src):
                return nc.gpsimd.tensor_tensor(dst, src, mhalf[:, 0:src.shape[1]], ALU.pow)

            def part(v):
                return v[:, :, 0:v.shape[2] * 6 // 8]

            def gu_mix(g, st):
                src, dst = (raw[g % 3], mixed) if st == 0 else (mixed, raw[g % 3])
                v, t = [x.rearrange("p (q a b) -> p q a b", a=2, b=P << st) for x in (src, dst)]
                if st == 0:
                    pool.wait_ge(S["gu_land%d" % (g % 3)], 16 * (g // 3 + 1))
                    if g:
                        pool.wait_ge(S["mixB_dve"], g)
                        pool.wait_ge(S["mixB_pool"], g)
                else:
                    pool.wait_ge(S["gu_rn"], g + 1)
                    pool.wait_ge(S["mixA_dve"], g + 1)
                    pool.wait_ge(S["mixA_pool"], g + 1)
                nc.gpsimd.tensor_tensor(part(t[:, :, 1, :]), part(v[:, :, 0, :]), part(v[:, :, 1, :]), ALU.subtract)\
                    .then_inc(S["mixA_pool" if st == 0 else "mixB_pool"], 1)
                if st == 1:
                    power(rn[:, 4 * g:4 * g + 4], ss[:, 4 * g:4 * g + 4]).then_inc(S["gu_pow"], 1)

            def down_mix(k):
                _, dt, st = DOWN_MIX_AT[k]
                if st == 0:
                    pool.wait_ge(S[f"d_land{dt}"], 16)
                if st == 1:
                    pool.wait_ge(S["d_ss"], 4 * dt + 4)
                if k:
                    pool.wait_ge(S["d_mix_dve"], k)
                    pool.wait_ge(S["d_mix_pool"], k)
                if k in (13, 15):
                    pool.wait_ge(S["turned"], 4 * (6 if k == 13 else 7))
                if (dt, st) == (3, 3):
                    pool.wait_ge(S["mixB_dve"], GROUPS)
                    pool.wait_ge(S["mixB_pool"], GROUPS)
                a, c = [x.rearrange("p (q a b) -> p q a b", a=2, b=P << st) for x in down_path[dt][st:st + 2]]
                nc.gpsimd.tensor_tensor(part(c[:, :, 1, :]), part(a[:, :, 0, :]), part(a[:, :, 1, :]), ALU.subtract)\
                    .then_inc(S["d_mix_pool"], 1)

            pool.wait_ge(S["pow_asked"], 1)
            power(stat[:, 1:2], stat[:, 0:1]).then_inc(S["pow_given"], 1)
            pool.wait_ge(S["wv_ss"], 1)
            power(vn[:, 4:8], vn[:, 0:4]).then_inc(S["wv_diag"], 1)
            pool.wait_ge(S["pow_asked"], 2)
            power(stat[:, 3:4], stat[:, 2:3]).then_inc(S["pow_given"], 1)
            pool.wait_ge(S["pow_asked"], 3)
            power(stat[:, 5:6], stat[:, 4:5]).then_inc(S["pow_given"], 1)
            pool.wait_ge(S["wo_scale"], 1)
            link(nc.gpsimd.partition_all_reduce(red[:, 0:1], st4[:, 4:5], P, bass.bass_isa.ReduceOp.add))
            nc.gpsimd.partition_all_reduce(red[:, 1:2], st4[:, 5:6], P, bass.bass_isa.ReduceOp.max)\
                .then_inc(S["wo_scale"], 1)
            pool.wait_ge(S["wo_scale"], 3)
            power(red[:, 3:4], red[:, 2:3]).then_inc(S["wo_scale"], 1)
            for g in range(3):
                gu_mix(g, 0)
                gu_mix(g, 1)
            pool.wait_ge(S["pow_asked"], 4)
            power(stat[:, 96:128], stat[:, 64:96]).then_inc(S["pow_given"], 1)
            down_mix(0)
            gu_mix(3, 0)
            gu_mix(3, 1)
            down_mix(1)
            down_mix(2)
            gu_mix(4, 0)
            gu_mix(4, 1)

            def down_scale(step):
                if step == 0:
                    pool.wait_ge(S["e_ready"], 1)
                    link(nc.gpsimd.partition_all_reduce(red[:, 4:5], st4[:, 8:9], P, bass.bass_isa.ReduceOp.add))
                    nc.gpsimd.partition_all_reduce(red[:, 5:6], st4[:, 9:10], P, bass.bass_isa.ReduceOp.max)\
                        .then_inc(S["e_reduced"], 1)
                else:
                    pool.wait_ge(S["e_ready"], 2)
                    power(red[:, 7:8], red[:, 6:7]).then_inc(S["e_reduced"], 1)

            def prepare(u):
                g, step = (u - EARLY + 2) // 4 + 4, (u - EARLY + 2) % 4
                if g < GROUPS and step < 2:
                    gu_mix(g, step)
                for k in range(len(DOWN_MIX_AT)):
                    if DOWN_MIX_AT[k][0] == u:
                        down_mix(k)
                if u in DOWN_SCALE_AT[1:3]:
                    down_scale(u - DOWN_SCALE_AT[1])

            def product(n, h):
                if h < H:
                    pool.wait_ge(S["ph_done"], H * n + h + 1)
                    nc.gpsimd.tensor_tensor(p16[:, 1, h % 4, :], prod[:, h % 2, :], p16[:, 0, h % 4, :], ALU.subtract)\
                        .then_inc(S["pl_done"], 1)

            def attend(n, s):
                if s in SUMS_AT:
                    q = SUMS_AT.index(s)
                    pool.wait_ge(S["oh_done"], QUADS * n + q + 1)
                    nc.gpsimd.tensor_tensor(o16[:, 1, :], wide[:, :], o16[:, 0, :], ALU.subtract)\
                        .then_inc(S["ol_done"], 1)
                if s in ROWS_AT:
                    m = ROWS_AT.index(s)
                    pool.wait_ge(S["h_stored"], 16)
                    pool.wait_ge(S["o_flipped"], QUADS * n + QUADS)
                    pool.wait_ge(S["h1_done"], 4 * n + m)
                    nc.gpsimd.indirect_dma_start(h_row[:, :], None, h_table,
                                                 bass.IndirectOffsetOnAxis(ids_c[:, m:m + 1].bitcast(U32), axis=0))\
                        .then_inc(S["hrow_land"], 16)
                if s in WO_AT:
                    m = WO_AT.index(s)
                    pool.wait_ge(S["ve_done"], 4 * n + m + 1)
                    power(rstd[:, :], ve[:, :]).then_inc(S["rstd_done"], 1)
                    pool.wait_ge(S["xh_done"], 4 * n + m + 1)
                    nc.gpsimd.tensor_tensor(x16[:, 1, :], wide[:, :], x16[:, 0, :], ALU.subtract)\
                        .then_inc(S["xl_done"], 1)

            def feed(b, s):
                if s < FT:
                    pool.wait_ge(S["ah_done"], FT * b + s + 1)
                    nc.gpsimd.tensor_tensor(hid[:, 1, s, :], a32[:, :], hid[:, 0, s, :], ALU.subtract)\
                        .then_inc(S["al_done"], 1)

            for s in range(SLOTS):
                product(0, s)
                attend(0, s)
                for u in units_of_slot(s):
                    prepare(u)
            with pool.Fori(0, NB - 1) as b:
                for s in range(SLOTS):
                    if s:
                        product(b + 1, s)
                    feed(b, s)
                    if s == 0:
                        product(b + 1, s)
                    attend(b + 1, s)
            for s in range(SLOTS):
                feed(NB - 1, s)

        @block.vector
        def _(dve):
            steps = [0]

            def link(ins):
                steps[0] += 1
                ins.then_inc(S["dve_step"], 1)
                dve.wait_ge(S["dve_step"], steps[0])

            def power_of_two(dst, src):
                return nc.vector.tensor_scalar(dst.bitcast(U32), src.bitcast(U32), EXPONENT, None, ALU.bitwise_and)

            def butterfly(t, v, done):
                k = v.shape[3] * 6 // 8
                nc.vector.tensor_tensor(t[:, :, 0, :], v[:, :, 0, :], v[:, :, 1, :], ALU.add)
                nc.vector.tensor_tensor(t[:, :, 1, k:], v[:, :, 0, k:], v[:, :, 1, k:], ALU.subtract).then_inc(done, 1)

            def gu_mix(g, st):
                src, dst = (raw[g % 3], mixed) if st == 0 else (mixed, raw[g % 3])
                v, t = [x.rearrange("p (q a b) -> p q a b", a=2, b=P << st) for x in (src, dst)]
                if st == 0:
                    dve.wait_ge(S["gu_land%d" % (g % 3)], 16 * (g // 3 + 1))
                    if g:
                        dve.wait_ge(S["mixB_dve"], g)
                        dve.wait_ge(S["mixB_pool"], g)
                    butterfly(t, v, S["mixA_dve"])
                else:
                    c = slice(4 * g, 4 * g + 4)
                    dve.wait_ge(S["gu_ss"], 4 * g + 4)
                    nc.vector.tensor_scalar(ss[:, c], ss[:, c], TINY, None, ALU.max).then_inc(S["gu_rn"], 1)
                    dve.wait_ge(S["mixA_dve"], g + 1)
                    dve.wait_ge(S["mixA_pool"], g + 1)
                    butterfly(t, v, S["mixB_dve"])

            def gu_scale(g):
                c = slice(4 * g, 4 * g + 4)
                dve.wait_ge(S["gu_pow"], g + 1)
                link(power_of_two(rnp[:, c], rn[:, c]))
                nc.vector.reciprocal(inv[:, c], rnp[:, c])
                if g > 1:
                    dve.wait_ge(S["turned"], 4 * (g - 1))
                elif g == 1:
                    dve.wait_ge(S["t_ready"], 16)
                nc.vector.tensor_tensor(gu_diags[g % 2], ident.rearrange("p (a b) -> p a b", a=1).broadcast_to([P, 4, P]),
                                        rnp[:, c].rearrange("p (a b) -> p a b", b=1).broadcast_to([P, 4, P]), ALU.mult)\
                    .then_inc(S["gu_diag"], 1)

            def unit(u):
                dve.wait_ge(S["w_hi"], u + 1)
                if u < GU_UNITS:
                    nc.vector.scalar_tensor_tensor(wgu[:, 1, u // 4, u % 4, :], HADA[u % 2][:, :], su_u[:, u % 4:u % 4 + 1],
                                                   wgu[:, 0, u // 4, u % 4, :], ALU.mult, ALU.subtract).then_inc(S["w_lo"], 1)
                else:
                    f = u - GU_UNITS
                    nc.vector.scalar_tensor_tensor(wd[:, 1, f, :], HADA[u % 2][:, :], su_e[:, f:f + 1],
                                                   wd[:, 0, f, :], ALU.mult, ALU.subtract).then_inc(S["w_lo"], 1)

            def down_mix(k):
                _, dt, st = DOWN_MIX_AT[k]
                if st == 0:
                    dve.wait_ge(S[f"d_land{dt}"], 16)
                if st == 1:
                    dve.wait_ge(S["d_ss"], 4 * dt + 4)
                if k:
                    dve.wait_ge(S["d_mix_dve"], k)
                    dve.wait_ge(S["d_mix_pool"], k)
                if k in (13, 15):
                    dve.wait_ge(S["turned"], 4 * (6 if k == 13 else 7))
                if (dt, st) == (3, 3):
                    dve.wait_ge(S["mixB_dve"], GROUPS)
                    dve.wait_ge(S["mixB_pool"], GROUPS)
                a, c = [x.rearrange("p (q a b) -> p q a b", a=2, b=P << st) for x in down_path[dt][st:st + 2]]
                butterfly(c, a, S["d_mix_dve"])

            def ids(n):
                dve.wait_ge(S["ids_land"], 16 * (n + 1))
                dve.wait_ge(S["picked"], H * n)
                nc.vector.tensor_scalar(onehotT[:, :], ids_b[:, :], iota_col, None, ALU.is_equal)\
                    .then_inc(S["onehotT_ready"], 1)
                dve.wait_ge(S["idc_land"], 16 * (n + 1))
                dve.wait_ge(S["onehot_ready"], 2 * n)
                nc.vector.tensor_copy(ids_f[:, :], ids_c[:, :]).then_inc(S["onehot_ready"], 1)
                dve.wait_ge(S["onehot_ready"], 2 * n + 1)
                dve.wait_ge(S["count_ready"], n)
                for c in range(4):
                    last = nc.vector.tensor_scalar(onehot[:, c, :], iota_row, ids_f[:, c:c + 1], None, ALU.is_equal)
                last.then_inc(S["onehot_ready"], 1)

            dve.wait_ge(S["emb_ss"], 1)
            nc.vector.tensor_scalar(stat[:, 0:1], stat[:, 10:11], 1.0 / D, 1e-6, ALU.mult, ALU.add).then_inc(S["pow_asked"], 1)
            dve.wait_ge(S["pow_given"], 1)
            nc.vector.scalar_tensor_tensor(embn, emb_s, stat[:, 1:2], nw_b, ALU.mult, ALU.mult).then_inc(S["emb_n"], 1)
            dve.wait_ge(S["wv_sq"], 4)
            nc.vector.tensor_scalar(vn[:, 0:4], vn[:, 12:16], TINY, None, ALU.max).then_inc(S["wv_ss"], 1)
            dve.wait_ge(S["wv_diag"], 1)
            link(power_of_two(vn[:, 4:8], vn[:, 4:8]))
            link(nc.vector.reciprocal(vn[:, 8:12], vn[:, 4:8]))
            dve.wait_ge(S["c_land"], 16)
            for rt in range(DC):
                last = nc.vector.tensor_scalar(v_diag[:, rt, :], ident, vn[:, 4 + rt:5 + rt], None, ALU.mult)
            last.then_inc(S["wv_diag"], 1)
            dve.wait_ge(S["emb_ss"], 2)
            nc.vector.tensor_scalar(stat[:, 2:3], stat[:, 11:12], 1.0 / D, 1e-6, ALU.mult, ALU.add).then_inc(S["pow_asked"], 1)
            dve.wait_ge(S["pow_given"], 2)
            nc.vector.tensor_scalar(h_tok, PROJ[:, :], stat[:, 3:4], None, ALU.mult).then_inc(S["tok_ready"], 1)
            dve.wait_ge(S["tok_ready"], 1)
            link(nc.vector.bn_stats(bn[:, :], h_tok))
            link(nc.vector.bn_aggr(mv[:, :], bn[:, :]))
            nc.vector.tensor_scalar(stat[:, 4:5], mv[:, 1:2], 1e-5, None, ALU.add).then_inc(S["pow_asked"], 1)
            dve.wait_ge(S["pow_given"], 3)
            nc.vector.tensor_scalar(x1, h_tok, mv[:, 0:1], stat[:, 5:6], ALU.subtract, ALU.mult).then_inc(S["x1_ready"], 1)
            dve.wait_ge(S["wo_sq"], 4)
            nc.vector.reduce_sum(st4[:, 4:5], st4[:, 0:4], AX.X)
            nc.vector.reduce_max(st4[:, 5:6], vn[:, 8:12], AX.X).then_inc(S["wo_scale"], 1)
            dve.wait_ge(S["wo_scale"], 2)
            link(nc.vector.tensor_tensor(red[:, 2:3], red[:, 1:2], red[:, 1:2], ALU.mult))
            nc.vector.scalar_tensor_tensor(red[:, 2:3], red[:, 0:1], TINY, red[:, 2:3], ALU.max, ALU.mult).then_inc(S["wo_scale"], 1)
            dve.wait_ge(S["wo_scale"], 4)
            link(power_of_two(gl[:, 2:3], red[:, 3:4]))
            link(nc.vector.tensor_scalar(vn[:, 0:4], vn[:, 8:12], gl[:, 2:3], 2.0 ** 15, ALU.mult, ALU.mult))
            link(nc.vector.reciprocal(gl[:, 4:5], gl[:, 2:3]))
            nc.vector.tensor_scalar(k_o, gl[:, 4:5], 2.0 ** -15 / V_TOP, None, ALU.mult).then_inc(S["wo_scale"], 1)
            nc.vector.memset(val[:, 0, :, DH:DH + 1], 1.0)
            nc.vector.memset(val[:, 1, :, DH:DH + 1], 0.0).then_inc(S["v_lo"], 1)
            for g in range(3):
                gu_mix(g, 0)
                gu_mix(g, 1)
                if g < 2:
                    gu_scale(g)
            dve.wait_ge(S["par_land"], PARAMS)
            nc.vector.tensor_scalar(su_u[:, :], su_u[:, :], W_TOP, None, ALU.mult).then_inc(S["su_ready"], 1)
            dve.wait_ge(S["qkv_ready"], 1)

            def heads(v, n=2 * H):
                return v.rearrange("p (h d) -> p h d", d=DH)

            def wide_row(v, n):
                return v.rearrange("p (a d) -> p a d", a=1).broadcast_to([P, n, DH])

            dve.wait_ge(S["v_hi"], 1)
            nc.vector.scalar_tensor_tensor(val[:, 1, :, 0:DH], heads(QKV[2][:, :]), V_TOP, val[:, 0, :, 0:DH],
                                           ALU.mult, ALU.subtract).then_inc(S["v_lo"], 1)
            for i in range(2):
                last = nc.vector.tensor_tensor(heads(qk[:, 512 * i:512 * i + 512]), heads(QKV[i][:, :]),
                                               wide_row(gb[:, 0:32], H), ALU.mult)
            link(last)
            unit(0)
            link(nc.vector.tensor_tensor(heads(qk2), heads(qk), wide_row(gb[:, 32:64], 2 * H), ALU.add))
            unit(1)
            link(nc.vector.reduce_sum(stat[:, 32:64], heads(qk2), AX.X))
            link(nc.vector.tensor_scalar(stat[:, 32:64], stat[:, 32:64], 1.0 / DH, None, ALU.mult))

            def per_head(v):
                return v.rearrange("p (h a) -> p h a", a=1).broadcast_to([P, 2 * H, DH])

            link(nc.vector.tensor_tensor(heads(qk), heads(qk2), per_head(stat[:, 32:64]), ALU.subtract))
            unit(2)
            link(nc.vector.tensor_tensor(qk2, qk, qk, ALU.mult))
            link(nc.vector.reduce_sum(stat[:, 64:96], heads(qk2), AX.X))
            nc.vector.tensor_scalar(stat[:, 64:96], stat[:, 64:96], 1.0 / DH, 1e-5, ALU.mult, ALU.add)\
                .then_inc(S["pow_asked"], 1)
            unit(3)

            def wo_low(k):
                dve.wait_ge(S["wo_hi"], k + 1)
                nc.vector.scalar_tensor_tensor(wo_t[:, 1, k, :], TURN_SMALL[k % 2][:, :], vn[:, k:k + 1], wo_t[:, 0, k, :],
                                               ALU.mult, ALU.subtract).then_inc(S["wo_lo"], 1)

            wo_low(0)
            wo_low(1)
            gu_scale(2)
            unit(4)
            unit(5)
            wo_low(2)
            wo_low(3)
            ids(0)
            dve.wait_ge(S["pow_given"], 4)
            nc.vector.tensor_tensor(heads(qk2), heads(qk), per_head(stat[:, 96:128]), ALU.mult).then_inc(S["feat_ready"], 1)
            down_mix(0)
            unit(6)
            gu_mix(3, 0)
            unit(7)
            gu_mix(3, 1)
            unit(8)
            down_mix(1)
            unit(9)
            gu_scale(3)
            att_v = att[:, :, :, :].rearrange("p l (q j) v -> p l j q v", j=4)
            for j in range(4):
                dve.wait_ge(S["a_hi"], j + 1)
                nc.vector.scalar_tensor_tensor(att_v[:, 1, j, :, :], sq[:, j, :].rearrange("p (q v) -> p q v", v=P), 32.0,
                                               att_v[:, 0, j, :, :], ALU.mult, ALU.subtract).then_inc(S["a_lo"], 1)
            unit(10)
            down_mix(2)

            def down_bound():
                link(nc.vector.scalar_tensor_tensor(sc[:, :], inv, 1.0 / (W_TOP * D ** 0.5), ws_g[:, :], ALU.mult, ALU.mult))
                link(nc.vector.tensor_tensor(ebound, ws_g[:, 0:FT], ws_g[:, FT:2 * FT], ALU.mult))
                link(nc.vector.tensor_scalar(ebound.bitcast(U32), ebound.bitcast(U32), 0x7FFFFFFF, None, ALU.bitwise_and))
                link(nc.vector.scalar_tensor_tensor(ebound, inv[:, 0:FT], float(D), ebound, ALU.mult, ALU.mult))
                link(nc.vector.tensor_tensor(ebound, inv[:, FT:2 * FT], ebound, ALU.mult))
                link(nc.vector.tensor_scalar(ebound, ebound, TINY, None, ALU.max))
                link(nc.vector.reciprocal(ebound, ebound))
                link(power_of_two(ebound, ebound))
                link(nc.vector.reciprocal(einv, ebound))
                link(nc.vector.scalar_tensor_tensor(kap[:, :], ebound, 2.0 ** 15, sc[:, FT:2 * FT], ALU.mult, ALU.mult))

            def down_scale(step):
                if step == 0:
                    dve.wait_ge(S["d_ss"], 4 * DC)
                    link(nc.vector.reduce_sum(st4[:, 12:16], ssd.rearrange("p (a b) -> p a b", b=4), AX.X))
                    for _ in range(2):
                        link(nc.vector.tensor_tensor(st4[:, 12:16], st4[:, 12:16], ws_d[:, :], ALU.mult))
                    nc.vector.reduce_sum(st4[:, 8:9], st4[:, 12:16], AX.X)
                    nc.vector.reduce_max(st4[:, 9:10], einv, AX.X).then_inc(S["e_ready"], 1)
                    dve.wait_ge(S["turned"], 28)
                    for i in range(4):
                        last = nc.vector.tensor_scalar(d_diag[:, i, :], ident, ws_d[:, i:i + 1], None, ALU.mult)
                    last.then_inc(S["d_diag"], 1)
                elif step == 1:
                    dve.wait_ge(S["e_reduced"], 1)
                    link(nc.vector.tensor_tensor(red[:, 6:7], red[:, 5:6], red[:, 5:6], ALU.mult))
                    nc.vector.scalar_tensor_tensor(red[:, 6:7], red[:, 4:5], TINY, red[:, 6:7], ALU.max, ALU.mult)\
                        .then_inc(S["e_ready"], 1)
                else:
                    dve.wait_ge(S["e_reduced"], 2)
                    link(power_of_two(gl[:, 3:4], red[:, 7:8]))
                    link(nc.vector.tensor_scalar(einv, einv, gl[:, 3:4], 2.0 ** 9, ALU.mult, ALU.mult))
                    link(nc.vector.tensor_tensor(su_e, einv, su_d[:, :], ALU.mult))
                    link(nc.vector.reciprocal(gl[:, 5:6], gl[:, 3:4]))
                    nc.vector.tensor_scalar(k_d, gl[:, 5:6], 2.0 ** -24 / INTER ** 0.5, None, ALU.mult).then_inc(S["e_ready"], 1)

            def prepare(u):
                g, step = (u - EARLY + 2) // 4 + 4, (u - EARLY + 2) % 4
                if g < GROUPS:
                    if step < 2:
                        gu_mix(g, step)
                    elif step == 2:
                        gu_scale(g)
                for k in range(len(DOWN_MIX_AT)):
                    if DOWN_MIX_AT[k][0] == u:
                        down_mix(k)
                if u == DOWN_SCALE_AT[0]:
                    down_bound()
                if u in DOWN_SCALE_AT[1:]:
                    down_scale(u - DOWN_SCALE_AT[1])

            def product(n, s):
                if s < H:
                    i = H * n + s
                    dve.wait_ge(S["picked"], i + 1)
                    if s == 0:
                        dve.wait_ge(S["count_copied"], n + 1)
                    if not (isinstance(n, int) and i < 2):
                        dve.wait_ge(S["pl_done"], i - 1)
                    nc.vector.tensor_tensor(prod[:, s % 2, :], PICK[s % 2][:, :], cnt[:, :], ALU.mult)\
                        .then_inc(S["p_done"], 1)

            def attend(n, s):
                if s in SUMS_AT:
                    i = QUADS * n + SUMS_AT.index(s)
                    dve.wait_ge(S["heads_ready"], i + 1)
                    for k in range(2):
                        z = HEADS[k][:, :, DH:DH + 1].rearrange("p (m h) a -> p m (h a)", m=2)
                        last = nc.vector.tensor_tensor(zr[:, 2 * k:2 * k + 2, :], z,
                                                       eps_col.rearrange("p (m a) -> p m a", a=1).broadcast_to([P, 2, 4]),
                                                       ALU.add)
                    last.then_inc(S["den_done"], 1)
                    dve.wait_ge(S["den_done"], i + 1)
                    nc.vector.reciprocal(zr[:, :, :], zr[:, :, :]).then_inc(S["rden_done"], 1)
                    dve.wait_ge(S["rden_done"], i + 1)
                    dve.wait_ge(S["ol_done"], i)
                    dve.wait_ge(S["xl_done"], 4 * n)
                    for k in range(2):
                        last = nc.vector.tensor_tensor(
                            wide[:, 256 * k:256 * k + 256].rearrange("p (i d) -> p i d", d=DH), HEADS[k][:, :, 0:DH],
                            zr[:, 2 * k:2 * k + 2, :].rearrange("p m (h a) -> p (m h) a", a=1).broadcast_to([P, 8, DH]),
                            ALU.mult)
                    last.then_inc(S["o_done"], 1)
                if s in WO_AT:
                    m = WO_AT.index(s)
                    i = 4 * n + m
                    dve.wait_ge(S["wo_ready"], i + 1)
                    dve.wait_ge(S["hrow_land"], 16 * (i + 1))
                    row = h1[:, bass.ds(n % 2, 1), m, :].rearrange("p a d -> p (a d)")
                    nc.vector.scalar_tensor_tensor(row, WOUT[m % 2][:, :], k_o, h_row[:, :], ALU.mult, ALU.add)\
                        .then_inc(S["h1_done"], 1)
                    dve.wait_ge(S["par_land"], PARAMS)
                    dve.wait_ge(S["h1_done"], i + 1)
                    nc.vector.bn_stats(bn[:, :], row).then_inc(S["bn_done"], 1)
                    dve.wait_ge(S["par_land"], PARAMS)
                    dve.wait_ge(S["bn_done"], i + 1)
                    nc.vector.bn_aggr(mv[:, :], bn[:, :]).then_inc(S["mv_done"], 1)
                    dve.wait_ge(S["mv_done"], i + 1)
                    nc.vector.tensor_scalar(ve[:, :], mv[:, 1:2], 1e-5, None, ALU.add).then_inc(S["ve_done"], 1)
                    dve.wait_ge(S["rstd_done"], i + 1)
                    dve.wait_ge(S["xl_done"], i)
                    dve.wait_ge(S["ol_done"], QUADS * n + QUADS)
                    nc.vector.tensor_scalar(wide[:, :], row, mv[:, 0:1], rstd[:, :], ALU.subtract, ALU.mult)\
                        .then_inc(S["xn_done"], 1)

            def feed(b, s):
                if s < FT:
                    i = FT * b + s
                    dve.wait_ge(S["silu_done"], i + 1)
                    dve.wait_ge(S["up_ready"], i + 1)
                    if s:
                        dve.wait_ge(S["al_done"], i)
                    nc.vector.scalar_tensor_tensor(a32[:, :], UP[s % 2][:, :], kap[:, s:s + 1], sg[:, :],
                                                   ALU.mult, ALU.mult).then_inc(S["a_done"], 1)

            def finish(b, m):
                i = 4 * b + m
                dve.wait_ge(S["y_ready"], i + 1)
                if m:
                    dve.wait_ge(S["stored"], 16 * i)
                nc.vector.scalar_tensor_tensor(o_out[m][:, :], Y[m][:, :], k_d,
                                               h1[:, bass.ds(b % 2, 1), m, :].rearrange("p a d -> p (a d)"),
                                               ALU.mult, ALU.add).then_inc(S["y_done" if m < 3 else "y_last_done"], 1)

            gu_mix(4, 0)
            unit(11)
            gu_mix(4, 1)
            for s in range(SLOTS):
                product(0, s)
                us = units_of_slot(s)
                for u in us[:ahead(s)]:
                    unit(u)
                attend(0, s)
                for u in us[:ahead(s)]:
                    prepare(u)
                for u in us[ahead(s):]:
                    unit(u)
                    prepare(u)
            with dve.Fori(0, NB - 1) as b:
                for s in range(SLOTS):
                    if s == 0:
                        ids(b + 1)
                    else:
                        product(b + 1, s)
                    feed(b, s)
                    if s == 0:
                        product(b + 1, s)
                    if s in (20, 24, 28):
                        finish(b, (s - 20) // 4)
                    attend(b + 1, s)
                finish(b, 3)
            for s in range(SLOTS):
                feed(NB - 1, s)
            for m in range(4):
                finish(NB - 1, m)

        @block.scalar
        def _(act):
            squares = {}

            def square_sum(dst, src, name):
                if squares:
                    act.wait_ge(S[squares["last"]], squares[squares["last"]])
                squares[name] = squares.get(name, 0) + 1
                squares["last"] = name
                nc.scalar.activation(sg[:, :], src, ACT.Square, accum_out=dst).then_inc(S[name], 1)

            def copy(dst, src, **kw):
                return nc.scalar.activation(dst, src, ACT.Copy, **kw)

            def gu_squares(g, rows_of_four=range(4)):
                act.wait_ge(S["gu_land%d" % (g % 3)], 16 * (g // 3 + 1))
                for i in rows_of_four:
                    square_sum(ss[:, 4 * g + i:4 * g + i + 1], raw[g % 3][:, 512 * i:512 * i + 512], "gu_ss")

            def down_squares(dt, rows_of_four):
                act.wait_ge(S[f"d_land{dt}"], 16)
                for i in rows_of_four:
                    src = down_path[dt][0]
                    square_sum(ssd[:, 4 * dt + i:4 * dt + i + 1], src[:, 512 * i:512 * i + 512], "d_ss")

            def turn_copy(u):
                act.wait_ge(S["turned"], u + 1)
                if u >= 2:
                    act.wait_ge(S["hada_ready"], u - 1)
                copy(wt[:, u % 2, :], TURN[u % 2][:, :]).then_inc(S["turned_copied"], 1)

            def unit(u):
                if u + 1 < UNITS:
                    turn_copy(u + 1)
                act.wait_ge(S["hada_ready"], u + 1)
                if u == 0:
                    act.wait_ge(S["su_ready"], 1)
                if u == 16:
                    act.wait_ge(S["a_lo"], 4)
                    act.wait_ge(S["h_stored"], 16)
                if u < GU_UNITS:
                    copy(wgu[:, 0, u // 4, u % 4, :], HADA[u % 2][:, :], scale=su_u[:, u % 4:u % 4 + 1]).then_inc(S["w_hi"], 1)
                else:
                    f = u - GU_UNITS
                    if f == 0:
                        act.wait_ge(S["e_ready"], 3)
                    copy(wd[:, 0, f, :], HADA[u % 2][:, :], scale=su_e[:, f:f + 1]).then_inc(S["w_hi"], 1)

            act.wait_ge(S["e_land"], 32)
            square_sum(stat[:, 10:11], emb_s, "emb_ss")
            for dst, src in ((c16[:, :], c_half), (ccol[:, :], c_column), (gb[:, 0:DH], rows(gamma, DH)),
                             (gb[:, DH:2 * DH], rows(beta, DH)),
                             (su_u[:, :], su_ug.rearrange("(c p) -> p c", p=P)),
                             (su_d[:, :], su_dp.rearrange("(c p) -> p c", p=P)),
                             (ws_g[:, :].rearrange("p (w c) -> p w c", w=2)[:, 0, :], wsc_ug[INTER:2 * INTER].rearrange("(c p) -> p c", p=P)),
                             (ws_g[:, :].rearrange("p (w c) -> p w c", w=2)[:, 1, :], wsc_ug[0:INTER].rearrange("(c p) -> p c", p=P)),
                             (ws_d[:, :], wsc_dp.rearrange("(c p) -> p c", p=P))):
                nc.scalar.dma_start(dst, src).then_inc(S["par_land"], 16)

            def small_copy(u):
                act.wait_ge(S["t_ready"], u + 1)
                copy(small_t[u // 4][:, u % 4, :], TURN_SMALL[u % 2][:, :]).then_inc(S["t_copied"], 1)

            for u in range(4):
                small_copy(u)
                if u == 1:
                    act.wait_ge(S["vt_ready"], 1)
                    copy(xTf, VT[:, :]).then_inc(S["vt_copied"], 1)
            act.wait_ge(S["w_land2"], 16)
            for rt in range(DC):
                square_sum(vn[:, 12 + rt:13 + rt], small_raw[3][:, rt, :], "wv_sq")
            act.wait_ge(S["proj_ready"], 1)
            square_sum(stat[:, 11:12], PROJ[:, :], "emb_ss")
            for u in range(4, 10):
                small_copy(u)
            act.wait_ge(S["tok_ready"], 1)
            nc.scalar.dma_start(h_table, h_tok).then_inc(S["h_stored"], 16)
            act.wait_ge(S["w_land3"], 16)
            for rt in range(DC):
                square_sum(st4[:, rt:rt + 1], small_raw[4][:, rt, :], "wo_sq")
            for u in range(10, 16):
                small_copy(u)
            act.wait_ge(S["vt_ready"], 2)
            copy(xTf, VT[:, :]).then_inc(S["vt_copied"], 1)
            for g in range(3):
                gu_squares(g)
            act.wait_ge(S["qkv_ready"], 1)
            copy(val[:, 0, :, 0:DH], QKV[2][:, :].rearrange("p (h d) -> p h d", d=DH), scale=V_TOP).then_inc(S["v_hi"], 1)
            turn_copy(0)
            unit(0)
            unit(1)

            def wo_high(k):
                if k == 0:
                    act.wait_ge(S["wo_scale"], 5)
                act.wait_ge(S["t_ready"], 17 + k)
                copy(wo_t[:, 0, k, :], TURN_SMALL[k % 2][:, :], scale=vn[:, k:k + 1]).then_inc(S["wo_hi"], 1)

            wo_high(0)
            wo_high(1)
            for u in range(2, 6):
                unit(u)
            wo_high(2)
            wo_high(3)
            unit(6)
            unit(7)
            for i in range(2):
                act.wait_ge(S["qk_turned"], i + 1)
                copy(qkT[:, 512 * i:512 * i + 512], banks[6 + i][:, :]).then_inc(S["qk_copied"], 1)
            gu_squares(3)
            down_squares(0, range(4))
            unit(8)
            act.wait_ge(S["score_ready"], 1)
            att_v = att[:, :, :, :].rearrange("p l (q j) v -> p l j q v", j=4)
            for j in range(4):
                nc.scalar.activation(sq[:, j, :], SCORE[j][:, :], ACT.Square).then_inc(S["a_sq"], 1)
            unit(9)
            for j in range(4):
                act.wait_ge(S["a_sq"], j + 1)
                copy(att_v[:, 0, j, :, :], sq[:, j, :].rearrange("p (q v) -> p q v", v=P), scale=32.0).then_inc(S["a_hi"], 1)
            unit(10)
            unit(11)
            gu_squares(4)
            gu_squares(5, (0,))

            def product(n, s):
                if s == 0:
                    act.wait_ge(S["count_ready"], n + 1)
                    act.wait_ge(S["p_done"], H * n)
                    copy(cnt[:, :], COUNT[:, :]).then_inc(S["count_copied"], 1)
                if s < H:
                    i = H * n + s
                    act.wait_ge(S["p_done"], i + 1)
                    if s % 4 == 0:
                        act.wait_ge(S["heads_ready"], QUADS * n + s // 4)
                    copy(p16[:, 0, s % 4, :], prod[:, s % 2, :]).then_inc(S["ph_done"], 1)

            def attend(n, s):
                if s in SUMS_AT:
                    q = SUMS_AT.index(s)
                    act.wait_ge(S["o_done"], QUADS * n + q + 1)
                    copy(o16[:, 0, :], wide[:, :]).then_inc(S["oh_done"], 1)
                if s in O_FLIP_AT:
                    q = O_FLIP_AT.index(s)
                    act.wait_ge(S["o_flipped"], QUADS * n + q + 1)
                    if q == 0:
                        act.wait_ge(S["wo_ready"], 4 * n)
                    copy(oT[:, :, q, :], banks[6][:, :].bitcast(F16).rearrange("p (l t) -> p l t", l=2))\
                        .then_inc(S["oT_done"], 1)
                if s in X_FLIP_AT:
                    m = X_FLIP_AT.index(s)
                    act.wait_ge(S["flip_ready"], 4 * n + m + 1)
                    if m == 0:
                        act.wait_ge(S["up_ready"], FT * n)
                    copy(xT[:, :, :, m * P:(m + 1) * P],
                         PICK[m % 2][:, :].bitcast(F16).rearrange("p (l k t) -> p l k t", l=2, t=P)).then_inc(S["xT_done"], 1)

            def x_high(n, m):
                act.wait_ge(S["xn_done"], 4 * n + m + 1)
                act.wait_ge(S["flip_ready"], 4 * n + m)
                copy(x16[:, 0, :], wide[:, :]).then_inc(S["xh_done"], 1)

            def feed(b, s):
                if s < FT:
                    i = FT * b + s
                    act.wait_ge(S["gate_ready"], i + 1)
                    nc.scalar.activation(sg[:, :], GATE[s % 2][:, :], ACT.Silu, scale=sc[:, s:s + 1]).then_inc(S["silu_done"], 1)
                    act.wait_ge(S["a_done"], i + 1)
                    copy(hid[:, 0, s, :], a32[:, :]).then_inc(S["ah_done"], 1)

            for s in range(SLOTS):
                us = units_of_slot(s)
                for u in us[:ahead(s)]:
                    unit(u)
                if s - 1 == WO_AT[0]:
                    act.wait_ge(S["d_ss"], 4 * DC)
                    act.wait_ge(S["gu_ss"], 4 * GROUPS)
                if s - 1 in WO_AT:
                    x_high(0, WO_AT.index(s - 1))
                product(0, s)
                attend(0, s)
                for u in us:
                    if u in us[ahead(s):]:
                        unit(u)
                    g, i = (u - EARLY + 1) // 4 + 5, (u - EARLY + 1) % 4
                    if g < GROUPS:
                        gu_squares(g, (i,))
                    if u in DOWN_SQUARES_AT:
                        down_squares(*DOWN_SQUARES_AT[u])
            with act.Fori(0, NB - 1) as b:
                for s in range(SLOTS):
                    if s:
                        product(b + 1, s)
                    feed(b, s)
                    if s == 0:
                        product(b + 1, s)
                    attend(b + 1, s)
                    if s in WO_AT:
                        x_high(b + 1, WO_AT.index(s))
                act.wait_ge(S["y_ready"], 4 * b + 4)
                act.wait_ge(S["stored"], 64 * b + 64)
            for s in range(SLOTS):
                feed(NB - 1, s)

        @block.tensor
        def _(pe):
            mm = nc.tensor.matmul

            def turn(bank, pieces, rights, done):
                for i in range(4):
                    if rights is None:
                        last = nc.tensor.transpose(bank[:, i * P:(i + 1) * P], pieces(i), ident)
                    else:
                        last = mm(bank[:, i * P:(i + 1) * P], pieces(i), rights(i), start=True, stop=True)
                last.then_inc(done, 1)

            def split_mm(dst, w, v, first, final):
                mm(dst, w[0], v[0], start=first, stop=False)
                mm(dst, w[0], v[1], start=False, stop=False)
                return mm(dst, w[1], v[0], start=False, stop=final)

            def turn_unit(u):
                if u >= 2:
                    pe.wait_ge(S["turned_copied"], u - 1)
                if u < GU_UNITS:
                    g, k = u // 4, u % 4
                    if k == 0:
                        pe.wait_ge(S["gu_diag"], g + 1)
                        pe.wait_ge(S["mixB_dve"], g + 1)
                        pe.wait_ge(S["mixB_pool"], g + 1)
                    turn(TURN[u % 2], lambda i: raw[g % 3][:, 512 * i + k * P:512 * i + (k + 1) * P],
                         lambda i: gu_diags[g % 2][:, i, :], S["turned"])
                else:
                    f = u - GU_UNITS
                    if f == 0:
                        pe.wait_ge(S["d_diag"], 1)
                        pe.wait_ge(S["d_mix_dve"], 16)
                        pe.wait_ge(S["d_mix_pool"], 16)
                    turn(TURN[u % 2], lambda i: down_path[i][-1][:, f * P:(f + 1) * P],
                         lambda i: d_diag[:, i, :], S["turned"])

            def unit(u):
                pe.wait_ge(S["turned_copied"], u + 1)
                if u >= 2:
                    pe.wait_ge(S["w_lo"], u - 1)
                mm(HADA[u % 2][:, :], hada, wt[:, u % 2, :], start=True, stop=True).then_inc(S["hada_ready"], 1)
                if u + 2 < UNITS:
                    turn_unit(u + 2)

            pe.wait_ge(S["c_land"], 16)

            def small_unit(u):
                if u >= 2 and u < 18:
                    pe.wait_ge(S["t_copied"], u - 1)
                if u >= 18:
                    pe.wait_ge(S["wo_lo"], u - 17)
                w = small_raw[u // 4]
                k = u % 4
                r = (lambda i: v_diag[:, i, :]) if u // 4 == 3 else None
                turn(TURN_SMALL[u % 2], lambda i: w[:, i, k * P:(k + 1) * P], r, S["t_ready"])

            pe.wait_ge(S["p_land"], 16)
            for u in range(4):
                if u == 2:
                    pe.wait_ge(S["emb_n"], 1)
                    turn(VT, lambda i: embn[:, i * P:(i + 1) * P], None, S["vt_ready"])
                small_unit(u)
            pe.wait_ge(S["vt_copied"], 1)
            pe.wait_ge(S["t_copied"], 4)
            for k in range(DC):
                last = mm(PROJ[:, :], xTf[:, k * P:(k + 1) * P], small_t[0][:, k, :], start=(k == 0), stop=(k == DC - 1))
            last.then_inc(S["proj_ready"], 1)
            for u in range(4, 16):
                if u in (4, 8):
                    pe.wait_ge(S[f"w_land{u // 4 - 1}"], 16)
                if u == 12:
                    pe.wait_ge(S["wv_diag"], 2)
                small_unit(u)
            pe.wait_ge(S["x1_ready"], 1)
            turn(VT, lambda i: x1[:, i * P:(i + 1) * P], None, S["vt_ready"])
            pe.wait_ge(S["vt_copied"], 2)
            pe.wait_ge(S["t_copied"], 16)
            for i in range(3):
                for k in range(DC):
                    last = mm(QKV[i][:, :], xTf[:, k * P:(k + 1) * P], small_t[1 + i][:, k, :],
                              start=(k == 0), stop=(k == DC - 1))
            last.then_inc(S["qkv_ready"], 1)
            turn_unit(0)
            turn_unit(1)
            unit(0)
            unit(1)
            pe.wait_ge(S["v_lo"], 2)
            small_unit(16)
            small_unit(17)
            for u in range(2, 6):
                unit(u)
            small_unit(18)
            small_unit(19)
            unit(6)
            unit(7)
            pe.wait_ge(S["feat_ready"], 1)
            for i in range(2):
                turn(banks[6 + i], lambda j: qk2[:, 512 * i + j * P:512 * i + (j + 1) * P], None, S["qk_turned"])
            unit(8)
            pe.wait_ge(S["qk_copied"], 2)
            pe.wait_ge(S["wo_lo"], 4)
            for q in range(QUADS):
                for j in range(4):
                    r = slice(DH * j, DH * j + DH)
                    last = mm(SCORE[j][:, q * P:(q + 1) * P], qkT[r, q * P:(q + 1) * P],
                              qkT[r, 512 + q * P:512 + (q + 1) * P], start=True, stop=True)
            last.then_inc(S["score_ready"], 1)
            unit(9)
            unit(10)
            unit(11)

            def attend(n, s):
                if s == 0:
                    pe.wait_ge(S["onehot_ready"], 2 * n + 2)
                    pe.wait_ge(S["h1_done"], 4 * n)
                    if isinstance(n, int) and n == 0:
                        pe.wait_ge(S["qk_copied"], 2)
                        pe.wait_ge(S["a_sq"], 4)
                    for i in range(2):
                        c = SEQ * i
                        mm(COUNT[:, c:c + SEQ], onehot[:, 2 * i, :], cum0, start=True, stop=False)
                        last = mm(COUNT[:, c + P:c + SEQ], onehot[:, 2 * i + 1, :], cum1, start=False, stop=True)
                    last.then_inc(S["count_ready"], 1)
                for h in (0, 1) if s == 0 else (s + 1,) if s + 1 < H else ():
                    i = H * n + h
                    if h == 0:
                        pe.wait_ge(S["onehotT_ready"], n + 1)
                        pe.wait_ge(S["a_lo"], 4)
                    if h < 2:
                        pe.wait_ge(S["xT_done"], 4 * n)
                    if not (isinstance(n, int) and i < 2):
                        pe.wait_ge(S["p_done"], i - 1)
                    mm(PICK[h % 2][:, :], att[:, 0, h, :], onehotT[:, :], start=True, stop=False)
                    mm(PICK[h % 2][:, :], att[:, 1, h, :], onehotT[:, :], start=False, stop=True).then_inc(S["picked"], 1)
                if s in SUMS_AT:
                    q = SUMS_AT.index(s)
                    pe.wait_ge(S["pl_done"], H * n + 4 * q + 4)
                    pe.wait_ge(S["oT_done"], QUADS * n + q)
                    if q == 0:
                        pe.wait_ge(S["count_copied"], n + 1)
                    for m in range(4):
                        for j in range(4):
                            for w, p in ((0, 0), (1, 0), (0, 1)):
                                first = m % 2 == 0 and j == 0 and w == 0 and p == 0
                                final = m % 2 == 1 and j == 3 and p == 1
                                last = mm(HEADS[m // 2][:, 4 * (m % 2) + j, :], p16[:, p, j, m * P:(m + 1) * P],
                                          val[:, w, 4 * q + j, :], start=first, stop=final, skip_group_check=True)
                    last.then_inc(S["heads_ready"], 1)
                if s in O_FLIP_AT:
                    q = O_FLIP_AT.index(s)
                    pe.wait_ge(S["ol_done"], QUADS * n + q + 1)
                    bank = banks[6][:, :].bitcast(F16)
                    for l in range(2):
                        for m in range(4):
                            c = (4 * l + m) * P
                            last = nc.tensor.transpose(bank[:, c:c + P], o16[:, l, m * P:(m + 1) * P], ident16)
                    last.then_inc(S["o_flipped"], 1)
                if s in X_FLIP_AT:
                    m = X_FLIP_AT.index(s)
                    pe.wait_ge(S["xl_done"], 4 * n + m + 1)
                    if m >= 2:
                        pe.wait_ge(S["xT_done"], 4 * n + m - 1)
                    bank = PICK[m % 2][:, :].bitcast(F16)
                    for i in range(2):
                        for k in range(DC):
                            c = (DC * i + k) * P
                            last = nc.tensor.transpose(bank[:, c:c + P], x16[:, i, k * P:(k + 1) * P], ident16)
                    last.then_inc(S["flip_ready"], 1)
                if s in WO_AT:
                    m = WO_AT.index(s)
                    if m == 0:
                        pe.wait_ge(S["oT_done"], QUADS * n + QUADS)
                        pe.wait_ge(S["wo_lo"], 4)
                    if m >= 2:
                        pe.wait_ge(S["h1_done"], 4 * n + m - 1)
                    c = slice(m * P, m * P + P)
                    for k in range(DC):
                        last = split_mm(WOUT[m % 2][:, :], [oT[:, i, k, c] for i in range(2)],
                                        [wo_t[:, i, k, :] for i in range(2)], k == 0, k == DC - 1)
                    last.then_inc(S["wo_ready"], 1)

            def feed(b, s):
                if s < FT:
                    i = FT * b + s
                    if s == 0:
                        pe.wait_ge(S["xT_done"], 4 * b + 4)
                        pe.wait_ge(S["w_lo"], UNITS)
                    if s == 1 and isinstance(b, int):
                        pe.wait_ge(S["y_last_done"], b)
                    if s >= 2:
                        pe.wait_ge(S["a_done"], i - 1)
                    for half, bank, done in ((0, GATE[s % 2], S["gate_ready"]), (1, UP[s % 2], S["up_ready"])):
                        f = half * FT + s
                        c = slice(P * (f % 4), P * (f % 4) + P)
                        for k in range(DC):
                            last = split_mm(bank[:, :], [wgu[:, l, f // 4, k, c] for l in range(2)],
                                            [xT[:, l, k, :] for l in range(2)], k == 0, k == DC - 1)
                        last.then_inc(done, 1)
                else:
                    m, part = (s - FT) // 4, (s - FT) % 4
                    if m == 0:
                        pe.wait_ge(S["al_done"], FT * b + 4 * part + 4)
                        if part == 0:
                            pe.wait_ge(S["silu_done"], FT * b + FT - 1)
                    if m == 1 and part == 0:
                        pe.wait_ge(S["a_done"], FT * b + FT)
                    c = slice(m * P, m * P + P)
                    for f in range(4 * part, 4 * part + 4):
                        last = split_mm(Y[m][:, :], [hid[:, l, f, c] for l in range(2)],
                                        [wd[:, l, f, :] for l in range(2)], f == 0, f == FT - 1)
                    if part == 3:
                        last.then_inc(S["y_ready"], 1)

            for s in range(SLOTS):
                us = units_of_slot(s)
                for u in us[:ahead(s)]:
                    unit(u)
                attend(0, s)
                for u in us[ahead(s):]:
                    unit(u)
            with pe.Fori(0, NB - 1) as b:
                for s in range(SLOTS):
                    feed(b, s)
                    attend(b + 1, s)
                pe.wait_ge(S["y_done"], 3 * b + 3)
            for s in range(SLOTS):
                feed(NB - 1, s)


_INS = ["x", "L0_tok_emb_table", "L0_tok_norm_weight", "L0_tok_proj_weight", "L0_attn_Wq", "L0_attn_Wk", "L0_attn_Wv",
        "L0_attn_Wo", "L0_attn_gamma", "L0_attn_beta", "L0_ffn_SU_ug", "L0_ffn_SU_dp", "L0_ffn_Wscale_ug",
        "L0_ffn_Wscale_dp", "L0_ffn_W_up", "L0_ffn_W_gate", "L0_ffn_W_down"]


def constants(seq):
    import numpy as np
    hada = np.ones((1, 1), np.float32)
    while hada.shape[0] < P:
        hada = np.block([[hada, hada], [hada, -hada]])
    ident = np.eye(P, dtype=np.float32)
    place = np.arange(seq)
    weight = 2.0 ** -np.ceil(np.log2(place + 1.0))
    causal = (place[:, None] <= place[None, :]) * weight[None, :]
    half = np.concatenate([ident, causal[:P], causal[P:, P:], np.tile(np.arange(P), (P, 1))], axis=1)
    column = np.concatenate([(1e-5 * A_TOP * weight).reshape(-1, P).T, np.arange(P)[:, None]], axis=1)
    return {"c_square": np.concatenate([ident, hada], axis=1), "c_half": half.astype(np.float16),
            "c_column": column.astype(np.float32)}


def kernel(**inputs):
    import numpy as np
    from concourse.bacc import Bacc
    from concourse.bass_utils import run_bass_kernel_spmd

    nc = Bacc("TRN2", target_bir_lowering=False, num_devices=1)
    given = {name: np.ascontiguousarray(inputs[name]) for name in _INS}
    batch, seq = given["x"].shape
    given.update(constants(seq))
    arrays, args = {}, []
    for name, a in given.items():
        arrays[f"in_{name}"] = a
        args.append(nc.dram_tensor(f"in_{name}", a.shape, mybir.dt.from_np(a.dtype), kind="ExternalInput").ap())
    shape = (batch, seq, given["L0_tok_emb_table"].shape[1])
    out = nc.dram_tensor("out", shape, F32, kind="ExternalOutput").ap()
    tower(nc, *args, out)
    return run_bass_kernel_spmd(nc, [arrays], core_ids=[0]).results[0]["out"]
```
